# Optimizing a Trainium2 kernel written in Bass

```python
import numpy as np
import jax
import jax.numpy as jnp

def _softmax(x, axis=-1):
    return jax.nn.softmax(x, axis=axis)

def _gelu(x):
    return jax.nn.gelu(x, approximate=True)

def _silu(x):
    return jax.nn.silu(x)

def _sigmoid(x):
    return jax.nn.sigmoid(x)

def _layernorm(x, axis=-1, eps=1e-05):
    m = jnp.mean(x, axis=axis, keepdims=True)
    v = jnp.var(x, axis=axis, keepdims=True)
    return (x - m) / jnp.sqrt(v + eps)

def _scatter_add(tgt, idx, src, axis=0):
    return tgt.at[idx].add(src)

def _segment_sum(src, seg, n):
    return jax.ops.segment_sum(src, seg, n)
kernel_name = 'mk_gnn_resnorm_d2_gnn_r32_3bfae3'

def setup_inputs(seed: int=0):
    np.random.seed(seed)
    _w = jnp.asarray

    def _rec_inputs():
        import jax
        import jax.numpy as jnp
        _gk = jax.random.key(seed)
        x = -0.0003713 + 1 * jax.random.normal(jax.random.fold_in(_gk, 1), (3125, 128), jnp.float32)
        _s = jax.random.randint(jax.random.fold_in(_gk, 2), (25000,), 0, 3125, jnp.int32)
        _d = jax.random.randint(jax.random.fold_in(_gk, 3), (25000,), 0, 3125, jnp.int32)
        _loop = jnp.arange(3125, dtype=jnp.int32)
        src = jnp.concatenate([_s, _d, _loop])
        dst = jnp.concatenate([_d, _s, _loop])
        _o = jnp.argsort(dst, stable=True)
        src = src[_o]
        dst = dst[_o]
        edge_attr_128 = -5.16925e-05 + 1.00005 * jax.random.normal(jax.random.fold_in(_gk, 11), (53125, 128), jnp.float32)
        return (x, src, dst, edge_attr_128)
    x, src, dst, edge_attr_128 = _rec_inputs()

    def _L0_gnn_setup():
        import jax, jax.numpy as jnp
        import numpy as np
        N_NODES = 3125
        N_EDGES = 50000
        D = 128
        D_OUT = 128
        key = jax.random.key(seed)
        k1, k2, k3, k4 = jax.random.split(key, 4)
        x = jax.random.normal(k1, (N_NODES, D), dtype=jnp.float32)
        edge_index = jax.random.randint(k2, (2, N_EDGES), 0, N_NODES, dtype=jnp.int64)
        W = jax.random.normal(k3, (2 * D, D_OUT), dtype=jnp.float32) * 0.05
        b = jax.random.normal(k4, (D_OUT,), dtype=jnp.float32) * 0.05
        return {'x': x, 'edge_index': edge_index, 'W': W, 'b': b}
    _L0_gnn_all = _L0_gnn_setup()
    _L0_gnn_in = {k: v for k, v in _L0_gnn_all.items() if k in ('W', 'b')}
    del _L0_gnn_all

    def _L1_gnn_setup():
        import jax, jax.numpy as jnp
        import numpy as np
        N = 50000
        E = 25000
        D = 128
        H = 4
        C = 32
        NEG_SLOPE = 0.2
        key = jax.random.key(seed)
        ks = jax.random.split(key, 10)
        s = 1.0 / np.sqrt(D)
        return {'x': jax.random.normal(ks[0], (N, D), jnp.float32), 'edge_index': jax.random.randint(ks[1], (2, E), 0, N, dtype=jnp.int32), 'edge_attr': jax.random.normal(ks[2], (E, D), jnp.float32), 'W_l': jax.random.normal(ks[3], (D, H * C), jnp.float32) * s, 'b_l': jnp.zeros((H * C,), jnp.float32), 'W_r': jax.random.normal(ks[4], (D, H * C), jnp.float32) * s, 'b_r': jnp.zeros((H * C,), jnp.float32), 'W_e': jax.random.normal(ks[5], (D, H * C), jnp.float32) * s, 'att': jax.random.normal(ks[6], (H, C), jnp.float32) * (1.0 / np.sqrt(C)), 'bias': jnp.zeros((H * C,), jnp.float32)}
    _L1_gnn_all = _L1_gnn_setup()
    _L1_gnn_in = {k: v for k, v in _L1_gnn_all.items() if k in ('W_l', 'b_l', 'W_r', 'b_r', 'W_e', 'att', 'bias')}
    del _L1_gnn_all
    return {'x': x, 'src': src, 'dst': dst, 'edge_attr_128': edge_attr_128, 'L0_gnn_W': _L0_gnn_in['W'], 'L0_gnn_b': _L0_gnn_in['b'], 'L1_gnn_W_l': _L1_gnn_in['W_l'], 'L1_gnn_b_l': _L1_gnn_in['b_l'], 'L1_gnn_W_r': _L1_gnn_in['W_r'], 'L1_gnn_b_r': _L1_gnn_in['b_r'], 'L1_gnn_W_e': _L1_gnn_in['W_e'], 'L1_gnn_att': _L1_gnn_in['att'], 'L1_gnn_bias': _L1_gnn_in['bias']}

def reference(x, src, dst, edge_attr_128, L0_gnn_W, L0_gnn_b, L1_gnn_W_l, L1_gnn_b_l, L1_gnn_W_r, L1_gnn_b_r, L1_gnn_W_e, L1_gnn_att, L1_gnn_bias):
    import jax
    import jax.numpy as jnp

    def _L0_gnn_ref(x, edge_index, W, b):
        import jax, jax.numpy as jnp
        import numpy as np
        N_NODES = 3125
        N_EDGES = 50000
        D = 128
        D_OUT = 128
        row, col = (edge_index[0], edge_index[1])
        n = x.shape[0]
        agg = jax.ops.segment_sum(x[col], row, num_segments=n)
        deg = jax.ops.segment_sum(jnp.ones((row.shape[0],), dtype=x.dtype), row, num_segments=n)
        agg = agg / (deg[:, None] + 1e-06)
        h = jnp.concatenate([x, agg], axis=1)
        return jax.nn.relu(h @ W + b)

    def _L1_gnn_ref(x, edge_index, edge_attr, W_l, b_l, W_r, b_r, W_e, att, bias):
        import jax, jax.numpy as jnp
        import numpy as np
        N = 50000
        E = 25000
        D = 128
        H = 4
        C = 32
        NEG_SLOPE = 0.2
        n = x.shape[0]
        src, dst = (edge_index[0], edge_index[1])
        loop_sum = jax.ops.segment_sum(edge_attr, dst, num_segments=n)
        cnt = jax.ops.segment_sum(jnp.ones((src.shape[0],), x.dtype), dst, num_segments=n)
        loop_attr = loop_sum / jnp.maximum(cnt, 1.0)[:, None]
        loop_idx = jnp.arange(n, dtype=src.dtype)
        src_f = jnp.concatenate([src, loop_idx])
        dst_f = jnp.concatenate([dst, loop_idx])
        ea_f = jnp.concatenate([edge_attr, loop_attr], axis=0)
        x_l = (x @ W_l + b_l).reshape(n, H, C)
        x_r = (x @ W_r + b_r).reshape(n, H, C)
        e = (ea_f @ W_e).reshape(-1, H, C)
        s = jax.nn.leaky_relu(x_l[src_f] + x_r[dst_f] + e, negative_slope=NEG_SLOPE)
        alpha = jnp.einsum('ehc,hc->eh', s, att)
        amax = jax.ops.segment_max(alpha, dst_f, num_segments=n)
        ex = jnp.exp(alpha - amax[dst_f])
        denom = jax.ops.segment_sum(ex, dst_f, num_segments=n)
        alpha = ex / denom[dst_f]
        msg = x_l[src_f] * alpha[:, :, None]
        out = jax.ops.segment_sum(msg, dst_f, num_segments=n)
        return out.reshape(n, H * C) + bias
    edge_index = jnp.stack([src, dst])
    x = _layernorm(x + _L0_gnn_ref(x, edge_index, L0_gnn_W, L0_gnn_b), axis=-1)
    x = _layernorm(x + _L1_gnn_ref(x, edge_index, edge_attr_128, L1_gnn_W_l, L1_gnn_b_l, L1_gnn_W_r, L1_gnn_b_r, L1_gnn_W_e, L1_gnn_att, L1_gnn_bias), axis=-1)
    return x

_drawn_inputs = setup_inputs


def setup_inputs(seed=0):
    import zlib

    import numpy as np

    out = dict(_drawn_inputs(seed))
    spreads = {'L1_gnn_b_l': (0.0, 0.1), 'L1_gnn_b_r': (0.0, 0.77), 'L1_gnn_bias': (0.0, 0.1)}
    factors = {}
    for name, (base, spread) in spreads.items():
        noise = np.random.default_rng([zlib.crc32(name.encode()), seed]).standard_normal(out[name].shape)
        drawn = base * np.exp(spread * noise) if base else spread * noise
        out[name] = jnp.asarray(drawn.astype(out[name].dtype))
    for name, factor in factors.items():
        out[name] = (out[name] * factor).astype(out[name].dtype)
    return out
```

```python
from contextlib import ExitStack

import concourse.bass as bass
from concourse import mybir

F32 = mybir.dt.float32
BF16 = mybir.dt.bfloat16
I32 = mybir.dt.int32
ALU = mybir.AluOpType
ACT = mybir.ActivationFunctionType
AX = mybir.AxisListType

P = 128
BANK = 512
U = 4
B = 4
BIG = 1.0e30
SLOPE = 0.2
LN_EPS = 1e-5
DEG_EPS = 1e-6
ROWW = 132


class Shapes:

    def __init__(self, n_nodes, n_edges, heads):
        self.N, self.E, self.H = n_nodes, n_edges, heads
        self.NT = -(-n_nodes // P)
        self.LAST = n_nodes - (self.NT - 1) * P
        self.TE = 125
        self.T = n_edges // self.TE
        self.CR, self.CC = 85, 5
        self.K = 464
        self.KR, self.KC = 116, 4
        self.K2 = 440
        assert self.T * self.TE == n_edges and self.CR * self.CC == self.T
        assert self.K >= self.T + self.NT - 1 and self.K % (B * U) == 0
        assert self.KR * self.KC == self.K and self.KR <= P
        assert self.K2 >= n_edges // P + self.NT and self.K2 % (2 * U) == 0


def repeat(ap, dim, n):
    shape = list(ap.shape)
    shape.insert(dim, n)
    return ap.unsqueeze(dim).broadcast_to(shape)




class Steps:

    def __init__(self, sem):
        self.sem, self.n = sem, 0

    def inc(self, instruction):
        instruction.then_inc(self.sem, 1)
        self.n += 1
        return self.n


def numbers(nc, engine, table, first, count, top):
    _, values = nc.values_load_multi_w_load_instructions(
        table[0:1, bass.ds(first, count)], engines=[engine.engine], min_val=0, max_val=top)
    return values


def passes(engine, count, body):
    body(0)
    with engine.Fori(1, count) as i:
        body(i)


def wait_before(engine, sem, value):
    if not (isinstance(value, int) and value <= 0):
        engine.wait_ge(sem, value)


class Tables:
    pass


def prepare(nc, g, m, a):
    with ExitStack() as ctx:
        def sb(name, shape, dt=F32):
            return ctx.enter_context(nc.sbuf_tensor(name, shape, dt))

        def sem(name):
            return ctx.enter_context(nc.semaphore(name))

        CR, CC, TE, K, NT, T, KR, KC = g.CR, g.CC, g.TE, g.K, g.NT, g.T, g.KR, g.KC
        src_i = sb("src_i", [CR, CC, TE], I32)
        dst_i = sb("dst_i", [CR, CC, TE], I32)
        prev_i = sb("prev_i", [CR, CC], I32)
        tile_i = sb("tile_i", [CR, CC, 2], I32)
        src_f = sb("src_f", [CR, CC, TE])
        dst_f = sb("dst_f", [CR, CC, TE])
        prev_f = sb("prev_f", [CR, CC])
        first_f = sb("first_f", [CR, CC, TE])
        ends4 = sb("ends4", [CR, 2, CC, 4])
        tile_f = sb("tile_f", [CR, CC, 2])
        tile_no = sb("tile_no", [CR, CC])
        iota_k = sb("iota_k", [CR, K])
        upto = sb("upto", [CR, CC, K])
        pick = sb("pick", [CR, CC, K])
        bucket_i = sb("bucket_i", [CR, CC * TE], I32)
        bucket_f = sb("bucket_f", [CR, CC * TE], BF16)
        in_b = sb("in_b", [CR, NT, CC * TE], BF16)
        count_b = sb("count_b", [CR, NT])
        run_b = sb("run_b", [CR, 2, CC * TE])
        place = sb("place", [CR, CC * TE])
        before = sb("before", [CR, CR])
        ones = sb("ones", [CR, P])
        one_row = sb("one_row", [P, NT])
        tiles_r = sb("tiles_r", [P, NT])
        tiles_ri = sb("tiles_ri", [P, NT], I32)
        tiles_end = sb("tiles_end", [P, NT])
        start_b = sb("start_b", [CR, NT])
        tiles_c = sb("tiles_c", [NT, 1])
        tiles_ci = sb("tiles_ci", [NT, 1], I32)
        end_c = sb("end_c", [NT, 1])
        uptoc = sb("uptoc", [NT, NT])
        iota_k2 = sb("iota_k2", [NT, g.K2])
        ended = sb("ended", [NT, g.K2])
        slot_k = sb("slot_k", [P, K])
        node_of = sb("node_of", [P, K])
        t_of = sb("t_of", [1, K])
        nk2 = sb("nk2", [1, g.K2])
        work = sb("work", [P, K])
        work_i = sb("work_i", [P, 2, K], I32)
        work2 = sb("work2", [P, K])
        dst_r = sb("dst_r", [KR, KC, TE])
        dst_ri = sb("dst_ri", [KR, KC, TE], I32)
        node_r = sb("node_r", [KR, KC])
        slot_rows = sb("slot_rows", [KR, KC])
        zero = m.x1[:].rearrange("p n d -> p (n d)")[:, 0:g.K2 // 20 * ROWW]

        loaded = sem("loaded")
        weights_in = sem("weights_in")
        cleared = sem("cleared")
        ps = [ctx.enter_context(nc.psum_tensor(f"ps_prep{i}", [P, BANK], F32)) for i in range(8)]
        pool_sem, dve_sem, pe_sem = sem("pool_step"), sem("dve_step"), sem("pe_step")
        block = ctx.enter_context(nc.Block())
        NCLEAR = 20
        MAIN = (NT - 1) * P

        @block.sync
        def _(sp):
            sp.dma_start(src_i[:], a["src"].rearrange("(c r e) -> r c e", c=CC, r=CR)).then_inc(loaded, 16)
            sp.dma_start(dst_i[:], a["dst"].rearrange("(c r e) -> r c e", c=CC, r=CR)).then_inc(loaded, 16)
            ends = a["dst"].rearrange("(t e) -> t e", e=TE)[:, TE - 1:TE]
            sp.wait_ge(pool_sem, 1)
            sp.dma_start(prev_i[1:CR, 0:1], ends[0:CR - 1], allow_slow_non_contiguous=True).then_inc(loaded, 16)
            for c in range(1, CC):
                sp.dma_start(prev_i[:, c:c + 1], ends[c * CR - 1:(c + 1) * CR - 1],
                             allow_slow_non_contiguous=True).then_inc(loaded, 16)
            sp.wait_ge(pool_sem, 2)
            for dst, src in (
                (m.x[:, 0:NT - 1, :], a["x"][0:MAIN].rearrange("(n p) d -> p n d", p=P)),
                (m.x[0:g.LAST, NT - 1, :], a["x"][MAIN:g.N]),
                (m.w0[:], a["W0"].rearrange("(c p) d -> p c d", p=P)),
                (m.w_lr[:, 0, :], a["W_l"]), (m.w_lr[:, 1, :], a["W_r"]), (m.w_e[:], a["W_e"]),
                (m.rows[0:1, 0, :], a["b0"].unsqueeze(0)), (m.rows[0:1, 1, :], a["b_l"].unsqueeze(0)),
                (m.rows[0:1, 2, :], a["b_r"].unsqueeze(0)),
                (m.rows[0:1, 3, :], a["att"].rearrange("h c -> (h c)").unsqueeze(0)),
                (m.rows[0:1, 4, :], a["bias"].unsqueeze(0)),
            ):
                sp.dma_start(dst, src).then_inc(weights_in, 16)
            sp.wait_ge(pool_sem, 3)
            w = g.K2 // NCLEAR
            for i in range(NCLEAR):
                sp.dma_start(m.sorted_rows[:, i * w:(i + 1) * w, :].rearrange("p k w -> p (k w)"),
                             zero).then_inc(cleared, 16)
            sp.wait_ge(cleared, 16 * NCLEAR)
            sp.wait_ge(weights_in, 16 * 11)

        @block.gpsimd
        def _(pool):
            pool.memset(prev_i[:], -1).then_inc(pool_sem, 1)
            pool.memset(m.x[:, NT - 1, :], 0.0).then_inc(pool_sem, 1)
            pool.memset(zero, 0.0).then_inc(pool_sem, 1)
            iota = dict(allow_small_or_imprecise_dtypes=True)
            pool.iota(m.column[:], [[1, P]], 0, 0, **iota).then_inc(pool_sem, 1)
            pool.iota(m.row_no[:], [[0, 1]], 0, 1, **iota).then_inc(pool_sem, 1)
            pool.iota(iota_k[:], [[1, K]], 0, 0, **iota).then_inc(pool_sem, 1)
            pool.iota(tile_no[:], [[CR, CC]], 0, 1, **iota).then_inc(pool_sem, 1)
            pool.iota(slot_k[:], [[1, K]], 0, 0, **iota).then_inc(pool_sem, 1)
            pool.iota(iota_k2[:], [[1, g.K2]], 0, 0, **iota).then_inc(pool_sem, 1)
            pool.iota(slot_rows[:], [[KR, KC]], 0, 1, **iota).then_inc(pool_sem, 1)
            pool.memset(ones[:], 1.0).then_inc(pool_sem, 1)
            pool.memset(one_row[:], 1.0).then_inc(pool_sem, 1)
            pool.memset(m.ones_row[:], 1.0).then_inc(pool_sem, 1)

        PE_COUNT, PE_TOTALS, PE_NODE, PE_ENDC, PE_NK2, PE_TABLE, PE_ROWS, PE_PLACE = range(1, 9)
        step = Steps(dve_sem)
        at = {}

        @block.vector
        def _(dve):
            def link(ins):
                dve.wait_ge(dve_sem, step.inc(ins))

            dve.wait_ge(pool_sem, 13)
            dve.wait_ge(loaded, 16 * (2 + CC))
            link(dve.tensor_scalar(bucket_i[:], src_i[:].rearrange("r c e -> r (c e)"), 7, None,
                                   ALU.arith_shift_right))
            link(dve.tensor_copy(bucket_f[:], bucket_i[:]))
            for b in range(NT):
                step.inc(dve.tensor_scalar(in_b[:, b, :], bucket_f[:], float(b), None, ALU.is_equal))
            dve.wait_ge(dve_sem, step.n)
            step.inc(dve.tensor_scalar(before[:], m.column[0:CR, 0:CR], m.row_no[0:CR, 0:1], None, ALU.is_gt))
            step.inc(dve.tensor_scalar(uptoc[:], m.column[0:NT, 0:NT], m.row_no[0:NT, 0:1], None, ALU.is_ge))
            step.inc(dve.tensor_scalar(m.ident[:], m.column[:], m.row_no[:, 0:1], None, ALU.is_equal))
            at["count"] = step.inc(dve.tensor_reduce(count_b[:], in_b[:], AX.X, ALU.add))
            step.inc(dve.tensor_copy(src_f[:], src_i[:]))
            step.inc(dve.tensor_copy(dst_f[:], dst_i[:]))
            step.inc(dve.tensor_copy(prev_f[:], prev_i[:]))
            step.inc(dve.tensor_scalar(tile_i[:, :, 0], dst_i[:, :, TE - 1], 7, None, ALU.arith_shift_right))
            link(dve.tensor_scalar(tile_i[:, :, 1], prev_i[:], 7, None, ALU.arith_shift_right))
            link(dve.tensor_copy(tile_f[:], tile_i[:]))
            step.inc(dve.tensor_tensor(tile_f[:, :, 0], tile_f[:, :, 0], tile_no[:], ALU.add))
            link(dve.scalar_tensor_tensor(tile_f[:, :, 1], tile_f[:, :, 1], -1.0, tile_no[:], ALU.add, ALU.add))
            link(dve.tensor_scalar(work2[0:CR, 0:CC], tile_no[:], float(T - 1), float(K), ALU.is_equal, ALU.mult))
            link(dve.tensor_tensor(tile_f[:, :, 0], tile_f[:, :, 0], work2[0:CR, 0:CC], ALU.max))
            for c in range(CC):
                step.inc(dve.tensor_scalar(upto[:, c, :], iota_k[:], tile_f[:, c, 0:1], None, ALU.is_le))
                step.inc(dve.tensor_scalar(pick[:, c, :], iota_k[:], tile_f[:, c, 1:2], None, ALU.is_gt))
            dve.wait_ge(dve_sem, step.n)
            link(dve.tensor_tensor(pick[:], pick[:], upto[:], ALU.mult))
            step.inc(dve.tensor_tensor(first_f[:, :, 1:TE], dst_f[:, :, 1:TE], dst_f[:, :, 0:TE - 1], ALU.not_equal))
            step.inc(dve.tensor_tensor(first_f[:, :, 0], dst_f[:, :, 0], prev_f[:], ALU.not_equal))
            step.inc(dve.tensor_copy(ends4[:, 0], repeat(dst_f[:, :, 0], 2, 4)))
            at["pick"] = step.inc(dve.tensor_copy(ends4[:, 1], repeat(dst_f[:, :, TE - 1], 2, 4)))
            dve.wait_ge(dve_sem, step.n)
            dve.wait_ge(pe_sem, PE_COUNT)
            step.inc(dve.tensor_scalar(tiles_ri[:], ps[0][:, 0:NT], float(P - 1), None, ALU.add))
            link(dve.tensor_scalar(tiles_ci[:], ps[1][0:NT, 0:1], float(P - 1), None, ALU.add))
            step.inc(dve.tensor_scalar(tiles_ri[:], tiles_ri[:], 7, None, ALU.arith_shift_right))
            link(dve.tensor_scalar(tiles_ci[:], tiles_ci[:], 7, None, ALU.arith_shift_right))
            step.inc(dve.tensor_copy(tiles_r[:], tiles_ri[:]))
            at["tiles_c"] = step.inc(dve.tensor_copy(tiles_c[:], tiles_ci[:]))
            dve.wait_ge(dve_sem, step.n)
            link(dve.tensor_tensor_scan(tiles_end[:], one_row[:], tiles_r[:], 0.0, ALU.mult, ALU.add))
            link(dve.tensor_tensor(tiles_end[:], tiles_end[:], tiles_r[:], ALU.subtract))
            link(dve.tensor_scalar(start_b[:], tiles_end[0:CR, :], float(P), -1.0, ALU.mult, ALU.add))
            dve.wait_ge(pe_sem, PE_TOTALS)
            link(dve.tensor_tensor(start_b[:], start_b[:], ps[2][0:CR, 0:NT], ALU.add))
            link(dve.memset(place[:], 0.0))
            for b in range(NT):
                link(dve.tensor_tensor_scan(run_b[:, b % 2, :], repeat(ones[:, 0], 1, CC * TE), in_b[:, b, :],
                                            start_b[:, b:b + 1], ALU.mult, ALU.add))
                link(dve.tensor_tensor(run_b[:, b % 2, :], run_b[:, b % 2, :], in_b[:, b, :], ALU.mult))
                link(dve.tensor_tensor(place[:], place[:], run_b[:, b % 2, :], ALU.add))
            at["place"] = step.n
            dve.wait_ge(pe_sem, PE_NODE)
            link(dve.scalar_tensor_tensor(node_of[:], slot_k[:], float(-T), ps[3][:, 0:K], ALU.add, ALU.add))
            step.inc(dve.tensor_scalar(m.node_i[:], node_of[0:1, :], float(NT - 1), None, ALU.min))
            link(dve.tensor_tensor(t_of[:], slot_k[0:1, :], node_of[0:1, :], ALU.subtract))
            link(dve.tensor_copy(m.tile_i[:], t_of[:]))
            dve.wait_ge(pe_sem, PE_ENDC)
            link(dve.tensor_copy(end_c[:], ps[1][0:NT, 1:2]))
            at["ended"] = step.inc(dve.tensor_scalar(ended[:], iota_k2[:], end_c[:, 0:1], None, ALU.is_ge))
            dve.wait_ge(pe_sem, PE_NK2)
            link(dve.tensor_scalar(m.node2_i[:], ps[0][0:1, 0:g.K2], float(NT - 1), None, ALU.min))
            at["done_banks"] = step.n
            dve.wait_ge(pe_sem, PE_TABLE)
            link(dve.scalar_tensor_tensor(m.dst_lo[0:TE, :], node_of[0:TE, :], float(-P), ps[5][0:TE, 0:K],
                                          ALU.mult, ALU.add))
            step.inc(dve.tensor_copy(m.first[0:TE, :], ps[6][0:TE, 0:K]))
            link(dve.tensor_copy(m.src_idx[:], ps[4][0:TE, 0:K]))
            link(dve.tensor_scalar(work_i[0:TE, 0, :], m.src_idx[:], P - 1, None, ALU.bitwise_and))
            link(dve.tensor_copy(m.src_lo[:], work_i[0:TE, 0, :]))
            dve.wait_ge(pe_sem, PE_ROWS)
            step.inc(dve.tensor_copy(dst_r[:], ps[7][0:KR, 0:KC * TE].rearrange("k (c e) -> k c e", c=KC)))
            link(dve.scalar_tensor_tensor(node_r[:], ps[2][0:KR, 32:32 + KC], float(-T), slot_rows[:],
                                          ALU.add, ALU.add))
            link(dve.tensor_copy(dst_ri[:], dst_r[:]))
            link(dve.tensor_scalar(dst_ri[:], dst_ri[:], 7, None, ALU.arith_shift_right))
            for c in range(KC):
                link(dve.tensor_scalar(m.others[:, c, :], dst_ri[:, c, :], node_r[:, c:c + 1], -BIG,
                                       ALU.not_equal, ALU.mult))
                for h in range(g.H):
                    step.inc(dve.memset(m.begins[:, c, h, 0:1], -BIG))
                    step.inc(dve.memset(m.ends[:, c, h, TE - 1:TE], -BIG))
                    step.inc(dve.tensor_tensor(m.begins[:, c, h, 1:TE], dst_r[:, c, 1:TE], dst_r[:, c, 0:TE - 1],
                                               ALU.not_equal))
                    step.inc(dve.tensor_tensor(m.ends[:, c, h, 0:TE - 1], dst_r[:, c, 1:TE], dst_r[:, c, 0:TE - 1],
                                               ALU.not_equal))
                dve.wait_ge(dve_sem, step.n)
                step.inc(dve.tensor_scalar(m.begins[:, c, :, 1:TE], m.begins[:, c, :, 1:TE], -BIG, None, ALU.mult))
                step.inc(dve.tensor_scalar(m.ends[:, c, :, 0:TE - 1], m.ends[:, c, :, 0:TE - 1], -BIG, None, ALU.mult))
                step.inc(dve.tensor_scalar(m.not_first[:, c, :], dst_r[:, c, :], dst_r[:, c, 0:1], -BIG,
                                           ALU.not_equal, ALU.mult))
                link(dve.tensor_scalar(m.not_last[:, c, :], dst_r[:, c, :], dst_r[:, c, TE - 1:TE], -BIG,
                                       ALU.not_equal, ALU.mult))
            dve.wait_ge(pe_sem, PE_PLACE)
            step.inc(dve.tensor_copy(m.end_rows[:, 0, :], ps[0][0:4, 0:K]))
            link(dve.tensor_copy(m.end_rows[:, 1, :], ps[1][0:4, 0:K]))
            step.inc(dve.tensor_tensor(m.whole[:], m.end_rows[:, 0, :], m.end_rows[:, 1, :], ALU.not_equal))
            link(dve.tensor_tensor(m.joined[:, 1:K], m.end_rows[:, 0, 1:K], m.end_rows[:, 1, 0:K - 1], ALU.not_equal))
            step.inc(dve.tensor_scalar(m.whole[:], m.whole[:], -BIG, None, ALU.mult))
            link(dve.tensor_scalar(m.joined[:, 1:K], m.joined[:, 1:K], -BIG, None, ALU.mult))
            link(dve.tensor_copy(work_i[0:TE, 0, :], ps[3][0:TE, 0:K]))
            link(dve.tensor_scalar(work_i[0:TE, 1, :], work_i[0:TE, 0, :], P - 1, None, ALU.bitwise_and))
            link(dve.tensor_scalar(work_i[0:TE, 0, :], work_i[0:TE, 0, :], 7, None, ALU.arith_shift_right))
            link(dve.tensor_copy(work2[0:TE, :], work_i[0:TE, 0, :]))
            link(dve.scalar_tensor_tensor(work2[0:TE, :], work_i[0:TE, 1, :], float(g.K2), work2[0:TE, :],
                                          ALU.mult, ALU.add))
            link(dve.tensor_scalar(work[0:TE, :], m.dst_lo[0:TE, :], 0.0, float(P * g.K2), ALU.is_lt, ALU.mult))
            link(dve.tensor_tensor(work2[0:TE, :], work2[0:TE, :], work[0:TE, :], ALU.add))
            link(dve.tensor_scalar(work[0:TE, :], m.dst_lo[0:TE, :], float(P), float(P * g.K2), ALU.is_ge, ALU.mult))
            link(dve.tensor_tensor(work2[0:TE, :], work2[0:TE, :], work[0:TE, :], ALU.add))
            link(dve.tensor_copy(m.place_idx[:], work2[0:TE, :]))

        @block.tensor
        def _(pe):
            pe.wait_ge(dve_sem, at["count"])
            pe.matmul(ps[0][:, 0:NT], ones[:], count_b[:], start=True, stop=True)
            pe.matmul(ps[1][0:NT, 0:1], count_b[:], ones[:, 0:1], start=True, stop=True).then_inc(pe_sem, 1)
            pe.matmul(ps[2][0:CR, 0:NT], before[:], count_b[:], start=True, stop=True).then_inc(pe_sem, 1)
            pe.wait_ge(dve_sem, at["pick"])
            for c in range(CC):
                mm = pe.matmul(ps[3][:, 0:K], ones[:], upto[:, c, :], start=(c == 0), stop=(c == CC - 1))
            mm.then_inc(pe_sem, 1)
            pe.wait_ge(dve_sem, at["tiles_c"])
            pe.matmul(ps[1][0:NT, 1:2], uptoc[:], tiles_c[:], start=True, stop=True).then_inc(pe_sem, 1)
            pe.wait_ge(dve_sem, at["ended"])
            pe.matmul(ps[0][0:1, 0:g.K2], ones[0:NT, 0:1], ended[:], start=True, stop=True).then_inc(pe_sem, 1)
            for bank, table in ((4, src_f), (5, dst_f), (6, first_f)):
                for c in range(CC):
                    mm = pe.matmul(ps[bank][0:TE, 0:K], table[:, c, :], pick[:, c, :],
                                   start=(c == 0), stop=(c == CC - 1))
            mm.then_inc(pe_sem, 1)
            for q in range(KC):
                for c in range(CC):
                    pe.matmul(ps[7][0:KR, q * TE:(q + 1) * TE], pick[:, c, q * KR:(q + 1) * KR], dst_f[:, c, :],
                              start=(c == 0), stop=(c == CC - 1))
                for c in range(CC):
                    mm = pe.matmul(ps[2][0:KR, 32 + q:33 + q], upto[:, c, q * KR:(q + 1) * KR], ones[:, 0:1],
                                   start=(c == 0), stop=(c == CC - 1))
            mm.then_inc(pe_sem, 1)
            pe.wait_ge(dve_sem, at["done_banks"])
            for which in range(2):
                for c in range(CC):
                    pe.matmul(ps[which][0:4, 0:K], ends4[:, which, c, :], pick[:, c, :],
                              start=(c == 0), stop=(c == CC - 1))
            for c in range(CC):
                mm = pe.matmul(ps[3][0:TE, 0:K], place[:, c * TE:(c + 1) * TE], pick[:, c, :],
                               start=(c == 0), stop=(c == CC - 1))
            mm.then_inc(pe_sem, 1)


def spread(nc, g, m, a):
    NB = g.K // U
    TE = g.TE
    with ExitStack() as ctx:
        def sb(name, shape, dt=F32):
            return ctx.enter_context(nc.sbuf_tensor(name, shape, dt))

        def sem(name):
            return ctx.enter_context(nc.semaphore(name))

        attr = [sb(f"attr{b}", [TE, U, P + 1]) for b in range(B)]
        onehot = [sb(f"onehot{b}", [TE, U, P]) for b in range(2)]
        onehot_t = [sb(f"onehot_t{b}", [P, U, TE]) for b in range(2)]
        row = [sb(f"row{b}", [TE, U, ROWW]) for b in range(B)]
        index = [sb(f"index{b}", [TE, U], I32) for b in range(B)]
        ps_t = [ctx.enter_context(nc.psum_tensor(f"ps_t{b}", [P, BANK], F32)) for b in range(2)]
        ps_x = [ctx.enter_context(nc.psum_tensor(f"ps_x{b}", [P, BANK], F32)) for b in range(2)]
        ps_a = [ctx.enter_context(nc.psum_tensor(f"ps_a{b}", [P, 2, BANK], F32)) for b in range(2)]
        attr_in = [sem(f"attr_in{b}") for b in range(B)]
        row_out = [sem(f"row_out{b}") for b in range(B)]
        block_summed, onehot_ready = sem("block_summed"), sem("onehot_ready")
        turned, turned_copied, spread_done, row_copied = (
            sem("turned"), sem("turned_copied"), sem("spread_done"), sem("row_copied"))
        meta_ready, sums_free, added = sem("meta_ready"), sem("sums_free"), sem("added")
        preset = sem("preset")
        index_ready, begun = sem("index_ready"), sem("begun")
        block = ctx.enter_context(nc.Block())

        @block.sync
        def _(sp):
            def one_pass(i):
                tiles = numbers(nc, sp, m.tile_i, i * (B * U), B * U, g.T - 1)
                for b in range(B):
                    sp.wait_ge(block_summed, i * B + b + 1)
                    for u in range(U):
                        sp.dma_start(attr[b][:, u, 0:P], a["ea"][bass.ds(tiles[b * U + u] * TE, TE), :]).then_inc(attr_in[b], 16)

            passes(sp, NB // B, one_pass)

        @block.gpsimd
        def _(pool):
            limit = pool.to_reg(P * g.K2 - 1)
            def one_pass(i):
                for b in range(B):
                    wait_before(pool, row_out[b], i * (16 * U))
                    pool.tensor_copy(index[b][:], m.place_idx[:, bass.ds(i * (B * U) + b * U, U)]).then_inc(
                        index_ready, 1)
                    pool.wait_ge(index_ready, i * B + b + 1)
                    pool.wait_ge(row_copied, i * B + b + 3)
                    pool.wait_ge(meta_ready, i * B + b + 2)
                    pool.sem_inc(begun, 1)
                    for u in range(U):
                        pool.indirect_dma_start(
                            out=m.sorted_rows.rearrange("p k w -> (p k) w"),
                            out_offset=bass.IndirectOffsetOnAxis(ap=index[b][:, u:u + 1], axis=0),
                            in_=row[b][:, u, :], in_offset=None,
                            bounds_check=limit, oob_is_err=False).then_inc(row_out[b], 16)

            passes(pool, NB // B, one_pass)
            for b in range(B):
                pool.wait_ge(row_out[b], 16 * U * (NB // B))

        @block.scalar
        def _(act):
            act.sem_inc(row_copied, 2)
            def one_pass(i):
                for b in range(B):
                    act.wait_ge(turned, i * B + b + 1)
                    act.copy(onehot_t[b % 2][:], ps_t[b % 2][:, 0:U * TE].rearrange("p (u e) -> p u e", u=U)).then_inc(
                        turned_copied, 1)
                    act.wait_ge(spread_done, i * B + b + 1)
                    wait_before(act, row_out[b], i * (16 * U))
                    act.copy(row[b][:, :, 0:P], ps_x[b % 2][0:TE, :].rearrange("p (u d) -> p u d", u=U)).then_inc(
                        row_copied, 1)

            passes(act, NB // B, one_pass)

        @block.vector
        def _(dve):
            for b in range(B):
                dve.memset(attr[b][:, :, P:P + 1], 1.0).then_inc(preset, 1)
                dve.memset(row[b][:, :, P:ROWW], 1.0).then_inc(preset, 1)
            dve.memset(m.attr_sum[:], 0.0).then_inc(added, 1)
            dve.wait_ge(preset, 2 * B)
            dve.sem_inc(meta_ready, 1)
            dve.sem_inc(sums_free, 2)
            def one_pass(i):
                nodes = numbers(nc, dve, m.node_i, i * (B * U), B * U, g.NT - 1)
                for b in range(B):
                    k0 = i * (B * U) + b * U
                    dve.wait_ge(block_summed, i * B + b + 1)
                    dve.tensor_tensor(onehot[b % 2][:], repeat(m.column[0:TE, :], 1, U),
                                      repeat(m.dst_lo[0:TE, bass.ds(k0, U)], 2, P),
                                      ALU.is_equal).then_inc(onehot_ready, 1)
                    wait_before(dve, row_out[b], i * (16 * U))
                    dve.tensor_copy(row[b][:, :, P + 1], m.src_lo[:, bass.ds(k0, U)]).then_inc(meta_ready, 1)
                    dve.wait_ge(block_summed, i * B + b + 3)
                    for u in range(U):
                        acc = m.attr_sum[:, bass.ds(nodes[b * U + u], 1), :]
                        dve.wait_ge(added, i * (B * U) + (b * U + u + 1))
                        dve.tensor_tensor(acc, acc, ps_a[b % 2][:, u // 2, (u % 2) * 256:(u % 2) * 256 + P + 1].unsqueeze(1),
                                          ALU.add).then_inc(added, 1)
                    dve.wait_ge(added, i * (B * U) + ((b + 1) * U + 1))
                    dve.sem_inc(sums_free, 1)

            passes(dve, NB // B, one_pass)

        @block.tensor
        def _(pe):
            pe.sem_inc(block_summed, 2)
            pe.wait_ge(preset, 2 * B)
            def one_pass(i):
                nodes = numbers(nc, pe, m.node_i, i * (B * U), B * U, g.NT - 1)
                for b in range(B):
                    k0 = i * (B * U) + b * U
                    pe.wait_ge(onehot_ready, i * B + b + 1)
                    for u in range(U):
                        mm = pe.transpose(ps_t[b % 2][:, u * TE:(u + 1) * TE], onehot[b % 2][:, u, :], m.ident[0:TE, 0:TE])
                    mm.then_inc(turned, 1)
                    pe.wait_ge(attr_in[b], (i + 1) * (16 * U))
                    pe.wait_ge(sums_free, i * B + b + 1)
                    for u in range(U):
                        mm = pe.matmul(ps_a[b % 2][:, u // 2, (u % 2) * 256:(u % 2) * 256 + P + 1], onehot[b % 2][:, u, :],
                                       attr[b][:, u, :], start=True, stop=True)
                    mm.then_inc(block_summed, 1)
                    pe.wait_ge(turned_copied, i * B + b + 1)
                    pe.wait_ge(row_copied, i * B + b + 1)
                    for u in range(U):
                        mm = pe.matmul(ps_x[b % 2][0:TE, u * P:(u + 1) * P], onehot_t[b % 2][:, u, :],
                                       m.x[:, bass.ds(nodes[b * U + u], 1), :], start=True, stop=True)
                    mm.then_inc(spread_done, 1)

            passes(pe, NB // B, one_pass)

def gather_src(nc, g, m):
    NB = g.K2 // U
    with ExitStack() as ctx:
        def sb(name, shape, dt=F32):
            return ctx.enter_context(nc.sbuf_tensor(name, shape, dt))

        def sem(name):
            return ctx.enter_context(nc.semaphore(name))

        row = [sb(f"row_in{b}", [P, U, ROWW]) for b in range(2)]
        onehot = [sb(f"onehot_s{b}", [P, U, P]) for b in range(2)]
        ps = [ctx.enter_context(nc.psum_tensor(f"ps_src{b}", [P, 2, BANK], F32)) for b in range(2)]
        row_in = [sem(f"row_in_sem{b}") for b in range(2)]
        onehot_ready, block_summed, sums_free, added = (
            sem("onehot_ready_s"), sem("block_summed_s"), sem("sums_free_s"), sem("added_s"))
        block = ctx.enter_context(nc.Block())

        @block.sync
        def _(sp):
            def one_pass(i):
                for b in range(2):
                    sp.wait_ge(block_summed, i * 2 + b + 1)
                    sp.dma_start(row[b][:], m.sorted_rows[:, bass.ds(i * (2 * U) + b * U, U), :]).then_inc(
                        row_in[b], 16)

            passes(sp, NB // 2, one_pass)

        @block.vector
        def _(dve):
            dve.sem_inc(sums_free, 2)
            dve.memset(m.src_sum[:], 0.0).then_inc(added, 1)
            def one_pass(i):
                nodes = numbers(nc, dve, m.node2_i, i * (2 * U), 2 * U, g.NT - 1)
                for b in range(2):
                    dve.wait_ge(row_in[b], i * 16 + 16)
                    dve.wait_ge(block_summed, i * 2 + b + 1)
                    dve.tensor_tensor(onehot[b][:], repeat(m.column[:], 1, U), repeat(row[b][:, :, P + 1], 2, P),
                                      ALU.is_equal).then_inc(onehot_ready, 1)
                for b in range(2):
                    dve.wait_ge(block_summed, i * 2 + b + 3)
                    for u in range(U):
                        acc = m.src_sum[:, bass.ds(nodes[b * U + u], 1), :]
                        dve.wait_ge(added, i * (2 * U) + (b * U + u + 1))
                        dve.tensor_tensor(acc, acc, ps[b][:, u // 2, (u % 2) * 256:(u % 2) * 256 + P + 1].unsqueeze(1),
                                          ALU.add).then_inc(added, 1)
                    dve.wait_ge(added, i * (2 * U) + ((b + 1) * U + 1))
                    dve.sem_inc(sums_free, 1)

            passes(dve, NB // 2, one_pass)

        @block.tensor
        def _(pe):
            pe.sem_inc(block_summed, 2)
            def one_pass(i):
                for b in range(2):
                    pe.wait_ge(onehot_ready, i * 2 + b + 1)
                    pe.wait_ge(sums_free, i * 2 + b + 1)
                    for u in range(U):
                        mm = pe.matmul(ps[b][:, u // 2, (u % 2) * 256:(u % 2) * 256 + P + 1], onehot[b][:, u, :],
                                       row[b][:, u, 0:P + 1], start=True, stop=True)
                    mm.then_inc(block_summed, 1)

            passes(pe, NB // 2, one_pass)

def layer_norm(g, vec, wait_sqrt, sqrt_step, y, square, stats, done, sqrt_ready):
    D = y.shape[2]

    def link(ins):
        vec.wait_ge(done.sem, done.inc(ins))

    mean, var, rstd = stats[:, 0, :], stats[:, 1, :], stats[:, 2, :]
    link(vec.tensor_reduce(mean, y[:], AX.X, ALU.add))
    link(vec.tensor_scalar(mean, mean, 1.0 / D, None, ALU.mult))
    link(vec.tensor_tensor(y[:], y[:], repeat(mean, 2, D), ALU.subtract))
    link(vec.tensor_tensor(square[:], y[:], y[:], ALU.mult))
    link(vec.tensor_reduce(var, square[:], AX.X, ALU.add))
    link(vec.tensor_scalar(var, var, 1.0 / D, LN_EPS, ALU.mult, ALU.add))
    vec.sem_inc(sqrt_ready, 1)
    vec.wait_ge(wait_sqrt, sqrt_step)
    link(vec.reciprocal(rstd, rstd))
    link(vec.tensor_tensor(y[:], y[:], repeat(rstd, 2, D), ALU.mult))


def nodes(nc, g, m):
    NT, BN = g.NT, 5
    D = P
    with ExitStack() as ctx:
        def sb(name, shape, dt=F32):
            return ctx.enter_context(nc.sbuf_tensor(name, shape, dt))

        def sem(name):
            return ctx.enter_context(nc.semaphore(name))

        pair = [sb(f"pair{b}", [P, 2, D]) for b in range(BN)]
        pair_t = [sb(f"pair_t{b}", [P, 2, P]) for b in range(BN)]
        square = sb("square", [P, NT, D])
        stats = sb("stats", [P, 3, NT])
        degree = sb("degree", [P, 2, NT])
        ps = [ctx.enter_context(nc.psum_tensor(f"ps_node{b}", [P, BANK], F32)) for b in range(BN)]
        ps_att = ctx.enter_context(nc.psum_tensor("ps_att", [P, BANK], F32))
        steps_sem, ready, sqrt_ready, sqrt_done = sem("node_steps"), sem("node_ready"), sem("sqrt_ready"), sem("sqrt_done")
        paired, turned, copied, product, stored = (
            sem("paired"), sem("node_turned"), sem("node_copied"), sem("node_product"), sem("node_stored"))
        loop_product, table_out, att_ready = sem("loop_product"), sem("table_out"), sem("att_ready")
        block = ctx.enter_context(nc.Block())
        step = Steps(steps_sem)
        at = {}

        @block.vector
        def _(dve):
            def link(ins):
                dve.wait_ge(steps_sem, step.inc(ins))

            link(dve.tensor_scalar(degree[:, 0, :], m.src_sum[:, :, D], DEG_EPS, None, ALU.add))
            link(dve.tensor_scalar(degree[:, 1, :], m.attr_sum[:, :, D], 1.0, None, ALU.max))
            link(dve.reciprocal(degree[:], degree[:]))
            link(dve.tensor_tensor(m.src_sum[:, :, 0:D], m.src_sum[:, :, 0:D], repeat(degree[:, 0, :], 2, D), ALU.mult))
            at["means"] = step.n
            link(dve.tensor_tensor(m.attr_sum[:, :, 0:D], m.attr_sum[:, :, 0:D], repeat(degree[:, 1, :], 2, D),
                                   ALU.mult))
            dve.wait_ge(att_ready, 1)
            link(dve.tensor_copy(m.att[:], ps_att[:, 0:D]))
            dve.sem_inc(stored, 1)
            def one_pass(i):
                for b in range(BN):
                    dve.wait_ge(product, i * BN + b + 1)
                    dve.scalar_tensor_tensor(m.x1[:, bass.ds(i * BN + b, 1), :], ps[b][:, 256:384].unsqueeze(1), 0.0,
                                             pair[b][:, 0:1, :], ALU.max, ALU.add).then_inc(stored, 1)

            passes(dve, NT // BN, one_pass)
            dve.wait_ge(stored, NT + 1)
            layer_norm(g, dve, sqrt_done, 1, m.x1, square, stats, step, sqrt_ready)
            at["x1"] = step.n
            dve.wait_ge(stored, 2 * NT + 1)
            link(dve.tensor_tensor(square[:], square[:], m.x[:], ALU.add))
            link(dve.tensor_tensor(square[:], square[:], m.src_sum[:, :, 0:D], ALU.add))
            link(dve.scalar_tensor_tensor(square[:], square[:], SLOPE, square[:], ALU.mult, ALU.max))
            link(dve.tensor_tensor(square[:], square[:], repeat(m.att[:], 1, NT), ALU.mult))
            link(dve.tensor_reduce(m.loop_score[:], square[:].rearrange("p n (h c) -> p n h c", h=g.H), AX.X, ALU.add))

        @block.gpsimd
        def _(pool):
            for which in range(2):
                if which == 0:
                    pool.wait_ge(steps_sem, at["means"])
                else:
                    pool.wait_ge(steps_sem, at["x1"])
                first, second = ((m.x, m.src_sum), (m.x1, m.attr_sum))[which]
                def one_pass(i):
                    for b in range(BN):
                        pool.wait_ge(stored, i * BN + (which * NT + 1))
                        n = i * BN + b
                        pool.tensor_copy(pair[b][:, 0:1, :], first[:, bass.ds(n, 1), :]).then_inc(paired, 1)
                        pool.tensor_copy(pair[b][:, 1:2, :], second[:, bass.ds(n, 1), 0:D]).then_inc(paired, 1)

                passes(pool, NT // BN, one_pass)

        @block.scalar
        def _(act):
            for which in range(2):
                if which == 1:
                    act.wait_ge(sqrt_ready, 1)
                    act.activation(stats[:, 2, :], stats[:, 1, :], ACT.Sqrt).then_inc(sqrt_done, 1)
                def one_pass(i):
                    for b in range(BN):
                        act.wait_ge(turned, i * BN + (which * NT + b + 1))
                        act.copy(pair_t[b][:], ps[b][:, 0:256].rearrange("p (c n) -> p c n", c=2)).then_inc(copied, 1)
                    if which == 1:
                        for b in range(BN):
                            n = i * BN + b
                            act.wait_ge(product, i * BN + (NT + b + 1))
                            act.copy(m.x[:, bass.ds(n, 1), :], ps[b][:, 256:384].unsqueeze(1))
                            act.copy(m.src_sum[:, bass.ds(n, 1), 0:D], ps[b][:, 384:512].unsqueeze(1))
                            act.copy(square[:, bass.ds(n, 1), :], ps[b][:, 0:128].unsqueeze(1)).then_inc(stored, 1)

                passes(act, NT // BN, one_pass)

            act.wait_ge(stored, 2 * NT + 1)
            act.dma_start(m.xl_rows.rearrange("(n p) d -> p n d", p=P), m.x[:]).then_inc(table_out, 16)
            act.wait_ge(table_out, 16)

        @block.tensor
        def _(pe):
            pe.matmul(ps_att[:, 0:D], m.ones_row[:], m.rows[0:1, 3, :], start=True, stop=True).then_inc(att_ready, 1)
            for which in range(2):
                def one_pass(i):
                    for b in range(BN):
                        pe.wait_ge(paired, i * (2 * BN) + (which * 2 * NT + 2 * b + 2))
                        for c in range(2):
                            mm = pe.transpose(ps[b][:, c * P:(c + 1) * P], pair[b][:, c, :], m.ident[:])
                        mm.then_inc(turned, 1)
                    for b in range(BN):
                        pe.wait_ge(copied, i * BN + (which * NT + b + 1))
                        if which == 0:
                            pe.matmul(ps[b][:, 256:384], pair_t[b][:, 0, :], m.w0[:, 0, :], start=True, stop=False)
                            pe.matmul(ps[b][:, 256:384], pair_t[b][:, 1, :], m.w0[:, 1, :], start=False, stop=False)
                            pe.matmul(ps[b][:, 256:384], m.ones_row[:], m.rows[0:1, 0, :],
                                      start=False, stop=True).then_inc(product, 1)
                        else:
                            pe.matmul(ps[b][:, 256:512], pair_t[b][:, 0, :], m.w_lr[:].rearrange("p c d -> p (c d)"),
                                      start=True, stop=False)
                            pe.matmul(ps[b][:, 256:512], m.ones_row[:], m.rows[0:1, 1:3, :].rearrange("p c d -> p (c d)"),
                                      start=False, stop=True)
                            pe.matmul(ps[b][:, 0:128], pair_t[b][:, 1, :], m.w_e[:], start=True,
                                      stop=True).then_inc(product, 1)

                passes(pe, NT // BN, one_pass)

def scores(nc, g, m, a):
    NB = g.K // U
    TE = g.TE
    with ExitStack() as ctx:
        def sb(name, shape, dt=F32):
            return ctx.enter_context(nc.sbuf_tensor(name, shape, dt))

        def sem(name):
            return ctx.enter_context(nc.semaphore(name))

        attr = [sb(f"attr_c{b}", [TE, U, P]) for b in range(B)]
        xl = [sb(f"xl{b}", [TE, U, P]) for b in range(B)]
        index = [sb(f"index_c{b}", [TE, U], I32) for b in range(B)]
        onehot = [sb(f"onehot_c{b}", [TE, U, P]) for b in range(2)]
        onehot_t = [sb(f"onehot_ct{b}", [P, U, TE]) for b in range(2)]
        attr_t = [sb(f"attr_t{b}", [P, U, TE]) for b in range(2)]
        work = [sb(f"work_c{b}", [TE, U, P]) for b in range(2)]
        ps_t = [ctx.enter_context(nc.psum_tensor(f"ps_ct{b}", [P, BANK], F32)) for b in range(2)]
        ps_e = [ctx.enter_context(nc.psum_tensor(f"ps_ce{b}", [P, BANK], F32)) for b in range(2)]
        ps_s = [ctx.enter_context(nc.psum_tensor(f"ps_cs{b}", [P, BANK], F32)) for b in range(2)]
        attr_in = [sem(f"attr_c_in{b}") for b in range(B)]
        xl_in = [sem(f"xl_in{b}") for b in range(B)]
        xl_out = [sem(f"xl_out{b}") for b in range(B)]
        index_ready, begun, onehot_ready, turned, turned_copied = (
            sem("index_c_ready"), sem("begun_c"), sem("onehot_c_ready"), sem("turned_c"), sem("turned_c_copied"))
        attr_turned, attr_copied, summed, score_steps, xl_used = (
            sem("attr_turned"), sem("attr_copied"), sem("summed_c"), sem("score_steps"), sem("xl_used"))
        block = ctx.enter_context(nc.Block())

        @block.sync
        def _(sp):
            def one_pass(i):
                tiles = numbers(nc, sp, m.tile_i, i * (B * U), B * U, g.T - 1)
                for b in range(B):
                    sp.wait_ge(attr_turned, i * B + b + 1)
                    for u in range(U):
                        sp.dma_start(attr[b][:, u, :], a["ea"][bass.ds(tiles[b * U + u] * TE, TE), :]).then_inc(
                            attr_in[b], 16)

            passes(sp, NB // B, one_pass)

        @block.gpsimd
        def _(pool):
            def one_pass(i):
                for b in range(B):
                    wait_before(pool, xl_in[b], i * (16 * U))
                    wait_before(pool, xl_out[b], i * 16)
                    pool.wait_ge(xl_used, i * B + b + 1)
                    pool.tensor_copy(index[b][:], m.src_idx[:, bass.ds(i * (B * U) + b * U, U)]).then_inc(
                        index_ready, 1)
                    pool.wait_ge(index_ready, i * B + b + 1)
                    pool.sem_inc(begun, 1)
                    for u in range(U):
                        pool.indirect_dma_start(
                            out=xl[b][:, u, :], out_offset=None, in_=m.xl_rows,
                            in_offset=bass.IndirectOffsetOnAxis(ap=index[b][:, u:u + 1], axis=0)).then_inc(xl_in[b], 16)

            passes(pool, NB // B, one_pass)

        @block.scalar
        def _(act):
            def one_pass(i):
                for b in range(B):
                    act.wait_ge(attr_turned, i * B + b + 1 + B)
                    act.wait_ge(summed, i * B + b + 1)
                    act.copy(attr_t[b % 2][:], ps_e[b % 2][:, 0:U * TE].rearrange("p (u e) -> p u e", u=U)).then_inc(
                        attr_copied, 1)
                    act.wait_ge(turned, i * B + b + 1)
                    act.copy(onehot_t[b % 2][:], ps_t[b % 2][:, 0:U * TE].rearrange("p (u e) -> p u e", u=U)).then_inc(
                        turned_copied, 1)
                    act.wait_ge(xl_in[b], i * (16 * U) + 16 * U)
                    act.dma_start(m.xl_edges[:, bass.ds(i * (B * U) + b * U, U), :], xl[b][:]).then_inc(xl_out[b], 16)

            passes(act, NB // B, one_pass)
            for b in range(B):
                act.wait_ge(xl_out[b], 16 * (NB // B))

        @block.vector
        def _(dve):
            dve.sem_inc(xl_used, B)
            dve.sem_inc(score_steps, 1)
            def one_pass(i):
                for b in range(B):
                    k0 = i * (B * U) + b * U
                    wait_before(dve, turned, i * B + b)
                    dve.tensor_tensor(onehot[b % 2][:], repeat(m.column[0:TE, :], 1, U),
                                      repeat(m.dst_lo[0:TE, bass.ds(k0, U)], 2, P),
                                      ALU.is_equal).then_inc(onehot_ready, 1)
                    s = work[b % 2]
                    base = i * (4 * B) + 4 * b
                    dve.wait_ge(xl_in[b], i * (16 * U) + 16 * U)
                    dve.wait_ge(summed, i * B + b + 3)
                    dve.wait_ge(score_steps, base + 1)
                    dve.tensor_tensor(s[:], ps_s[b % 2][0:TE, :].rearrange("p (u d) -> p u d", u=U), xl[b][:],
                                      ALU.add).then_inc(score_steps, 1)
                    dve.wait_ge(score_steps, base + 2)
                    dve.sem_inc(xl_used, 1)
                    dve.scalar_tensor_tensor(s[:], s[:], SLOPE, s[:], ALU.mult, ALU.max).then_inc(score_steps, 1)
                    dve.wait_ge(score_steps, base + 3)
                    dve.tensor_tensor(s[:], s[:], repeat(m.att[0:TE, :], 1, U), ALU.mult).then_inc(score_steps, 1)
                    dve.wait_ge(score_steps, base + 4)
                    dve.tensor_reduce(m.score[:, :, bass.ds(k0, U)].rearrange("p h u -> p u h"),
                                      s[:].rearrange("p u (h c) -> p u h c", h=g.H), AX.X,
                                      ALU.add).then_inc(score_steps, 1)

            passes(dve, NB // B, one_pass)

        @block.tensor
        def _(pe):
            pe.sem_inc(attr_turned, B)
            pe.sem_inc(summed, 2)
            def one_pass(i):
                nodes = numbers(nc, pe, m.node_i, i * (B * U), B * U, g.NT - 1)
                for b in range(B):
                    pe.wait_ge(attr_in[b], i * (16 * U) + 16 * U)
                    for u in range(U):
                        mm = pe.transpose(ps_e[b % 2][:, u * TE:(u + 1) * TE], attr[b][:, u, :], m.ident[0:TE, 0:TE])
                    mm.then_inc(attr_turned, 1)
                    pe.wait_ge(onehot_ready, i * B + b + 1)
                    for u in range(U):
                        mm = pe.transpose(ps_t[b % 2][:, u * TE:(u + 1) * TE], onehot[b % 2][:, u, :],
                                          m.ident[0:TE, 0:TE])
                    mm.then_inc(turned, 1)
                    pe.wait_ge(attr_copied, i * B + b + 1)
                    pe.wait_ge(xl_used, i * B + (b - 2 + B + 1))
                    pe.wait_ge(turned_copied, i * B + b + 1)
                    for u in range(U):
                        out = ps_s[b % 2][0:TE, u * P:(u + 1) * P]
                        pe.matmul(out, attr_t[b % 2][:, u, :], m.w_e[:], start=True, stop=False)
                        mm = pe.matmul(out, onehot_t[b % 2][:, u, :],
                                       m.src_sum[:, bass.ds(nodes[b * U + u], 1), 0:P], start=False, stop=True)
                    mm.then_inc(summed, 1)

            passes(pe, NB // B, one_pass)

def maxima(nc, g, m):
    TE, KR, KC, H, K = g.TE, g.KR, g.KC, g.H, g.K
    with ExitStack() as ctx:
        def sb(name, shape, dt=F32):
            return ctx.enter_context(nc.sbuf_tensor(name, shape, dt))

        def sem(name):
            return ctx.enter_context(nc.semaphore(name))

        score = sb("score_rows", [KR, KC, H, TE])
        masked = sb("masked_rows", [KR, KC, H, TE])
        run = sb("run_rows", [KR, 2, KC * H * TE])
        ends = sb("max_ends", [KR, 2, KC, H])
        rows = sb("max_rows", [H, 2, K])
        way = sb("way", [H, 2, 2, K])
        carry = sb("carry", [H, 2, K])
        carry_k = sb("carry_k", [KR, 2, KC, H])
        extra = sb("extra", [KR, KC, H, TE])
        ps = [ctx.enter_context(nc.psum_tensor(f"ps_max{q}", [P, BANK], F32)) for q in range(8)]
        rows_ready, steps_sem, ends_turned, carry_turned, exp_done, back = (
            sem("rows_ready"), sem("max_steps"), sem("ends_turned"), sem("carry_turned"), sem("exp_done"), sem("back"))
        block = ctx.enter_context(nc.Block())
        step = Steps(steps_sem)
        at = {}
        flat = "k c h e -> k (c h e)"
        R = H * TE

        @block.vector
        def _(dve):
            def link(ins):
                dve.wait_ge(steps_sem, step.inc(ins))

            dve.wait_ge(rows_ready, 1)
            for q in range(KC):
                step.inc(dve.tensor_copy(score[:, q], ps[q][0:KR, 0:R].rearrange("k (h e) -> k h e", h=H)))
            dve.wait_ge(steps_sem, step.n)
            for q in range(KC):
                step.inc(dve.tensor_tensor(masked[:, q], score[:, q], repeat(m.others[:, q], 1, H), ALU.add))
            dve.wait_ge(steps_sem, step.n)
            link(dve.tensor_tensor_scan(run[:, 0, :], m.begins[:].rearrange(flat), masked[:].rearrange(flat),
                                        -BIG, ALU.add, ALU.max))
            link(dve.tensor_tensor_scan(run[:, 1, ::-1], m.ends[:].rearrange(flat)[:, ::-1],
                                        masked[:].rearrange(flat)[:, ::-1], -BIG, ALU.add, ALU.max))
            link(dve.tensor_tensor(run[:, 0, :], run[:, 0, :], run[:, 1, :], ALU.max))
            by_slot = run[:, 0, :].rearrange("k (c h e) -> k c h e", c=KC, h=H)
            step.inc(dve.tensor_copy(ends[:, 0], by_slot[:, :, :, 0]))
            at["ends"] = step.inc(dve.tensor_copy(ends[:, 1], by_slot[:, :, :, TE - 1]))
            dve.wait_ge(ends_turned, 1)
            step.inc(dve.tensor_copy(rows[:, 0, :], ps[4][0:H, 0:K]))
            link(dve.tensor_copy(rows[:, 1, :], ps[5][0:H, 0:K]))
            step.inc(dve.tensor_tensor(way[:, 0, 0, 1:K], m.joined[0:H, 1:K], m.whole[0:H, 0:K - 1], ALU.add))
            step.inc(dve.tensor_tensor(way[:, 0, 1, 1:K], m.joined[0:H, 1:K], rows[:, 1, 0:K - 1], ALU.add))
            step.inc(dve.tensor_tensor(way[:, 1, 0, 0:K - 1], m.joined[0:H, 1:K], m.whole[0:H, 1:K], ALU.add))
            step.inc(dve.tensor_tensor(way[:, 1, 1, 0:K - 1], m.joined[0:H, 1:K], rows[:, 0, 1:K], ALU.add))
            link(dve.memset(carry[:], -BIG))
            link(dve.tensor_tensor_scan(carry[:, 0, 1:K], way[:, 0, 0, 1:K], way[:, 0, 1, 1:K], -BIG, ALU.add, ALU.max))
            link(dve.tensor_tensor_scan(carry[:, 1, 0:K - 1][:, ::-1], way[:, 1, 0, 0:K - 1][:, ::-1],
                                        way[:, 1, 1, 0:K - 1][:, ::-1], -BIG, ALU.add, ALU.max))
            at["carry"] = step.n
            dve.wait_ge(carry_turned, 1)
            link(dve.tensor_copy(carry_k[:].rearrange("k f c h -> k (f c h)"), ps[6][0:KR, 0:2 * KC * H]))
            for f, away in ((0, m.not_first), (1, m.not_last)):
                for q in range(KC):
                    step.inc(dve.tensor_tensor(extra[:, q], repeat(carry_k[:, f, q, :], 2, TE),
                                               repeat(away[:, q], 1, H), ALU.add))
                dve.wait_ge(steps_sem, step.n)
                link(dve.tensor_tensor(run[:, 0, :], run[:, 0, :], extra[:].rearrange(flat), ALU.max))
            link(dve.tensor_tensor(run[:, 0, :], run[:, 0, :], score[:].rearrange(flat), ALU.max))
            link(dve.tensor_tensor(score[:].rearrange(flat), score[:].rearrange(flat), run[:, 0, :], ALU.subtract))
            at["shifted"] = step.n
            for which in range(2):
                for h in range(H):
                    dve.wait_ge(back, which * H + h + 1)
                    src = ps[which * H + h][0:TE, 0:K]
                    if which == 0:
                        step.inc(dve.tensor_copy(m.exp_max[:, :, h], src))
                    else:
                        step.inc(dve.tensor_tensor(m.exp_max[:, :, H + h], src, m.first[0:TE, :], ALU.mult))

        @block.scalar
        def _(act):
            act.wait_ge(steps_sem, at["shifted"])
            act.activation(score[:], score[:], ACT.Exp).then_inc(exp_done, 1)

        @block.tensor
        def _(pe):
            for q in range(KC):
                for h in range(H):
                    mm = pe.transpose(ps[q][0:KR, h * TE:(h + 1) * TE], m.score[:, h, q * KR:(q + 1) * KR],
                                      m.ident[0:TE, 0:TE])
            mm.then_inc(rows_ready, 1)
            pe.wait_ge(steps_sem, at["ends"])
            for f in range(2):
                for q in range(KC):
                    mm = pe.transpose(ps[4 + f][0:H, q * KR:(q + 1) * KR], ends[:, f, q, :], m.ident[0:KR, 0:KR])
            mm.then_inc(ends_turned, 1)
            pe.wait_ge(steps_sem, at["carry"])
            for f in range(2):
                for q in range(KC):
                    c0 = (f * KC + q) * H
                    mm = pe.transpose(ps[6][0:KR, c0:c0 + H], carry[:, f, q * KR:(q + 1) * KR], m.ident[0:H, 0:H])
            mm.then_inc(carry_turned, 1)
            by_slot = run[:, 0, :].rearrange("k (c h e) -> k c h e", c=KC, h=H)
            pe.wait_ge(exp_done, 1)
            for which, table in ((0, score[:]), (1, by_slot)):
                for h in range(H):
                    for q in range(KC):
                        mm = pe.transpose(ps[which * H + h][0:TE, q * KR:(q + 1) * KR], table[:, q, h, :],
                                          m.ident[0:KR, 0:KR])
                    mm.then_inc(back, 1)


def messages(nc, g, m):
    NB = g.K // U
    TE, H = g.TE, g.H
    W = P + 2 * H
    with ExitStack() as ctx:
        def sb(name, shape, dt=F32):
            return ctx.enter_context(nc.sbuf_tensor(name, shape, dt))

        def sem(name):
            return ctx.enter_context(nc.semaphore(name))

        xl = [sb(f"xl_m{b}", [TE, U, P]) for b in range(B)]
        message = [sb(f"message{b}", [TE, U, W]) for b in range(2)]
        onehot = [sb(f"onehot_m{b}", [TE, U, P]) for b in range(2)]
        ps = [ctx.enter_context(nc.psum_tensor(f"ps_m{b}", [P, 2, BANK], F32)) for b in range(2)]
        xl_in = [sem(f"xl_m_in{b}") for b in range(B)]
        message_ready, column_ready, summed, sums_free, added = (
            sem("message_ready"), sem("column_ready"), sem("summed_m"), sem("sums_m_free"), sem("added_m"))
        block = ctx.enter_context(nc.Block())

        @block.sync
        def _(sp):
            def one_pass(i):
                for b in range(B):
                    sp.wait_ge(message_ready, i * B + b + 1)
                    sp.dma_start(xl[b][:], m.xl_edges[:, bass.ds(i * (B * U) + b * U, U), :]).then_inc(xl_in[b], 16)

            passes(sp, NB // B, one_pass)

        @block.scalar
        def _(act):
            def one_pass(i):
                for b in range(B):
                    act.wait_ge(summed, i * B + b + 1)
                    act.copy(message[b % 2][:, :, P:W], m.exp_max[:, bass.ds(i * (B * U) + b * U, U), :]).then_inc(
                        column_ready, 1)

            passes(act, NB // B, one_pass)

        @block.vector
        def _(dve):
            dve.sem_inc(message_ready, B)
            dve.sem_inc(sums_free, 2)
            dve.memset(m.message_sum[:], 0.0).then_inc(added, 1)
            def one_pass(i):
                nodes = numbers(nc, dve, m.node_i, i * (B * U), B * U, g.NT - 1)
                for half in range(B // 2):
                    for b in (2 * half, 2 * half + 1):
                        k0 = i * (B * U) + b * U
                        dve.wait_ge(summed, i * B + b + 1)
                        dve.tensor_tensor(onehot[b % 2][:], repeat(m.column[0:TE, :], 1, U),
                                          repeat(m.dst_lo[0:TE, bass.ds(k0, U)], 2, P), ALU.is_equal)
                        dve.wait_ge(xl_in[b], i * 16 + 16)
                        for u in range(U):
                            ins = dve.tensor_tensor(
                                message[b % 2][:, u, 0:P].rearrange("p (h c) -> p h c", h=H),
                                xl[b][:, u, :].rearrange("p (h c) -> p h c", h=H),
                                m.exp_max[:, bass.ds(k0 + u, 1), 0:H].rearrange("p u h -> p (u h)").unsqueeze(2)
                                .broadcast_to([TE, H, P // H]), ALU.mult)
                        ins.then_inc(message_ready, 1)
                    for b in (2 * half, 2 * half + 1):
                        dve.wait_ge(summed, i * B + b + 3)
                        for u in range(U):
                            acc = m.message_sum[:, bass.ds(nodes[b * U + u], 1), :]
                            dve.wait_ge(added, i * (B * U) + (b * U + u + 1))
                            dve.tensor_tensor(acc, acc, ps[b % 2][:, u // 2, (u % 2) * 256:(u % 2) * 256 + W].unsqueeze(1),
                                              ALU.add).then_inc(added, 1)
                        dve.wait_ge(added, i * (B * U) + ((b + 1) * U + 1))
                        dve.sem_inc(sums_free, 1)

            passes(dve, NB // B, one_pass)

        @block.tensor
        def _(pe):
            pe.sem_inc(summed, 2)
            def one_pass(i):
                for b in range(B):
                    pe.wait_ge(message_ready, i * B + b + 1 + B)
                    pe.wait_ge(column_ready, i * B + b + 1)
                    pe.wait_ge(sums_free, i * B + b + 1)
                    for u in range(U):
                        mm = pe.matmul(ps[b % 2][:, u // 2, (u % 2) * 256:(u % 2) * 256 + W], onehot[b % 2][:, u, :],
                                       message[b % 2][:, u, :], start=True, stop=True)
                    mm.then_inc(summed, 1)

            passes(pe, NB // B, one_pass)

def finish(nc, g, m, out):
    NT, H, D = g.NT, g.H, P
    C = D // H
    with ExitStack() as ctx:
        def sb(name, shape, dt=F32):
            return ctx.enter_context(nc.sbuf_tensor(name, shape, dt))

        def sem(name):
            return ctx.enter_context(nc.semaphore(name))

        top = sb("top", [P, NT, H])
        part = sb("part", [P, 2, NT, H])
        total = sb("total", [P, NT, H])
        square = sb("square_f", [P, NT, D])
        stats = sb("stats_f", [P, 3, NT])
        ps_bias = ctx.enter_context(nc.psum_tensor("ps_bias", [P, BANK], F32))
        steps_sem, exp_done, bias_ready, sqrt_ready, sqrt_done, stored = (
            sem("finish_steps"), sem("part_exp"), sem("bias_ready"), sem("sqrt_f_ready"), sem("sqrt_f_done"), sem("out_stored"))
        block = ctx.enter_context(nc.Block())
        step = Steps(steps_sem)
        at = {}

        @block.vector
        def _(dve):
            def link(ins):
                dve.wait_ge(steps_sem, step.inc(ins))

            sums = m.message_sum
            link(dve.tensor_scalar(total[:, :, 0], m.attr_sum[:, :, D], 0.0, -BIG, ALU.is_equal, ALU.mult))
            link(dve.tensor_tensor(part[:, 0], sums[:, :, D + H:D + 2 * H], repeat(total[:, :, 0], 2, H), ALU.add))
            link(dve.tensor_tensor(top[:], part[:, 0], m.loop_score[:], ALU.max))
            link(dve.tensor_tensor(part[:, 0], part[:, 0], top[:], ALU.subtract))
            link(dve.tensor_tensor(part[:, 1], m.loop_score[:], top[:], ALU.subtract))
            at["part"] = step.n
            dve.wait_ge(exp_done, 1)
            link(dve.tensor_tensor(total[:], sums[:, :, D:D + H], part[:, 0], ALU.mult))
            link(dve.tensor_tensor(total[:], total[:], part[:, 1], ALU.add))
            link(dve.reciprocal(total[:], total[:]))
            for w in range(2):
                link(dve.tensor_tensor(part[:, w], part[:, w], total[:], ALU.mult))
            for h in range(H):
                c = slice(h * C, (h + 1) * C)
                step.inc(dve.tensor_tensor(sums[:, :, c], sums[:, :, c], repeat(part[:, 0, :, h], 2, C), ALU.mult))
                step.inc(dve.tensor_tensor(m.x[:, :, c], m.x[:, :, c], repeat(part[:, 1, :, h], 2, C), ALU.mult))
            dve.wait_ge(steps_sem, step.n)
            link(dve.tensor_tensor(m.x1[:], m.x1[:], sums[:, :, 0:D], ALU.add))
            link(dve.tensor_tensor(m.x1[:], m.x1[:], m.x[:], ALU.add))
            dve.wait_ge(bias_ready, 1)
            link(dve.tensor_tensor(m.x1[:], m.x1[:], repeat(ps_bias[:, 0:D], 1, NT), ALU.add))
            layer_norm(g, dve, sqrt_done, 1, m.x1, square, stats, step, sqrt_ready)
            at["out"] = step.n

        @block.scalar
        def _(act):
            act.wait_ge(steps_sem, at["part"])
            act.activation(part[:], part[:], ACT.Exp).then_inc(exp_done, 1)
            act.wait_ge(sqrt_ready, 1)
            act.activation(stats[:, 2, :], stats[:, 1, :], ACT.Sqrt).then_inc(sqrt_done, 1)

        @block.tensor
        def _(pe):
            pe.matmul(ps_bias[:, 0:D], m.ones_row[:], m.rows[0:1, 4, :], start=True, stop=True).then_inc(bias_ready, 1)

        @block.sync
        def _(sp):
            MAIN = (NT - 1) * P
            sp.wait_ge(steps_sem, at["out"])
            sp.dma_start(out[0:MAIN].rearrange("(n p) d -> p n d", p=P), m.x1[:, 0:NT - 1, :]).then_inc(stored, 16)
            sp.dma_start(out[MAIN:g.N], m.x1[0:g.LAST, NT - 1, :]).then_inc(stored, 16)
            sp.wait_ge(stored, 32)


def program(nc, a, out, upto_phase=8, probe=None):
    g = Shapes(a["x"].shape[0], a["src"].shape[0], a["att"].shape[0])
    m = Tables()
    with ExitStack() as ctx:
        def sb(name, shape, dt=F32):
            return ctx.enter_context(nc.sbuf_tensor(name, shape, dt))

        D = a["x"].shape[1]
        m.x = sb("x_nodes", [P, g.NT, D])
        m.w0 = sb("w0", [P, 2, D])
        m.w_lr = sb("w_lr", [P, 2, D])
        m.w_e = sb("w_e", [P, D])
        m.rows = sb("rows", [1, 5, D])
        m.ones_row = sb("ones_row", [1, P])
        m.column = sb("column", [P, P])
        m.row_no = sb("row_no", [P, 1])
        m.ident = sb("ident", [P, P])
        m.node_i = sb("slot_node", [1, g.K], I32)
        m.tile_i = sb("slot_tile", [1, g.K], I32)
        m.node2_i = sb("node2_i", [1, g.K2], I32)
        m.dst_lo = sb("dst_lo", [P, g.K])
        m.first = sb("first", [P, g.K])
        m.src_idx = sb("src_idx", [g.TE, g.K], I32)
        m.src_lo = sb("src_lo", [g.TE, g.K])
        m.place_idx = sb("place_idx", [g.TE, g.K], I32)
        m.others = sb("others", [g.KR, g.KC, g.TE])
        m.not_first = sb("not_first", [g.KR, g.KC, g.TE])
        m.not_last = sb("not_last", [g.KR, g.KC, g.TE])
        m.begins = sb("begins", [g.KR, g.KC, g.H, g.TE])
        m.ends = sb("ends", [g.KR, g.KC, g.H, g.TE])
        m.end_rows = sb("end_rows", [4, 2, g.K])
        m.whole = sb("whole", [4, g.K])
        m.joined = sb("joined", [4, g.K])
        m.sorted_rows = nc.dram_tensor("sorted_rows", (P, g.K2, ROWW), F32, kind="Internal").ap()
        m.att = sb("att_all", [P, D])
        m.x1 = sb("x1", [P, g.NT, D])
        m.loop_score = sb("loop_score", [P, g.NT, g.H])
        m.src_sum = sb("src_sum", [P, g.NT, D + 1])
        m.xl_rows = nc.dram_tensor("xl_rows", (P * g.NT, D), F32, kind="Internal").ap()
        m.xl_edges = nc.dram_tensor("xl_edges", (g.TE, g.K, D), F32, kind="Internal").ap()
        m.attr_sum = sb("attr_sum", [P, g.NT, D + 1])
        prepare(nc, g, m, a)
        if upto_phase >= 2:
            spread(nc, g, m, a)
        if upto_phase >= 3:
            gather_src(nc, g, m)
        if upto_phase >= 4:
            nodes(nc, g, m)
        if upto_phase >= 5:
            m.score = sb("score", [g.TE, g.H, g.K])
            scores(nc, g, m, a)
        if upto_phase >= 6:
            m.exp_max = sb("exp_max", [g.TE, g.K, 2 * g.H])
            maxima(nc, g, m)
        if upto_phase >= 7:
            m.message_sum = sb("message_sum", [P, g.NT, D + 2 * g.H])
            messages(nc, g, m)
        if upto_phase >= 8:
            finish(nc, g, m, out)
        if probe:
            probe(nc, g, m)


_NAMES = {
    "x": "x", "src": "src", "dst": "dst", "edge_attr_128": "ea", "L0_gnn_W": "W0", "L0_gnn_b": "b0",
    "L1_gnn_W_l": "W_l", "L1_gnn_b_l": "b_l", "L1_gnn_W_r": "W_r", "L1_gnn_b_r": "b_r", "L1_gnn_W_e": "W_e",
    "L1_gnn_att": "att", "L1_gnn_bias": "bias",
}


def kernel(**inputs):
    import numpy as _np
    import concourse.bacc as _bacc
    from concourse import mybir as _mybir
    from concourse.bass_utils import run_bass_kernel_spmd as _run

    nc = _bacc.Bacc("TRN2", target_bir_lowering=False, num_devices=1)
    arrays, aps = {}, {}
    for name, short in _NAMES.items():
        array = _np.ascontiguousarray(inputs[name])
        arrays[f"in_{short}"] = array
        aps[short] = nc.dram_tensor(f"in_{short}", array.shape, _mybir.dt.from_np(array.dtype),
                                    kind="ExternalInput").ap()
    out = nc.dram_tensor("out_0", inputs["x"].shape, _mybir.dt.float32, kind="ExternalOutput").ap()
    program(nc, aps, out)
    result = _run(nc, [arrays], core_ids=[0])
    return result.results[0]["out_0"]
```

```python
from contextlib import ExitStack

import concourse.bass as bass
from concourse import mybir

F32 = mybir.dt.float32
BF16 = mybir.dt.bfloat16
I32 = mybir.dt.int32
ALU = mybir.AluOpType
ACT = mybir.ActivationFunctionType
AX = mybir.AxisListType

P = 128
BANK = 512
U = 4
B = 4
BIG = 1.0e30
SLOPE = 0.2
LN_EPS = 1e-5
DEG_EPS = 1e-6
ROWW = 132


class Shapes:

    def __init__(self, n_nodes, n_edges, heads):
        self.N, self.E, self.H = n_nodes, n_edges, heads
        self.NT = -(-n_nodes // P)
        self.LAST = n_nodes - (self.NT - 1) * P
        self.TE = 125
        self.T = n_edges // self.TE
        self.CR, self.CC = 85, 5
        self.K = 464
        self.KR, self.KC = 116, 4
        self.K2 = 448
        assert self.T * self.TE == n_edges and self.CR * self.CC == self.T
        assert self.K >= self.T + self.NT - 1 and self.K % (B * U) == 0
        assert self.KR * self.KC == self.K and self.KR <= P
        assert self.K2 >= n_edges // P + self.NT and self.K2 % (B * U) == 0


def repeat(ap, dim, n):
    shape = list(ap.shape)
    shape.insert(dim, n)
    return ap.unsqueeze(dim).broadcast_to(shape)




class Steps:

    def __init__(self, sem):
        self.sem, self.n = sem, 0

    def inc(self, instruction):
        instruction.then_inc(self.sem, 1)
        self.n += 1
        return self.n


def numbers(nc, engine, table, first, count, top):
    _, values = nc.values_load_multi_w_load_instructions(
        table[0:1, bass.ds(first, count)], engines=[engine.engine], min_val=0, max_val=top,
        skip_runtime_bounds_check_because="prepare() bounds the tables' numbers")
    return values


def passes(engine, count, body):
    body(0)
    with engine.Fori(1, count) as i:
        body(i)


def wait_before(engine, sem, value):
    if not (isinstance(value, int) and value <= 0):
        engine.wait_ge(sem, value)


def numbers_before(nc, engine, table, i, count, top):
    if isinstance(i, int):
        return [None] + list(numbers(nc, engine, table, 0, count - 1, top))
    return numbers(nc, engine, table, i * count - 1, count, top)


def block_numbers_before(nc, engine, table, i, top):
    if isinstance(i, int):
        values = numbers(nc, engine, table, 0, (B - 1) * U, top)
        return [None] + [values[b * U:(b + 1) * U] for b in range(B - 1)]
    values = numbers(nc, engine, table, i * (B * U) - U, B * U, top)
    return [values[b * U:(b + 1) * U] for b in range(B)]


def clear_window(pe, m, ps, width):
    for half in range(U // 2):
        pe.matmul(ps[:, 2 * half:2 * half + 2, 0:width], m.zeros[:, 0:P],
                  m.zeros[:, 0:2 * width].rearrange("o (a w) -> o a w", a=2), start=True, stop=False,
                  skip_group_check=True)


class Tables:
    pass


def prepare(nc, g, m, a):
    with ExitStack() as ctx:
        def sb(name, shape, dt=F32):
            return ctx.enter_context(nc.sbuf_tensor(name, shape, dt))

        def sem(name):
            return ctx.enter_context(nc.semaphore(name))

        CR, CC, TE, K, NT, T, KR, KC = g.CR, g.CC, g.TE, g.K, g.NT, g.T, g.KR, g.KC
        src_i = sb("src_i", [CR, CC, TE], I32)
        dst_i = sb("dst_i", [CR, CC, TE], I32)
        prev_i = sb("prev_i", [CR, CC], I32)
        tile_i = sb("tile_i", [CR, CC, 2], I32)
        src_f = sb("src_f", [CR, CC, TE])
        dst_f = sb("dst_f", [CR, CC, TE])
        prev_f = sb("prev_f", [CR, CC])
        first_f = sb("first_f", [CR, CC, TE])
        ends4 = sb("ends4", [CR, 2, CC, 4])
        tile_f = sb("tile_f", [CR, CC, 2])
        tile_no = sb("tile_no", [CR, CC])
        iota_k = sb("iota_k", [CR, K])
        upto = sb("upto", [CR, CC, K])
        pick = sb("pick", [CR, CC, K])
        bucket_i = sb("bucket_i", [CR, CC * TE], I32)
        bucket_f = sb("bucket_f", [CR, CC * TE], BF16)
        in_b = sb("in_b", [CR, NT, CC * TE], BF16)
        count_b = sb("count_b", [CR, NT])
        run_b = sb("run_b", [CR, 2, CC * TE])
        place = sb("place", [CR, CC * TE])
        before = sb("before", [CR, CR])
        ones = sb("ones", [CR, P])
        one_row = sb("one_row", [P, NT])
        tiles_r = sb("tiles_r", [P, NT])
        tiles_ri = sb("tiles_ri", [P, NT], I32)
        tiles_end = sb("tiles_end", [P, NT])
        start_b = sb("start_b", [CR, NT])
        tiles_c = sb("tiles_c", [NT, 1])
        tiles_ci = sb("tiles_ci", [NT, 1], I32)
        end_c = sb("end_c", [NT, 1])
        uptoc = sb("uptoc", [NT, NT])
        iota_k2 = sb("iota_k2", [NT, g.K2])
        ended = sb("ended", [NT, g.K2])
        slot_k = sb("slot_k", [P, K])
        node_of = sb("node_of", [P, K])
        t_of = sb("t_of", [1, K])
        numbers_f = sb("numbers_f", [1, max(K, g.K2)])
        nk2 = sb("nk2", [1, g.K2])
        work = sb("work", [P, K])
        work_i = sb("work_i", [P, 2, K], I32)
        work2 = sb("work2", [P, K])
        dst_r = sb("dst_r", [KR, KC, TE])
        dst_ri = sb("dst_ri", [KR, KC, TE], I32)
        node_r = sb("node_r", [KR, KC])
        slot_rows = sb("slot_rows", [KR, KC])
        zero = m.x1[:].rearrange("p n d -> p (n d)")[:, 0:g.K2 // 28 * ROWW]

        loaded = sem("loaded")
        weights_in = sem("weights_in")
        cleared = sem("cleared")
        ps = [ctx.enter_context(nc.psum_tensor(f"ps_prep{i}", [P, BANK], F32)) for i in range(8)]
        pool_sem, dve_sem, pe_sem = sem("pool_step"), sem("dve_step"), sem("pe_step")
        block = ctx.enter_context(nc.Block())
        NCLEAR = 28
        MAIN = (NT - 1) * P

        @block.sync
        def _(sp):
            sp.dma_start(src_i[:], a["src"].rearrange("(c r e) -> r c e", c=CC, r=CR)).then_inc(loaded, 16)
            sp.dma_start(dst_i[:], a["dst"].rearrange("(c r e) -> r c e", c=CC, r=CR)).then_inc(loaded, 16)
            ends = a["dst"].rearrange("(t e) -> t e", e=TE)[:, TE - 1:TE]
            sp.wait_ge(pool_sem, 1)
            sp.dma_start(prev_i[1:CR, 0:1], ends[0:CR - 1], allow_slow_non_contiguous=True).then_inc(loaded, 16)
            for c in range(1, CC):
                sp.dma_start(prev_i[:, c:c + 1], ends[c * CR - 1:(c + 1) * CR - 1],
                             allow_slow_non_contiguous=True).then_inc(loaded, 16)
            sp.wait_ge(pool_sem, 2)
            for dst, src in (
                (m.x[:, 0:NT - 1, :], a["x"][0:MAIN].rearrange("(n p) d -> p n d", p=P)),
                (m.x[0:g.LAST, NT - 1, :], a["x"][MAIN:g.N]),
                (m.w0[:], a["W0"].rearrange("(c p) d -> p c d", p=P)),
                (m.w_lr[:, 0, :], a["W_l"]), (m.w_lr[:, 1, :], a["W_r"]), (m.w_e[:], a["W_e"]),
                (m.rows[0:1, 0, :], a["b0"].unsqueeze(0)), (m.rows[0:1, 1, :], a["b_l"].unsqueeze(0)),
                (m.rows[0:1, 2, :], a["b_r"].unsqueeze(0)),
                (m.rows[0:1, 3, :], a["att"].rearrange("h c -> (h c)").unsqueeze(0)),
                (m.rows[0:1, 4, :], a["bias"].unsqueeze(0)),
            ):
                sp.dma_start(dst, src).then_inc(weights_in, 16)
            sp.wait_ge(pool_sem, 3)
            w = g.K2 // NCLEAR
            for i in range(NCLEAR):
                sp.dma_start(m.sorted_rows[:, i * w:(i + 1) * w, :].rearrange("p k w -> p (k w)"),
                             zero).then_inc(cleared, 16)
            sp.wait_ge(cleared, 16 * NCLEAR)
            sp.wait_ge(weights_in, 16 * 11)

        @block.gpsimd
        def _(pool):
            pool.memset(prev_i[:], -1).then_inc(pool_sem, 1)
            pool.memset(m.x[:, NT - 1, :], 0.0).then_inc(pool_sem, 1)
            pool.memset(zero, 0.0).then_inc(pool_sem, 1)
            iota = dict(allow_small_or_imprecise_dtypes=True)
            pool.iota(m.column[:], [[1, P]], 0, 0, **iota).then_inc(pool_sem, 1)
            pool.iota(m.row_no[:], [[0, 1]], 0, 1, **iota).then_inc(pool_sem, 1)
            pool.iota(iota_k[:], [[1, K]], 0, 0, **iota).then_inc(pool_sem, 1)
            pool.iota(tile_no[:], [[CR, CC]], 0, 1, **iota).then_inc(pool_sem, 1)
            pool.iota(slot_k[:], [[1, K]], 0, 0, **iota).then_inc(pool_sem, 1)
            pool.iota(iota_k2[:], [[1, g.K2]], 0, 0, **iota).then_inc(pool_sem, 1)
            pool.iota(slot_rows[:], [[KR, KC]], 0, 1, **iota).then_inc(pool_sem, 1)
            pool.memset(ones[:], 1.0).then_inc(pool_sem, 1)
            pool.memset(one_row[:], 1.0).then_inc(pool_sem, 1)
            pool.memset(m.ones_row[:], 1.0).then_inc(pool_sem, 1)
            pool.memset(m.zeros[:], 0.0).then_inc(pool_sem, 1)

        PE_COUNT, PE_TOTALS, PE_NODE, PE_ENDC, PE_NK2, PE_TABLE, PE_ROWS, PE_PLACE = range(1, 9)
        step = Steps(dve_sem)
        at = {}

        @block.vector
        def _(dve):
            def link(ins):
                dve.wait_ge(dve_sem, step.inc(ins))

            def windows(link, table, base, window, work_f):
                blocks = work_f.rearrange("o (j u) -> o j u", u=U)
                link(dve.tensor_copy(work_f, table[:]))
                link(dve.tensor_copy(base[:], blocks[:, :, 0]))
                link(dve.tensor_tensor(window[:].rearrange("o (j u) -> o j u", u=U), blocks,
                                       repeat(blocks[:, :, 0], 2, U), ALU.subtract))

            dve.wait_ge(pool_sem, 14)
            dve.wait_ge(loaded, 16 * (2 + CC))
            link(dve.tensor_scalar(bucket_i[:], src_i[:].rearrange("r c e -> r (c e)"), 7, None,
                                   ALU.arith_shift_right))
            link(dve.tensor_copy(bucket_f[:], bucket_i[:]))
            for b in range(NT):
                step.inc(dve.tensor_scalar(in_b[:, b, :], bucket_f[:], float(b), None, ALU.is_equal))
            dve.wait_ge(dve_sem, step.n)
            step.inc(dve.tensor_scalar(before[:], m.column[0:CR, 0:CR], m.row_no[0:CR, 0:1], None, ALU.is_gt))
            step.inc(dve.tensor_scalar(uptoc[:], m.column[0:NT, 0:NT], m.row_no[0:NT, 0:1], None, ALU.is_ge))
            step.inc(dve.tensor_scalar(m.ident[:], m.column[:], m.row_no[:, 0:1], None, ALU.is_equal))
            at["count"] = step.inc(dve.tensor_reduce(count_b[:], in_b[:], AX.X, ALU.add))
            step.inc(dve.tensor_copy(src_f[:], src_i[:]))
            step.inc(dve.tensor_copy(dst_f[:], dst_i[:]))
            step.inc(dve.tensor_copy(prev_f[:], prev_i[:]))
            step.inc(dve.tensor_scalar(tile_i[:, :, 0], dst_i[:, :, TE - 1], 7, None, ALU.arith_shift_right))
            link(dve.tensor_scalar(tile_i[:, :, 1], prev_i[:], 7, None, ALU.arith_shift_right))
            link(dve.tensor_copy(tile_f[:], tile_i[:]))
            step.inc(dve.tensor_tensor(tile_f[:, :, 0], tile_f[:, :, 0], tile_no[:], ALU.add))
            link(dve.scalar_tensor_tensor(tile_f[:, :, 1], tile_f[:, :, 1], -1.0, tile_no[:], ALU.add, ALU.add))
            link(dve.tensor_scalar(work2[0:CR, 0:CC], tile_no[:], float(T - 1), float(K), ALU.is_equal, ALU.mult))
            link(dve.tensor_tensor(tile_f[:, :, 0], tile_f[:, :, 0], work2[0:CR, 0:CC], ALU.max))
            for c in range(CC):
                step.inc(dve.tensor_scalar(upto[:, c, :], iota_k[:], tile_f[:, c, 0:1], None, ALU.is_le))
                step.inc(dve.tensor_scalar(pick[:, c, :], iota_k[:], tile_f[:, c, 1:2], None, ALU.is_gt))
            dve.wait_ge(dve_sem, step.n)
            link(dve.tensor_tensor(pick[:], pick[:], upto[:], ALU.mult))
            step.inc(dve.tensor_tensor(first_f[:, :, 1:TE], dst_f[:, :, 1:TE], dst_f[:, :, 0:TE - 1], ALU.not_equal))
            step.inc(dve.tensor_tensor(first_f[:, :, 0], dst_f[:, :, 0], prev_f[:], ALU.not_equal))
            step.inc(dve.tensor_copy(ends4[:, 0], repeat(dst_f[:, :, 0], 2, 4)))
            at["pick"] = step.inc(dve.tensor_copy(ends4[:, 1], repeat(dst_f[:, :, TE - 1], 2, 4)))
            dve.wait_ge(dve_sem, step.n)
            dve.wait_ge(pe_sem, PE_COUNT)
            step.inc(dve.tensor_scalar(tiles_ri[:], ps[0][:, 0:NT], float(P - 1), float(P), ALU.add, ALU.max))
            link(dve.tensor_scalar(tiles_ci[:], ps[1][0:NT, 0:1], float(P - 1), float(P), ALU.add, ALU.max))
            step.inc(dve.tensor_scalar(tiles_ri[:], tiles_ri[:], 7, None, ALU.arith_shift_right))
            link(dve.tensor_scalar(tiles_ci[:], tiles_ci[:], 7, None, ALU.arith_shift_right))
            step.inc(dve.tensor_copy(tiles_r[:], tiles_ri[:]))
            at["tiles_c"] = step.inc(dve.tensor_copy(tiles_c[:], tiles_ci[:]))
            dve.wait_ge(dve_sem, step.n)
            link(dve.tensor_tensor_scan(tiles_end[:], one_row[:], tiles_r[:], 0.0, ALU.mult, ALU.add))
            link(dve.tensor_tensor(tiles_end[:], tiles_end[:], tiles_r[:], ALU.subtract))
            link(dve.tensor_scalar(start_b[:], tiles_end[0:CR, :], float(P), -1.0, ALU.mult, ALU.add))
            dve.wait_ge(pe_sem, PE_TOTALS)
            link(dve.tensor_tensor(start_b[:], start_b[:], ps[2][0:CR, 0:NT], ALU.add))
            link(dve.memset(place[:], 0.0))
            for b in range(NT):
                link(dve.tensor_tensor_scan(run_b[:, b % 2, :], repeat(ones[:, 0], 1, CC * TE), in_b[:, b, :],
                                            start_b[:, b:b + 1], ALU.mult, ALU.add))
                link(dve.tensor_tensor(run_b[:, b % 2, :], run_b[:, b % 2, :], in_b[:, b, :], ALU.mult))
                link(dve.tensor_tensor(place[:], place[:], run_b[:, b % 2, :], ALU.add))
            at["place"] = step.n
            dve.wait_ge(pe_sem, PE_NODE)
            link(dve.scalar_tensor_tensor(node_of[:], slot_k[:], float(-T), ps[3][:, 0:K], ALU.add, ALU.add))
            step.inc(dve.tensor_scalar(m.node_i[:], node_of[0:1, :], float(NT - 1), None, ALU.min))
            link(dve.tensor_tensor(t_of[:], slot_k[0:1, :], node_of[0:1, :], ALU.subtract))
            windows(link, m.node_i, m.base_i, m.window_i, numbers_f[:, 0:K])
            link(dve.tensor_copy(m.tile_i[:], t_of[:]))
            dve.wait_ge(pe_sem, PE_ENDC)
            link(dve.tensor_copy(end_c[:], ps[1][0:NT, 1:2]))
            at["ended"] = step.inc(dve.tensor_scalar(ended[:], iota_k2[:], end_c[:, 0:1], None, ALU.is_ge))
            dve.wait_ge(pe_sem, PE_NK2)
            link(dve.tensor_scalar(m.node2_i[:], ps[0][0:1, 0:g.K2], float(NT - 1), None, ALU.min))
            at["done_banks"] = step.n
            windows(link, m.node2_i, m.base2_i, m.window2_i, numbers_f[:, 0:g.K2])
            dve.wait_ge(pe_sem, PE_TABLE)
            link(dve.scalar_tensor_tensor(m.dst_lo[0:TE, :], node_of[0:TE, :], float(-P), ps[5][0:TE, 0:K],
                                          ALU.mult, ALU.add))
            step.inc(dve.tensor_copy(m.first[0:TE, :], ps[6][0:TE, 0:K]))
            link(dve.tensor_copy(m.src_idx[:], ps[4][0:TE, 0:K]))
            link(dve.tensor_scalar(work_i[0:TE, 0, :], m.src_idx[:], P - 1, None, ALU.bitwise_and))
            link(dve.tensor_copy(m.src_lo[:], work_i[0:TE, 0, :]))
            dve.wait_ge(pe_sem, PE_ROWS)
            step.inc(dve.tensor_copy(dst_r[:], ps[7][0:KR, 0:KC * TE].rearrange("k (c e) -> k c e", c=KC)))
            link(dve.scalar_tensor_tensor(node_r[:], ps[2][0:KR, 32:32 + KC], float(-T), slot_rows[:],
                                          ALU.add, ALU.add))
            link(dve.tensor_copy(dst_ri[:], dst_r[:]))
            link(dve.tensor_scalar(dst_ri[:], dst_ri[:], 7, None, ALU.arith_shift_right))
            for c in range(KC):
                link(dve.tensor_scalar(m.others[:, c, :], dst_ri[:, c, :], node_r[:, c:c + 1], -BIG,
                                       ALU.not_equal, ALU.mult))
                for h in range(g.H):
                    step.inc(dve.memset(m.begins[:, c, h, 0:1], -BIG))
                    step.inc(dve.memset(m.ends[:, c, h, TE - 1:TE], -BIG))
                    step.inc(dve.tensor_tensor(m.begins[:, c, h, 1:TE], dst_r[:, c, 1:TE], dst_r[:, c, 0:TE - 1],
                                               ALU.not_equal))
                    step.inc(dve.tensor_tensor(m.ends[:, c, h, 0:TE - 1], dst_r[:, c, 1:TE], dst_r[:, c, 0:TE - 1],
                                               ALU.not_equal))
                dve.wait_ge(dve_sem, step.n)
                step.inc(dve.tensor_scalar(m.begins[:, c, :, 1:TE], m.begins[:, c, :, 1:TE], -BIG, None, ALU.mult))
                step.inc(dve.tensor_scalar(m.ends[:, c, :, 0:TE - 1], m.ends[:, c, :, 0:TE - 1], -BIG, None, ALU.mult))
                step.inc(dve.tensor_scalar(m.not_first[:, c, :], dst_r[:, c, :], dst_r[:, c, 0:1], -BIG,
                                           ALU.not_equal, ALU.mult))
                link(dve.tensor_scalar(m.not_last[:, c, :], dst_r[:, c, :], dst_r[:, c, TE - 1:TE], -BIG,
                                       ALU.not_equal, ALU.mult))
            dve.wait_ge(pe_sem, PE_PLACE)
            step.inc(dve.tensor_copy(m.end_rows[:, 0, :], ps[0][0:4, 0:K]))
            link(dve.tensor_copy(m.end_rows[:, 1, :], ps[1][0:4, 0:K]))
            step.inc(dve.tensor_tensor(m.whole[:], m.end_rows[:, 0, :], m.end_rows[:, 1, :], ALU.not_equal))
            link(dve.tensor_tensor(m.joined[:, 1:K], m.end_rows[:, 0, 1:K], m.end_rows[:, 1, 0:K - 1], ALU.not_equal))
            step.inc(dve.tensor_scalar(m.whole[:], m.whole[:], -BIG, None, ALU.mult))
            link(dve.tensor_scalar(m.joined[:, 1:K], m.joined[:, 1:K], -BIG, None, ALU.mult))
            link(dve.tensor_copy(work_i[0:TE, 0, :], ps[3][0:TE, 0:K]))
            link(dve.tensor_scalar(work_i[0:TE, 1, :], work_i[0:TE, 0, :], P - 1, None, ALU.bitwise_and))
            link(dve.tensor_scalar(work_i[0:TE, 0, :], work_i[0:TE, 0, :], 7, None, ALU.arith_shift_right))
            link(dve.tensor_copy(work2[0:TE, :], work_i[0:TE, 0, :]))
            link(dve.scalar_tensor_tensor(work2[0:TE, :], work_i[0:TE, 1, :], float(g.K2), work2[0:TE, :],
                                          ALU.mult, ALU.add))
            link(dve.tensor_scalar(work[0:TE, :], m.dst_lo[0:TE, :], 0.0, float(P * g.K2), ALU.is_lt, ALU.mult))
            link(dve.tensor_tensor(work2[0:TE, :], work2[0:TE, :], work[0:TE, :], ALU.add))
            link(dve.tensor_scalar(work[0:TE, :], m.dst_lo[0:TE, :], float(P), float(P * g.K2), ALU.is_ge, ALU.mult))
            link(dve.tensor_tensor(work2[0:TE, :], work2[0:TE, :], work[0:TE, :], ALU.add))
            link(dve.tensor_copy(m.place_idx[:], work2[0:TE, :]))

        @block.tensor
        def _(pe):
            pe.wait_ge(dve_sem, at["count"])
            pe.matmul(ps[0][:, 0:NT], ones[:], count_b[:], start=True, stop=True)
            pe.matmul(ps[1][0:NT, 0:1], count_b[:], ones[:, 0:1], start=True, stop=True).then_inc(pe_sem, 1)
            pe.matmul(ps[2][0:CR, 0:NT], before[:], count_b[:], start=True, stop=True).then_inc(pe_sem, 1)
            pe.wait_ge(dve_sem, at["pick"])
            for c in range(CC):
                mm = pe.matmul(ps[3][:, 0:K], ones[:], upto[:, c, :], start=(c == 0), stop=(c == CC - 1))
            mm.then_inc(pe_sem, 1)
            pe.wait_ge(dve_sem, at["tiles_c"])
            pe.matmul(ps[1][0:NT, 1:2], uptoc[:], tiles_c[:], start=True, stop=True).then_inc(pe_sem, 1)
            pe.wait_ge(dve_sem, at["ended"])
            pe.matmul(ps[0][0:1, 0:g.K2], ones[0:NT, 0:1], ended[:], start=True, stop=True).then_inc(pe_sem, 1)
            for bank, table in ((4, src_f), (5, dst_f), (6, first_f)):
                for c in range(CC):
                    mm = pe.matmul(ps[bank][0:TE, 0:K], table[:, c, :], pick[:, c, :],
                                   start=(c == 0), stop=(c == CC - 1))
            mm.then_inc(pe_sem, 1)
            for q in range(KC):
                for c in range(CC):
                    pe.matmul(ps[7][0:KR, q * TE:(q + 1) * TE], pick[:, c, q * KR:(q + 1) * KR], dst_f[:, c, :],
                              start=(c == 0), stop=(c == CC - 1))
                for c in range(CC):
                    mm = pe.matmul(ps[2][0:KR, 32 + q:33 + q], upto[:, c, q * KR:(q + 1) * KR], ones[:, 0:1],
                                   start=(c == 0), stop=(c == CC - 1))
            mm.then_inc(pe_sem, 1)
            pe.wait_ge(dve_sem, at["done_banks"])
            for which in range(2):
                for c in range(CC):
                    pe.matmul(ps[which][0:4, 0:K], ends4[:, which, c, :], pick[:, c, :],
                              start=(c == 0), stop=(c == CC - 1))
            for c in range(CC):
                mm = pe.matmul(ps[3][0:TE, 0:K], place[:, c * TE:(c + 1) * TE], pick[:, c, :],
                               start=(c == 0), stop=(c == CC - 1))
            mm.then_inc(pe_sem, 1)


def spread(nc, g, m, a):
    NB = g.K // U
    TE = g.TE
    with ExitStack() as ctx:
        def sb(name, shape, dt=F32):
            return ctx.enter_context(nc.sbuf_tensor(name, shape, dt))

        def sem(name):
            return ctx.enter_context(nc.semaphore(name))

        attr = [sb(f"attr{b}", [TE, U, P + 1]) for b in range(B)]
        onehot = [sb(f"onehot{b}", [TE, U, P]) for b in range(2)]
        onehot_t = [sb(f"onehot_t{b}", [P, U, TE]) for b in range(2)]
        row = [sb(f"row{b}", [TE, U, ROWW]) for b in range(B)]
        index = [sb(f"index{b}", [TE, U], I32) for b in range(B)]
        ps_t = [ctx.enter_context(nc.psum_tensor(f"ps_t{b}", [P, BANK], F32)) for b in range(2)]
        ps_x = [ctx.enter_context(nc.psum_tensor(f"ps_x{b}", [P, BANK], F32)) for b in range(2)]
        ps_a = [ctx.enter_context(nc.psum_tensor(f"ps_a{b}", [P, 2, BANK], F32)) for b in range(2)]
        attr_in = [sem(f"attr_in{b}") for b in range(B)]
        row_out = [sem(f"row_out{b}") for b in range(B)]
        block_summed, onehot_ready = sem("block_summed"), sem("onehot_ready")
        turned, turned_copied, spread_done, row_copied = (
            sem("turned"), sem("turned_copied"), sem("spread_done"), sem("row_copied"))
        meta_ready, sums_free, added = sem("meta_ready"), sem("sums_free"), sem("added")
        preset = sem("preset")
        index_ready, begun = sem("index_ready"), sem("begun")
        block = ctx.enter_context(nc.Block())

        @block.sync
        def _(sp):
            def one_pass(i):
                tiles = numbers(nc, sp, m.tile_i, i * (B * U), B * U, g.T - 1)
                for b in range(B):
                    wait_before(sp, block_summed, i * B + (b - 1))
                    for u in range(U):
                        sp.dma_start(attr[b][:, u, 0:P], a["ea"][bass.ds(tiles[b * U + u] * TE, TE), :]).then_inc(attr_in[b], 16)

            passes(sp, NB // B, one_pass)

        @block.gpsimd
        def _(pool):
            limit = pool.to_reg(P * g.K2 - 1)
            def one_pass(i):
                for b in range(B):
                    wait_before(pool, row_out[b], i * (16 * U))
                    pool.tensor_copy(index[b][:], m.place_idx[:, bass.ds(i * (B * U) + b * U, U)]).then_inc(
                        index_ready, 1)
                    pool.wait_ge(index_ready, i * B + b + 1)
                    pool.wait_ge(row_copied, i * B + b + 3)
                    pool.wait_ge(meta_ready, i * B + b + 2)
                    pool.sem_inc(begun, 1)
                    for u in range(U):
                        pool.indirect_dma_start(
                            out=m.sorted_rows.rearrange("p k w -> (p k) w"),
                            out_offset=bass.IndirectOffsetOnAxis(ap=index[b][:, u:u + 1], axis=0),
                            in_=row[b][:, u, :], in_offset=None,
                            bounds_check=limit, oob_is_err=False).then_inc(row_out[b], 16)

            passes(pool, NB // B, one_pass)
            for b in range(B):
                pool.wait_ge(row_out[b], 16 * U * (NB // B))

        @block.scalar
        def _(act):
            act.sem_inc(row_copied, 2)
            def one_pass(i):
                for b in range(B):
                    act.wait_ge(turned, i * B + b + 1)
                    act.copy(onehot_t[b % 2][:], ps_t[b % 2][:, 0:U * TE].rearrange("p (u e) -> p u e", u=U)).then_inc(
                        turned_copied, 1)
                    act.wait_ge(spread_done, i * B + b + 1)
                    wait_before(act, row_out[b], i * (16 * U))
                    act.copy(row[b][:, :, 0:P], ps_x[b % 2][0:TE, :].rearrange("p (u d) -> p u d", u=U)).then_inc(
                        row_copied, 1)

            passes(act, NB // B, one_pass)

        @block.vector
        def _(dve):
            for b in range(B):
                dve.memset(attr[b][:, :, P:P + 1], 1.0).then_inc(preset, 1)
                dve.memset(row[b][:, :, P:ROWW], 1.0).then_inc(preset, 1)
            dve.memset(m.attr_sum[:], 0.0).then_inc(added, 1)
            dve.wait_ge(preset, 2 * B)
            dve.sem_inc(meta_ready, 1)
            dve.sem_inc(sums_free, 2)
            def add_sums(j, nodes, parity):
                dve.wait_ge(block_summed, j + 3)
                for u in range(U):
                    acc = m.attr_sum[:, bass.ds(nodes[u], 1), :]
                    dve.wait_ge(added, j * U + (u + 1))
                    dve.tensor_tensor(acc, acc, ps_a[parity][:, u // 2, (u % 2) * 256:(u % 2) * 256 + P + 1].unsqueeze(1),
                                      ALU.add).then_inc(added, 1)
                dve.wait_ge(added, j * U + (U + 1))
                dve.sem_inc(sums_free, 1)

            def one_pass(i):
                nodes = block_numbers_before(nc, dve, m.node_i, i, g.NT - 1)
                for b in range(B):
                    k0 = i * (B * U) + b * U
                    dve.wait_ge(block_summed, i * B + b + 1)
                    dve.tensor_tensor(onehot[b % 2][:], repeat(m.column[0:TE, :], 1, U),
                                      repeat(m.dst_lo[0:TE, bass.ds(k0, U)], 2, P),
                                      ALU.is_equal).then_inc(onehot_ready, 1)
                    wait_before(dve, row_out[b], i * (16 * U))
                    dve.tensor_copy(row[b][:, :, P + 1], m.src_lo[:, bass.ds(k0, U)]).then_inc(meta_ready, 1)
                    if nodes[b] is not None:
                        add_sums(i * B + (b - 1), nodes[b], (b - 1) % 2)

            passes(dve, NB // B, one_pass)
            add_sums(NB - 1, numbers(nc, dve, m.node_i, g.K - U, U, g.NT - 1), (NB - 1) % 2)

        @block.tensor
        def _(pe):
            pe.sem_inc(block_summed, 2)
            pe.wait_ge(preset, 2 * B)
            def one_pass(i):
                nodes = numbers(nc, pe, m.node_i, i * (B * U), B * U, g.NT - 1)
                for b in range(B):
                    k0 = i * (B * U) + b * U
                    pe.wait_ge(onehot_ready, i * B + b + 1)
                    for u in range(U):
                        mm = pe.transpose(ps_t[b % 2][:, u * TE:(u + 1) * TE], onehot[b % 2][:, u, :], m.ident[0:TE, 0:TE])
                    mm.then_inc(turned, 1)
                    pe.wait_ge(attr_in[b], (i + 1) * (16 * U))
                    pe.wait_ge(sums_free, i * B + b + 1)
                    for u in range(U):
                        mm = pe.matmul(ps_a[b % 2][:, u // 2, (u % 2) * 256:(u % 2) * 256 + P + 1], onehot[b % 2][:, u, :],
                                       attr[b][:, u, :], start=True, stop=True)
                    mm.then_inc(block_summed, 1)
                    pe.wait_ge(turned_copied, i * B + b + 1)
                    pe.wait_ge(row_copied, i * B + b + 1)
                    for u in range(U):
                        mm = pe.matmul(ps_x[b % 2][0:TE, u * P:(u + 1) * P], onehot_t[b % 2][:, u, :],
                                       m.x[:, bass.ds(nodes[b * U + u], 1), :], start=True, stop=True)
                    mm.then_inc(spread_done, 1)

            passes(pe, NB // B, one_pass)

def gather_src(nc, g, m):
    NB = g.K2 // U
    with ExitStack() as ctx:
        def sb(name, shape, dt=F32):
            return ctx.enter_context(nc.sbuf_tensor(name, shape, dt))

        def sem(name):
            return ctx.enter_context(nc.semaphore(name))

        row = [sb(f"row_in{b}", [P, U, ROWW]) for b in range(B)]
        onehot = [sb(f"onehot_s{b}", [P, U, P]) for b in range(2)]
        ps = [ctx.enter_context(nc.psum_tensor(f"ps_src{b}", [P, U, BANK // 2], F32)) for b in range(2)]
        row_in = [sem(f"row_in_sem{b}") for b in range(B)]
        onehot_ready, block_summed, added = (
            sem("onehot_ready_s"), sem("block_summed_s"), sem("added_s"))
        block = ctx.enter_context(nc.Block())

        @block.sync
        def _(sp):
            def one_pass(i):
                for b in range(B):
                    wait_before(sp, block_summed, i * B + (b - 1))
                    sp.dma_start(row[b][:], m.sorted_rows[:, bass.ds(i * (B * U) + b * U, U), :]).then_inc(
                        row_in[b], 16)

            passes(sp, NB // B, one_pass)

        @block.vector
        def _(dve):
            dve.memset(m.src_sum[:], 0.0).then_inc(added, 1)

            def add_sums(j, base, parity):
                acc = m.src_sum[:, bass.ds(base, U), :]
                dve.wait_ge(block_summed, j + 3)
                dve.wait_ge(added, j + 1)
                dve.tensor_tensor(acc, acc, ps[parity][:, :, 0:P + 1], ALU.add).then_inc(added, 1)

            def one_pass(i):
                bases = numbers_before(nc, dve, m.base2_i, i, B, g.NT - 1)
                for b in range(B):
                    dve.wait_ge(row_in[b], i * 16 + 16)
                    dve.wait_ge(block_summed, i * B + b + 1)
                    dve.tensor_tensor(onehot[b % 2][:], repeat(m.column[:], 1, U), repeat(row[b][:, :, P + 1], 2, P),
                                      ALU.is_equal).then_inc(onehot_ready, 1)
                    if bases[b] is not None:
                        add_sums(i * B + (b - 1), bases[b], (b - 1) % 2)

            passes(dve, NB // B, one_pass)
            add_sums(NB - 1, numbers(nc, dve, m.base2_i, NB - 1, 1, g.NT - 1)[0], (NB - 1) % 2)

        @block.tensor
        def _(pe):
            pe.sem_inc(block_summed, 2)

            def one_pass(i):
                window = numbers(nc, pe, m.window2_i, i * (B * U), B * U, U - 1)
                for b in range(B):
                    pe.wait_ge(onehot_ready, i * B + b + 1)
                    wait_before(pe, added, i * B + b)
                    clear_window(pe, m, ps[b % 2], P + 1)
                    for u in range(U):
                        mm = pe.matmul(ps[b % 2][:, bass.ds(window[b * U + u], 1), 0:P + 1],
                                       onehot[b % 2][:, u, :], row[b][:, u, 0:P + 1], start=False, stop=(u == U - 1),
                                       skip_group_check=True)
                    mm.then_inc(block_summed, 1)

            passes(pe, NB // B, one_pass)


def layer_norm(g, vec, wait_sqrt, sqrt_step, y, square, stats, done, sqrt_ready):
    D = y.shape[2]

    def link(ins):
        vec.wait_ge(done.sem, done.inc(ins))

    mean, var, rstd = stats[:, 0, :], stats[:, 1, :], stats[:, 2, :]
    link(vec.tensor_reduce(mean, y[:], AX.X, ALU.add))
    link(vec.tensor_scalar(mean, mean, 1.0 / D, None, ALU.mult))
    link(vec.tensor_tensor(y[:], y[:], repeat(mean, 2, D), ALU.subtract))
    link(vec.tensor_tensor(square[:], y[:], y[:], ALU.mult))
    link(vec.tensor_reduce(var, square[:], AX.X, ALU.add))
    link(vec.tensor_scalar(var, var, 1.0 / D, LN_EPS, ALU.mult, ALU.add))
    vec.sem_inc(sqrt_ready, 1)
    vec.wait_ge(wait_sqrt, sqrt_step)
    link(vec.reciprocal(rstd, rstd))
    link(vec.tensor_tensor(y[:], y[:], repeat(rstd, 2, D), ALU.mult))


def nodes(nc, g, m):
    NT, BN = g.NT, 5
    D = P
    with ExitStack() as ctx:
        def sb(name, shape, dt=F32):
            return ctx.enter_context(nc.sbuf_tensor(name, shape, dt))

        def sem(name):
            return ctx.enter_context(nc.semaphore(name))

        pair = [sb(f"pair{b}", [P, 2, D]) for b in range(BN)]
        pair_t = [sb(f"pair_t{b}", [P, 2, P]) for b in range(BN)]
        square = sb("square", [P, NT, D])
        stats = sb("stats", [P, 3, NT])
        degree = sb("degree", [P, 2, NT])
        ps = [ctx.enter_context(nc.psum_tensor(f"ps_node{b}", [P, BANK], F32)) for b in range(BN)]
        ps_att = ctx.enter_context(nc.psum_tensor("ps_att", [P, BANK], F32))
        steps_sem, ready, sqrt_ready, sqrt_done = sem("node_steps"), sem("node_ready"), sem("sqrt_ready"), sem("sqrt_done")
        paired, turned, copied, product, stored = (
            sem("paired"), sem("node_turned"), sem("node_copied"), sem("node_product"), sem("node_stored"))
        loop_product, table_out, att_ready = sem("loop_product"), sem("table_out"), sem("att_ready")
        block = ctx.enter_context(nc.Block())
        step = Steps(steps_sem)
        at = {}

        @block.vector
        def _(dve):
            def link(ins):
                dve.wait_ge(steps_sem, step.inc(ins))

            link(dve.tensor_scalar(degree[:, 0, :], m.src_sum[:, 0:NT, D], DEG_EPS, None, ALU.add))
            link(dve.tensor_scalar(degree[:, 1, :], m.attr_sum[:, :, D], 1.0, None, ALU.max))
            link(dve.reciprocal(degree[:], degree[:]))
            link(dve.tensor_tensor(m.src_sum[:, 0:NT, 0:D], m.src_sum[:, 0:NT, 0:D], repeat(degree[:, 0, :], 2, D), ALU.mult))
            at["means"] = step.n
            link(dve.tensor_tensor(m.attr_sum[:, :, 0:D], m.attr_sum[:, :, 0:D], repeat(degree[:, 1, :], 2, D),
                                   ALU.mult))
            dve.wait_ge(att_ready, 1)
            link(dve.tensor_copy(m.att[:], ps_att[:, 0:D]))
            dve.sem_inc(stored, 1)
            def one_pass(i):
                for b in range(BN):
                    dve.wait_ge(product, i * BN + b + 1)
                    dve.scalar_tensor_tensor(m.x1[:, bass.ds(i * BN + b, 1), :], ps[b][:, 256:384].unsqueeze(1), 0.0,
                                             pair[b][:, 0:1, :], ALU.max, ALU.add).then_inc(stored, 1)

            passes(dve, NT // BN, one_pass)
            dve.wait_ge(stored, NT + 1)
            layer_norm(g, dve, sqrt_done, 1, m.x1, square, stats, step, sqrt_ready)
            at["x1"] = step.n
            dve.wait_ge(stored, 2 * NT + 1)
            link(dve.tensor_tensor(square[:], square[:], m.x[:], ALU.add))
            link(dve.tensor_tensor(square[:], square[:], m.src_sum[:, 0:NT, 0:D], ALU.add))
            link(dve.scalar_tensor_tensor(square[:], square[:], SLOPE, square[:], ALU.mult, ALU.max))
            link(dve.tensor_tensor(square[:], square[:], repeat(m.att[:], 1, NT), ALU.mult))
            link(dve.tensor_reduce(m.loop_score[:], square[:].rearrange("p n (h c) -> p n h c", h=g.H), AX.X, ALU.add))

        @block.gpsimd
        def _(pool):
            for which in range(2):
                if which == 0:
                    pool.wait_ge(steps_sem, at["means"])
                else:
                    pool.wait_ge(steps_sem, at["x1"])
                first, second = ((m.x, m.src_sum), (m.x1, m.attr_sum))[which]
                def one_pass(i):
                    for b in range(BN):
                        pool.wait_ge(stored, i * BN + (which * NT + 1))
                        n = i * BN + b
                        pool.tensor_copy(pair[b][:, 0:1, :], first[:, bass.ds(n, 1), :]).then_inc(paired, 1)
                        pool.tensor_copy(pair[b][:, 1:2, :], second[:, bass.ds(n, 1), 0:D]).then_inc(paired, 1)

                passes(pool, NT // BN, one_pass)

        @block.scalar
        def _(act):
            for which in range(2):
                if which == 1:
                    act.wait_ge(sqrt_ready, 1)
                    act.activation(stats[:, 2, :], stats[:, 1, :], ACT.Sqrt).then_inc(sqrt_done, 1)
                def one_pass(i):
                    for b in range(BN):
                        act.wait_ge(turned, i * BN + (which * NT + b + 1))
                        act.copy(pair_t[b][:], ps[b][:, 0:256].rearrange("p (c n) -> p c n", c=2)).then_inc(copied, 1)
                    if which == 1:
                        for b in range(BN):
                            n = i * BN + b
                            act.wait_ge(product, i * BN + (NT + b + 1))
                            act.copy(m.x[:, bass.ds(n, 1), :], ps[b][:, 256:384].unsqueeze(1))
                            act.copy(m.src_sum[:, bass.ds(n, 1), 0:D], ps[b][:, 384:512].unsqueeze(1))
                            act.copy(square[:, bass.ds(n, 1), :], ps[b][:, 0:128].unsqueeze(1)).then_inc(stored, 1)

                passes(act, NT // BN, one_pass)

            act.wait_ge(stored, 2 * NT + 1)
            act.dma_start(m.xl_rows.rearrange("(n p) d -> p n d", p=P), m.x[:]).then_inc(table_out, 16)
            act.wait_ge(table_out, 16)

        @block.tensor
        def _(pe):
            pe.matmul(ps_att[:, 0:D], m.ones_row[:], m.rows[0:1, 3, :], start=True, stop=True).then_inc(att_ready, 1)
            for which in range(2):
                def one_pass(i):
                    for b in range(BN):
                        pe.wait_ge(paired, i * (2 * BN) + (which * 2 * NT + 2 * b + 2))
                        for c in range(2):
                            mm = pe.transpose(ps[b][:, c * P:(c + 1) * P], pair[b][:, c, :], m.ident[:])
                        mm.then_inc(turned, 1)
                    for b in range(BN):
                        pe.wait_ge(copied, i * BN + (which * NT + b + 1))
                        if which == 0:
                            pe.matmul(ps[b][:, 256:384], pair_t[b][:, 0, :], m.w0[:, 0, :], start=True, stop=False)
                            pe.matmul(ps[b][:, 256:384], pair_t[b][:, 1, :], m.w0[:, 1, :], start=False, stop=False)
                            pe.matmul(ps[b][:, 256:384], m.ones_row[:], m.rows[0:1, 0, :],
                                      start=False, stop=True).then_inc(product, 1)
                        else:
                            pe.matmul(ps[b][:, 256:512], pair_t[b][:, 0, :], m.w_lr[:].rearrange("p c d -> p (c d)"),
                                      start=True, stop=False)
                            pe.matmul(ps[b][:, 256:512], m.ones_row[:], m.rows[0:1, 1:3, :].rearrange("p c d -> p (c d)"),
                                      start=False, stop=True)
                            pe.matmul(ps[b][:, 0:128], pair_t[b][:, 1, :], m.w_e[:], start=True,
                                      stop=True).then_inc(product, 1)

                passes(pe, NT // BN, one_pass)

def scores(nc, g, m, a):
    NB = g.K // U
    TE = g.TE
    with ExitStack() as ctx:
        def sb(name, shape, dt=F32):
            return ctx.enter_context(nc.sbuf_tensor(name, shape, dt))

        def sem(name):
            return ctx.enter_context(nc.semaphore(name))

        attr = [sb(f"attr_c{b}", [TE, U, P]) for b in range(B)]
        xl = [sb(f"xl{b}", [TE, U, P]) for b in range(B)]
        index = [sb(f"index_c{b}", [TE, U], I32) for b in range(B)]
        onehot = [sb(f"onehot_c{b}", [TE, U, P]) for b in range(2)]
        onehot_t = [sb(f"onehot_ct{b}", [P, U, TE]) for b in range(2)]
        attr_t = [sb(f"attr_t{b}", [P, U, TE]) for b in range(2)]
        work = [sb(f"work_c{b}", [TE, U, P]) for b in range(2)]
        ps_t = [ctx.enter_context(nc.psum_tensor(f"ps_ct{b}", [P, BANK], F32)) for b in range(2)]
        ps_e = [ctx.enter_context(nc.psum_tensor(f"ps_ce{b}", [P, BANK], F32)) for b in range(2)]
        ps_s = [ctx.enter_context(nc.psum_tensor(f"ps_cs{b}", [P, BANK], F32)) for b in range(2)]
        attr_in = [sem(f"attr_c_in{b}") for b in range(B)]
        xl_in = [sem(f"xl_in{b}") for b in range(B)]
        xl_out = [sem(f"xl_out{b}") for b in range(B)]
        index_ready, begun, onehot_ready, turned, turned_copied = (
            sem("index_c_ready"), sem("begun_c"), sem("onehot_c_ready"), sem("turned_c"), sem("turned_c_copied"))
        attr_turned, attr_copied, summed, score_steps, xl_used = (
            sem("attr_turned"), sem("attr_copied"), sem("summed_c"), sem("score_steps"), sem("xl_used"))
        block = ctx.enter_context(nc.Block())

        @block.sync
        def _(sp):
            def keep_xl(i, b):
                sp.wait_ge(xl_in[b], i * (16 * U) + 16 * U)
                sp.dma_start(m.xl_edges[:, bass.ds(i * (B * U) + b * U, U), :], xl[b][:]).then_inc(xl_out[b], 16)

            def one_pass(i):
                tiles = numbers(nc, sp, m.tile_i, i * (B * U), B * U, g.T - 1)
                for b in range(B):
                    sp.wait_ge(attr_turned, i * B + b + 1)
                    for u in range(U):
                        sp.dma_start(attr[b][:, u, :], a["ea"][bass.ds(tiles[b * U + u] * TE, TE), :]).then_inc(
                            attr_in[b], 16)
                    if b >= 2:
                        keep_xl(i, b - 2)
                    elif not isinstance(i, int):
                        keep_xl(i - 1, b + 2)

            passes(sp, NB // B, one_pass)
            for b in range(2, B):
                keep_xl(NB // B - 1, b)
            for b in range(B):
                sp.wait_ge(xl_out[b], 16 * (NB // B))

        @block.gpsimd
        def _(pool):
            def one_pass(i):
                for b in range(B):
                    wait_before(pool, xl_in[b], i * (16 * U))
                    wait_before(pool, xl_out[b], i * 16)
                    pool.wait_ge(xl_used, i * B + b + 1)
                    pool.tensor_copy(index[b][:], m.src_idx[:, bass.ds(i * (B * U) + b * U, U)]).then_inc(
                        index_ready, 1)
                    pool.wait_ge(index_ready, i * B + b + 1)
                    pool.sem_inc(begun, 1)
                    for u in range(U):
                        pool.indirect_dma_start(
                            out=xl[b][:, u, :], out_offset=None, in_=m.xl_rows,
                            in_offset=bass.IndirectOffsetOnAxis(ap=index[b][:, u:u + 1], axis=0)).then_inc(xl_in[b], 16)

            passes(pool, NB // B, one_pass)

        @block.scalar
        def _(act):
            def one_pass(i):
                for b in range(B):
                    act.wait_ge(attr_turned, i * B + b + 1 + B)
                    wait_before(act, summed, i * B + (b + 1))
                    act.copy(attr_t[b % 2][:], ps_e[b % 2][:, 0:U * TE].rearrange("p (u e) -> p u e", u=U)).then_inc(
                        attr_copied, 1)
                    act.wait_ge(turned, i * B + b + 1)
                    act.copy(onehot_t[b % 2][:], ps_t[b % 2][:, 0:U * TE].rearrange("p (u e) -> p u e", u=U)).then_inc(
                        turned_copied, 1)

            passes(act, NB // B, one_pass)

        @block.vector
        def _(dve):
            dve.sem_inc(xl_used, B)
            dve.sem_inc(score_steps, 1)

            def score_block(i, b):
                k0 = i * (B * U) + b * U
                s = work[b % 2]
                base = i * (4 * B) + 4 * b
                dve.wait_ge(xl_in[b], i * (16 * U) + 16 * U)
                dve.wait_ge(summed, i * B + b + 3)
                dve.wait_ge(score_steps, base + 1)
                dve.tensor_tensor(s[:], ps_s[b % 2][0:TE, :].rearrange("p (u d) -> p u d", u=U), xl[b][:],
                                  ALU.add).then_inc(score_steps, 1)
                dve.wait_ge(score_steps, base + 2)
                dve.sem_inc(xl_used, 1)
                dve.scalar_tensor_tensor(s[:], s[:], SLOPE, s[:], ALU.mult, ALU.max).then_inc(score_steps, 1)
                dve.wait_ge(score_steps, base + 3)
                dve.tensor_tensor(s[:], s[:], repeat(m.att[0:TE, :], 1, U), ALU.mult).then_inc(score_steps, 1)
                dve.wait_ge(score_steps, base + 4)
                dve.tensor_reduce(m.score[:, :, bass.ds(k0, U)].rearrange("p h u -> p u h"),
                                  s[:].rearrange("p u (h c) -> p u h c", h=g.H), AX.X, ALU.add).then_inc(score_steps, 1)

            def one_pass(i):
                for b in range(B):
                    wait_before(dve, turned, i * B + (b - 1))
                    dve.tensor_tensor(onehot[b % 2][:], repeat(m.column[0:TE, :], 1, U),
                                      repeat(m.dst_lo[0:TE, bass.ds(i * (B * U) + b * U, U)], 2, P),
                                      ALU.is_equal).then_inc(onehot_ready, 1)
                    if b >= 2:
                        score_block(i, b - 2)
                    elif not isinstance(i, int):
                        score_block(i - 1, b + 2)

            passes(dve, NB // B, one_pass)
            for b in (B - 2, B - 1):
                score_block(NB // B - 1, b)

        @block.tensor
        def _(pe):
            pe.sem_inc(attr_turned, B)
            pe.sem_inc(summed, 2)

            def sum_block(j, nodes, parity):
                pe.wait_ge(attr_copied, j + 1)
                wait_before(pe, xl_used, j + (B - 1))
                pe.wait_ge(turned_copied, j + 1)
                for u in range(U):
                    out = ps_s[parity][0:TE, u * P:(u + 1) * P]
                    pe.matmul(out, attr_t[parity][:, u, :], m.w_e[:], start=True, stop=False)
                    mm = pe.matmul(out, onehot_t[parity][:, u, :], m.src_sum[:, bass.ds(nodes[u], 1), 0:P],
                                   start=False, stop=True)
                mm.then_inc(summed, 1)

            def one_pass(i):
                nodes = block_numbers_before(nc, pe, m.node_i, i, g.NT - 1)
                for b in range(B):
                    pe.wait_ge(attr_in[b], i * (16 * U) + 16 * U)
                    for u in range(U):
                        mm = pe.transpose(ps_e[b % 2][:, u * TE:(u + 1) * TE], attr[b][:, u, :], m.ident[0:TE, 0:TE])
                    mm.then_inc(attr_turned, 1)
                    pe.wait_ge(onehot_ready, i * B + b + 1)
                    for u in range(U):
                        mm = pe.transpose(ps_t[b % 2][:, u * TE:(u + 1) * TE], onehot[b % 2][:, u, :],
                                          m.ident[0:TE, 0:TE])
                    mm.then_inc(turned, 1)
                    if nodes[b] is not None:
                        sum_block(i * B + (b - 1), nodes[b], (b - 1) % 2)

            passes(pe, NB // B, one_pass)
            sum_block(NB - 1, numbers(nc, pe, m.node_i, g.K - U, U, g.NT - 1), (NB - 1) % 2)


def maxima(nc, g, m):
    TE, KR, KC, H, K = g.TE, g.KR, g.KC, g.H, g.K
    with ExitStack() as ctx:
        def sb(name, shape, dt=F32):
            return ctx.enter_context(nc.sbuf_tensor(name, shape, dt))

        def sem(name):
            return ctx.enter_context(nc.semaphore(name))

        score = sb("score_rows", [KR, KC, H, TE])
        masked = sb("masked_rows", [KR, KC, H, TE])
        run = sb("run_rows", [KR, 2, KC * H * TE])
        ends = sb("max_ends", [KR, 2, KC, H])
        rows = sb("max_rows", [H, 2, K])
        way = sb("way", [H, 2, 2, K])
        carry = sb("carry", [H, 2, K])
        carry_k = sb("carry_k", [KR, 2, KC, H])
        extra = sb("extra", [KR, KC, H, TE])
        ps = [ctx.enter_context(nc.psum_tensor(f"ps_max{q}", [P, BANK], F32)) for q in range(8)]
        rows_ready, steps_sem, ends_turned, carry_turned, exp_done, back = (
            sem("rows_ready"), sem("max_steps"), sem("ends_turned"), sem("carry_turned"), sem("exp_done"), sem("back"))
        block = ctx.enter_context(nc.Block())
        step = Steps(steps_sem)
        at = {}
        flat = "k c h e -> k (c h e)"
        R = H * TE

        @block.vector
        def _(dve):
            def link(ins):
                dve.wait_ge(steps_sem, step.inc(ins))

            dve.wait_ge(rows_ready, 1)
            for q in range(KC):
                step.inc(dve.tensor_copy(score[:, q], ps[q][0:KR, 0:R].rearrange("k (h e) -> k h e", h=H)))
            dve.wait_ge(steps_sem, step.n)
            for q in range(KC):
                step.inc(dve.tensor_tensor(masked[:, q], score[:, q], repeat(m.others[:, q], 1, H), ALU.add))
            dve.wait_ge(steps_sem, step.n)
            link(dve.tensor_tensor_scan(run[:, 0, :], m.begins[:].rearrange(flat), masked[:].rearrange(flat),
                                        -BIG, ALU.add, ALU.max))
            link(dve.tensor_tensor_scan(run[:, 1, ::-1], m.ends[:].rearrange(flat)[:, ::-1],
                                        masked[:].rearrange(flat)[:, ::-1], -BIG, ALU.add, ALU.max))
            link(dve.tensor_tensor(run[:, 0, :], run[:, 0, :], run[:, 1, :], ALU.max))
            by_slot = run[:, 0, :].rearrange("k (c h e) -> k c h e", c=KC, h=H)
            step.inc(dve.tensor_copy(ends[:, 0], by_slot[:, :, :, 0]))
            at["ends"] = step.inc(dve.tensor_copy(ends[:, 1], by_slot[:, :, :, TE - 1]))
            dve.wait_ge(ends_turned, 1)
            step.inc(dve.tensor_copy(rows[:, 0, :], ps[4][0:H, 0:K]))
            link(dve.tensor_copy(rows[:, 1, :], ps[5][0:H, 0:K]))
            step.inc(dve.tensor_tensor(way[:, 0, 0, 1:K], m.joined[0:H, 1:K], m.whole[0:H, 0:K - 1], ALU.add))
            step.inc(dve.tensor_tensor(way[:, 0, 1, 1:K], m.joined[0:H, 1:K], rows[:, 1, 0:K - 1], ALU.add))
            step.inc(dve.tensor_tensor(way[:, 1, 0, 0:K - 1], m.joined[0:H, 1:K], m.whole[0:H, 1:K], ALU.add))
            step.inc(dve.tensor_tensor(way[:, 1, 1, 0:K - 1], m.joined[0:H, 1:K], rows[:, 0, 1:K], ALU.add))
            link(dve.memset(carry[:], -BIG))
            link(dve.tensor_tensor_scan(carry[:, 0, 1:K], way[:, 0, 0, 1:K], way[:, 0, 1, 1:K], -BIG, ALU.add, ALU.max))
            link(dve.tensor_tensor_scan(carry[:, 1, 0:K - 1][:, ::-1], way[:, 1, 0, 0:K - 1][:, ::-1],
                                        way[:, 1, 1, 0:K - 1][:, ::-1], -BIG, ALU.add, ALU.max))
            at["carry"] = step.n
            dve.wait_ge(carry_turned, 1)
            link(dve.tensor_copy(carry_k[:].rearrange("k f c h -> k (f c h)"), ps[6][0:KR, 0:2 * KC * H]))
            for f, away in ((0, m.not_first), (1, m.not_last)):
                for q in range(KC):
                    step.inc(dve.tensor_tensor(extra[:, q], repeat(carry_k[:, f, q, :], 2, TE),
                                               repeat(away[:, q], 1, H), ALU.add))
                dve.wait_ge(steps_sem, step.n)
                link(dve.tensor_tensor(run[:, 0, :], run[:, 0, :], extra[:].rearrange(flat), ALU.max))
            link(dve.tensor_tensor(run[:, 0, :], run[:, 0, :], score[:].rearrange(flat), ALU.max))
            link(dve.tensor_tensor(score[:].rearrange(flat), score[:].rearrange(flat), run[:, 0, :], ALU.subtract))
            at["shifted"] = step.n
            for which in range(2):
                for h in range(H):
                    dve.wait_ge(back, which * H + h + 1)
                    src = ps[which * H + h][0:TE, 0:K]
                    if which == 0:
                        step.inc(dve.tensor_copy(m.exp_max[:, :, h], src))
                    else:
                        step.inc(dve.tensor_tensor(m.exp_max[:, :, H + h], src, m.first[0:TE, :], ALU.mult))

        @block.scalar
        def _(act):
            act.wait_ge(steps_sem, at["shifted"])
            act.activation(score[:], score[:], ACT.Exp).then_inc(exp_done, 1)

        @block.tensor
        def _(pe):
            for q in range(KC):
                for h in range(H):
                    mm = pe.transpose(ps[q][0:KR, h * TE:(h + 1) * TE], m.score[:, h, q * KR:(q + 1) * KR],
                                      m.ident[0:TE, 0:TE])
            mm.then_inc(rows_ready, 1)
            pe.wait_ge(steps_sem, at["ends"])
            for f in range(2):
                for q in range(KC):
                    mm = pe.transpose(ps[4 + f][0:H, q * KR:(q + 1) * KR], ends[:, f, q, :], m.ident[0:KR, 0:KR])
            mm.then_inc(ends_turned, 1)
            pe.wait_ge(steps_sem, at["carry"])
            for f in range(2):
                for q in range(KC):
                    c0 = (f * KC + q) * H
                    mm = pe.transpose(ps[6][0:KR, c0:c0 + H], carry[:, f, q * KR:(q + 1) * KR], m.ident[0:H, 0:H])
            mm.then_inc(carry_turned, 1)
            by_slot = run[:, 0, :].rearrange("k (c h e) -> k c h e", c=KC, h=H)
            pe.wait_ge(exp_done, 1)
            for which, table in ((0, score[:]), (1, by_slot)):
                for h in range(H):
                    for q in range(KC):
                        mm = pe.transpose(ps[which * H + h][0:TE, q * KR:(q + 1) * KR], table[:, q, h, :],
                                          m.ident[0:KR, 0:KR])
                    mm.then_inc(back, 1)


def messages(nc, g, m):
    NB = g.K // U
    TE, H = g.TE, g.H
    W = P + 2 * H
    with ExitStack() as ctx:
        def sb(name, shape, dt=F32):
            return ctx.enter_context(nc.sbuf_tensor(name, shape, dt))

        def sem(name):
            return ctx.enter_context(nc.semaphore(name))

        xl = [sb(f"xl_m{b}", [TE, U, P]) for b in range(B)]
        message = [sb(f"message{b}", [TE, U, W]) for b in range(2)]
        onehot = [sb(f"onehot_m{b}", [TE, U, P]) for b in range(2)]
        ps = [ctx.enter_context(nc.psum_tensor(f"ps_m{b}", [P, U, BANK // 2], F32)) for b in range(2)]
        xl_in = [sem(f"xl_m_in{b}") for b in range(B)]
        message_ready, column_ready, summed, added = (
            sem("message_ready"), sem("column_ready"), sem("summed_m"), sem("added_m"))
        block = ctx.enter_context(nc.Block())

        @block.sync
        def _(sp):
            def one_pass(i):
                for b in range(B):
                    sp.wait_ge(message_ready, i * B + b + 1)
                    sp.dma_start(xl[b][:], m.xl_edges[:, bass.ds(i * (B * U) + b * U, U), :]).then_inc(xl_in[b], 16)

            passes(sp, NB // B, one_pass)

        @block.scalar
        def _(act):
            def one_pass(i):
                for b in range(B):
                    act.wait_ge(summed, i * B + b + 1)
                    act.copy(message[b % 2][:, :, P:W], m.exp_max[:, bass.ds(i * (B * U) + b * U, U), :]).then_inc(
                        column_ready, 1)

            passes(act, NB // B, one_pass)

        @block.vector
        def _(dve):
            dve.sem_inc(message_ready, B)
            dve.memset(m.message_sum[:], 0.0).then_inc(added, 1)
            def add_sums(j, base, parity):
                acc = m.message_sum[:, bass.ds(base, U), :]
                dve.wait_ge(summed, j + 3)
                dve.wait_ge(added, j + 1)
                dve.tensor_tensor(acc, acc, ps[parity][:, :, 0:W], ALU.add).then_inc(added, 1)

            def one_pass(i):
                bases = numbers_before(nc, dve, m.base_i, i, B, g.NT - 1)
                for b in range(B):
                    k0 = i * (B * U) + b * U
                    dve.wait_ge(summed, i * B + b + 1)
                    dve.tensor_tensor(onehot[b % 2][:], repeat(m.column[0:TE, :], 1, U),
                                      repeat(m.dst_lo[0:TE, bass.ds(k0, U)], 2, P), ALU.is_equal)
                    dve.wait_ge(xl_in[b], i * 16 + 16)
                    dve.tensor_tensor(message[b % 2][:, :, 0:P].rearrange("p u (h c) -> p u h c", h=H),
                                      xl[b][:].rearrange("p u (h c) -> p u h c", h=H),
                                      repeat(m.exp_max[:, bass.ds(k0, U), 0:H], 3, P // H),
                                      ALU.mult).then_inc(message_ready, 1)
                    if bases[b] is not None:
                        add_sums(i * B + (b - 1), bases[b], (b - 1) % 2)

            passes(dve, NB // B, one_pass)
            add_sums(NB - 1, numbers(nc, dve, m.base_i, NB - 1, 1, g.NT - 1)[0], (NB - 1) % 2)

        @block.tensor
        def _(pe):
            pe.sem_inc(summed, 2)
            def one_pass(i):
                window = numbers(nc, pe, m.window_i, i * (B * U), B * U, U - 1)
                for b in range(B):
                    pe.wait_ge(message_ready, i * B + b + 1 + B)
                    pe.wait_ge(column_ready, i * B + b + 1)
                    wait_before(pe, added, i * B + b)
                    clear_window(pe, m, ps[b % 2], W)
                    for u in range(U):
                        mm = pe.matmul(ps[b % 2][:, bass.ds(window[b * U + u], 1), 0:W], onehot[b % 2][:, u, :],
                                       message[b % 2][:, u, :], start=False, stop=(u == U - 1),
                                       skip_group_check=True)
                    mm.then_inc(summed, 1)

            passes(pe, NB // B, one_pass)

def finish(nc, g, m, out):
    NT, H, D = g.NT, g.H, P
    C = D // H
    with ExitStack() as ctx:
        def sb(name, shape, dt=F32):
            return ctx.enter_context(nc.sbuf_tensor(name, shape, dt))

        def sem(name):
            return ctx.enter_context(nc.semaphore(name))

        top = sb("top", [P, NT, H])
        part = sb("part", [P, 2, NT, H])
        total = sb("total", [P, NT, H])
        square = sb("square_f", [P, NT, D])
        stats = sb("stats_f", [P, 3, NT])
        ps_bias = ctx.enter_context(nc.psum_tensor("ps_bias", [P, BANK], F32))
        steps_sem, exp_done, bias_ready, sqrt_ready, sqrt_done, stored = (
            sem("finish_steps"), sem("part_exp"), sem("bias_ready"), sem("sqrt_f_ready"), sem("sqrt_f_done"), sem("out_stored"))
        block = ctx.enter_context(nc.Block())
        step = Steps(steps_sem)
        at = {}

        @block.vector
        def _(dve):
            def link(ins):
                dve.wait_ge(steps_sem, step.inc(ins))

            sums = m.message_sum[:, 0:NT]
            link(dve.tensor_scalar(total[:, :, 0], m.attr_sum[:, :, D], 0.0, -BIG, ALU.is_equal, ALU.mult))
            link(dve.tensor_tensor(part[:, 0], sums[:, :, D + H:D + 2 * H], repeat(total[:, :, 0], 2, H), ALU.add))
            link(dve.tensor_tensor(top[:], part[:, 0], m.loop_score[:], ALU.max))
            link(dve.tensor_tensor(part[:, 0], part[:, 0], top[:], ALU.subtract))
            link(dve.tensor_tensor(part[:, 1], m.loop_score[:], top[:], ALU.subtract))
            at["part"] = step.n
            dve.wait_ge(exp_done, 1)
            link(dve.tensor_tensor(total[:], sums[:, :, D:D + H], part[:, 0], ALU.mult))
            link(dve.tensor_tensor(total[:], total[:], part[:, 1], ALU.add))
            link(dve.reciprocal(total[:], total[:]))
            for w in range(2):
                link(dve.tensor_tensor(part[:, w], part[:, w], total[:], ALU.mult))
            for h in range(H):
                c = slice(h * C, (h + 1) * C)
                step.inc(dve.tensor_tensor(sums[:, :, c], sums[:, :, c], repeat(part[:, 0, :, h], 2, C), ALU.mult))
                step.inc(dve.tensor_tensor(m.x[:, :, c], m.x[:, :, c], repeat(part[:, 1, :, h], 2, C), ALU.mult))
            dve.wait_ge(steps_sem, step.n)
            link(dve.tensor_tensor(m.x1[:], m.x1[:], sums[:, :, 0:D], ALU.add))
            link(dve.tensor_tensor(m.x1[:], m.x1[:], m.x[:], ALU.add))
            dve.wait_ge(bias_ready, 1)
            link(dve.tensor_tensor(m.x1[:], m.x1[:], repeat(ps_bias[:, 0:D], 1, NT), ALU.add))
            layer_norm(g, dve, sqrt_done, 1, m.x1, square, stats, step, sqrt_ready)
            at["out"] = step.n

        @block.scalar
        def _(act):
            act.wait_ge(steps_sem, at["part"])
            act.activation(part[:], part[:], ACT.Exp).then_inc(exp_done, 1)
            act.wait_ge(sqrt_ready, 1)
            act.activation(stats[:, 2, :], stats[:, 1, :], ACT.Sqrt).then_inc(sqrt_done, 1)

        @block.tensor
        def _(pe):
            pe.matmul(ps_bias[:, 0:D], m.ones_row[:], m.rows[0:1, 4, :], start=True, stop=True).then_inc(bias_ready, 1)

        @block.sync
        def _(sp):
            MAIN = (NT - 1) * P
            sp.wait_ge(steps_sem, at["out"])
            sp.dma_start(out[0:MAIN].rearrange("(n p) d -> p n d", p=P), m.x1[:, 0:NT - 1, :]).then_inc(stored, 16)
            sp.dma_start(out[MAIN:g.N], m.x1[0:g.LAST, NT - 1, :]).then_inc(stored, 16)
            sp.wait_ge(stored, 32)


def program(nc, a, out, upto_phase=8, probe=None):
    g = Shapes(a["x"].shape[0], a["src"].shape[0], a["att"].shape[0])
    m = Tables()
    with ExitStack() as ctx:
        def sb(name, shape, dt=F32):
            return ctx.enter_context(nc.sbuf_tensor(name, shape, dt))

        D = a["x"].shape[1]
        m.x = sb("x_nodes", [P, g.NT, D])
        m.w0 = sb("w0", [P, 2, D])
        m.w_lr = sb("w_lr", [P, 2, D])
        m.w_e = sb("w_e", [P, D])
        m.rows = sb("rows", [1, 5, D])
        m.ones_row = sb("ones_row", [1, P])
        m.column = sb("column", [P, P])
        m.row_no = sb("row_no", [P, 1])
        m.ident = sb("ident", [P, P])
        m.node_i = sb("slot_node", [1, g.K], I32)
        m.tile_i = sb("slot_tile", [1, g.K], I32)
        m.base_i = sb("base_i", [1, g.K // U], I32)
        m.window_i = sb("window_i", [1, g.K], I32)
        m.base2_i = sb("base2_i", [1, g.K2 // U], I32)
        m.window2_i = sb("window2_i", [1, g.K2], I32)
        m.zeros = sb("zeros", [1, 512], BF16)
        m.node2_i = sb("node2_i", [1, g.K2], I32)
        m.dst_lo = sb("dst_lo", [P, g.K])
        m.first = sb("first", [P, g.K])
        m.src_idx = sb("src_idx", [g.TE, g.K], I32)
        m.src_lo = sb("src_lo", [g.TE, g.K])
        m.place_idx = sb("place_idx", [g.TE, g.K], I32)
        m.others = sb("others", [g.KR, g.KC, g.TE])
        m.not_first = sb("not_first", [g.KR, g.KC, g.TE])
        m.not_last = sb("not_last", [g.KR, g.KC, g.TE])
        m.begins = sb("begins", [g.KR, g.KC, g.H, g.TE])
        m.ends = sb("ends", [g.KR, g.KC, g.H, g.TE])
        m.end_rows = sb("end_rows", [4, 2, g.K])
        m.whole = sb("whole", [4, g.K])
        m.joined = sb("joined", [4, g.K])
        m.sorted_rows = nc.dram_tensor("sorted_rows", (P, g.K2, ROWW), F32, kind="Internal").ap()
        m.att = sb("att_all", [P, D])
        m.x1 = sb("x1", [P, g.NT, D])
        m.loop_score = sb("loop_score", [P, g.NT, g.H])
        m.src_sum = sb("src_sum", [P, g.NT + U - 1, D + 1])
        m.xl_rows = nc.dram_tensor("xl_rows", (P * g.NT, D), F32, kind="Internal").ap()
        m.xl_edges = nc.dram_tensor("xl_edges", (g.TE, g.K, D), F32, kind="Internal").ap()
        m.attr_sum = sb("attr_sum", [P, g.NT, D + 1])
        prepare(nc, g, m, a)
        if upto_phase >= 2:
            spread(nc, g, m, a)
        if upto_phase >= 3:
            gather_src(nc, g, m)
        if upto_phase >= 4:
            nodes(nc, g, m)
        if upto_phase >= 5:
            m.score = sb("score", [g.TE, g.H, g.K])
            scores(nc, g, m, a)
        if upto_phase >= 6:
            m.exp_max = sb("exp_max", [g.TE, g.K, 2 * g.H])
            maxima(nc, g, m)
        if upto_phase >= 7:
            m.message_sum = sb("message_sum", [P, g.NT + U - 1, D + 2 * g.H])
            messages(nc, g, m)
        if upto_phase >= 8:
            finish(nc, g, m, out)
        if probe:
            probe(nc, g, m)


_NAMES = {
    "x": "x", "src": "src", "dst": "dst", "edge_attr_128": "ea", "L0_gnn_W": "W0", "L0_gnn_b": "b0",
    "L1_gnn_W_l": "W_l", "L1_gnn_b_l": "b_l", "L1_gnn_W_r": "W_r", "L1_gnn_b_r": "b_r", "L1_gnn_W_e": "W_e",
    "L1_gnn_att": "att", "L1_gnn_bias": "bias",
}


def kernel(**inputs):
    import numpy as _np
    import concourse.bacc as _bacc
    from concourse import mybir as _mybir
    from concourse.bass_utils import run_bass_kernel_spmd as _run

    nc = _bacc.Bacc("TRN2", target_bir_lowering=False, num_devices=1)
    arrays, aps = {}, {}
    for name, short in _NAMES.items():
        array = _np.ascontiguousarray(inputs[name])
        arrays[f"in_{short}"] = array
        aps[short] = nc.dram_tensor(f"in_{short}", array.shape, _mybir.dt.from_np(array.dtype),
                                    kind="ExternalInput").ap()
    out = nc.dram_tensor("out_0", inputs["x"].shape, _mybir.dt.float32, kind="ExternalOutput").ap()
    program(nc, aps, out)
    result = _run(nc, [arrays], core_ids=[0])
    return result.results[0]["out_0"]
```

```python
from contextlib import ExitStack

import concourse.bass as bass
from concourse import mybir

F32 = mybir.dt.float32
BF16 = mybir.dt.bfloat16
I32 = mybir.dt.int32
I16 = mybir.dt.int16
ALU = mybir.AluOpType
ACT = mybir.ActivationFunctionType
AX = mybir.AxisListType

P = 128
BANK = 512
SUM_BANKS = 7
U = 4
B = 6
B2 = 8
COUNT_W = 64
BIG = 1.0e30
SLOPE = 0.2
LN_EPS = 1e-5
DEG_EPS = 1e-6
ROWW = 132


class Shapes:

    def __init__(self, n_nodes, n_edges, heads):
        self.N, self.E, self.H = n_nodes, n_edges, heads
        self.NT = -(-n_nodes // P)
        self.LAST = n_nodes - (self.NT - 1) * P
        self.TE = 125
        self.T = n_edges // self.TE
        self.CR, self.CC = 85, 5
        self.K = 456
        self.KR, self.KC = 114, 4
        self.K2 = 448
        assert self.NT * P <= SUM_BANKS * BANK and self.NT * 2 * heads <= BANK
        assert self.T * self.TE == n_edges and self.CR * self.CC == self.T
        assert self.K >= self.T + self.NT - 1 and self.K % (B * U) == 0
        assert self.KR * self.KC == self.K and self.KR <= P
        assert self.K2 >= n_edges // P + self.NT and self.K2 % (B2 * U) == 0


def repeat(ap, dim, n):
    shape = list(ap.shape)
    shape.insert(dim, n)
    return ap.unsqueeze(dim).broadcast_to(shape)


class Steps:

    def __init__(self, sem):
        self.sem, self.n = sem, 0

    def inc(self, instruction):
        instruction.then_inc(self.sem, 1)
        self.n += 1
        return self.n


def numbers(nc, engine, table, first, count, top):
    _, values = nc.values_load_multi_w_load_instructions(
        table[0:1, bass.ds(first, count)], engines=[engine.engine], min_val=0, max_val=top,
        skip_runtime_bounds_check_because="prepare() bounds the tables' numbers")
    return values


def passes(engine, count, body):
    body(0)
    with engine.Fori(1, count) as i:
        body(i)


def wait_before(engine, sem, value):
    if not (isinstance(value, int) and value <= 0):
        engine.wait_ge(sem, value)


def numbers_before(nc, engine, table, i, count, top, lag):
    if isinstance(i, int):
        return [None] * lag + list(numbers(nc, engine, table, 0, count - lag, top))
    return numbers(nc, engine, table, i * count - lag, count, top)


def block_numbers_before(nc, engine, table, i, top):
    if isinstance(i, int):
        values = numbers(nc, engine, table, 0, (B - 1) * U, top)
        return [None] + [values[b * U:(b + 1) * U] for b in range(B - 1)]
    values = numbers(nc, engine, table, i * (B * U) - U, B * U, top)
    return [values[b * U:(b + 1) * U] for b in range(B)]


def clear_window(pe, m, ps, width):
    for half in range(U // 2):
        pe.matmul(ps[:, 2 * half:2 * half + 2, 0:width], m.zeros[:, 0:P],
                  m.zeros[:, 0:2 * width].rearrange("o (a w) -> o a w", a=2), start=True, stop=False,
                  skip_group_check=True)


class Tables:
    pass


def prepare(nc, g, m, a):
    with ExitStack() as ctx:
        def sb(name, shape, dt=F32):
            return ctx.enter_context(nc.sbuf_tensor(name, shape, dt))

        def sem(name):
            return ctx.enter_context(nc.semaphore(name))

        CR, CC, TE, K, NT, T, KR, KC = g.CR, g.CC, g.TE, g.K, g.NT, g.T, g.KR, g.KC
        src_i = sb("src_i", [CR, CC, TE], I32)
        dst_i = sb("dst_i", [CR, CC, TE], I32)
        prev_i = sb("prev_i", [CR, CC], I32)
        tile_i = sb("tile_i", [CR, CC, 2], I32)
        src_f = sb("src_f", [CR, CC, TE])
        dst_f = sb("dst_f", [CR, CC, TE])
        prev_f = sb("prev_f", [CR, CC])
        first_f = sb("first_f", [CR, CC, TE])
        ends4 = sb("ends4", [CR, 2, CC, 4])
        tile_f = sb("tile_f", [CR, CC, 2])
        tile_no = sb("tile_no", [CR, CC])
        iota_k = sb("iota_k", [CR, K])
        upto = sb("upto", [CR, CC, K], BF16)
        pick = sb("pick", [CR, CC, K])
        bucket_i = sb("bucket_i", [CR, CC * TE], I32)
        bucket_f = sb("bucket_f", [CR, CC * TE], BF16)
        in_b = sb("in_b", [CR, NT, CC * TE], mybir.dt.uint8)
        count_b = sb("count_b", [CR, NT])
        run_b = sb("run_b", [CR, NT, CC * TE], I16)
        part = m.src_sum[0:CR].rearrange("r n d -> r (n d)")[:, 0:4 * CC * TE].rearrange("r (b e) -> r b e", b=4)
        place = m.attr_sum[0:CR].rearrange("r n d -> r (n d)")[:, 0:2 * CC * TE].rearrange("r (b e) -> r b e", b=2)
        before = sb("before", [CR, CR])
        ones = sb("ones", [CR, P])
        ones_half = sb("ones_half", [CR, P], BF16)
        one_row = sb("one_row", [P, NT])
        tiles_r = sb("tiles_r", [P, NT])
        tiles_ri = sb("tiles_ri", [P, NT], I32)
        tiles_end = sb("tiles_end", [P, NT])
        start_b = sb("start_b", [CR, NT])
        tiles_c = sb("tiles_c", [NT, 1])
        tiles_ci = sb("tiles_ci", [NT, 1], I32)
        end_c = sb("end_c", [NT, 1])
        uptoc = sb("uptoc", [NT, NT])
        iota_k2 = sb("iota_k2", [NT, g.K2])
        ended = sb("ended", [NT, g.K2])
        slot_k = sb("slot_k", [P, K])
        node_of = sb("node_of", [P, K])
        t_of = sb("t_of", [1, K])
        numbers_f = sb("numbers_f", [1, K])
        work_i = sb("work_i", [P, 2, K], I32)
        spare = m.src_sum[:].rearrange("r n d -> r (n d)")[:, 4 * CC * TE:4 * CC * TE + 2 * K]
        work, work2 = spare[:, 0:K], spare[:, K:2 * K]
        slot_rows = sb("slot_rows", [KR, KC])
        zero = m.x1[:].rearrange("p n d -> p (n d)")[:, 0:g.K2 // 28 * ROWW]

        loaded = sem("loaded")
        weights_in = sem("weights_in")
        cleared = sem("cleared")
        ps = [ctx.enter_context(nc.psum_tensor(f"ps_prep{i}", [P, BANK], F32)) for i in range(8)]
        pool_sem, dve_sem, pe_sem, act_sem = sem("pool_step"), sem("dve_step"), sem("pe_step"), sem("act_step")
        part_added = sem("part_added")
        block = ctx.enter_context(nc.Block())
        NCLEAR = 28
        MAIN = (NT - 1) * P

        @block.sync
        def _(sp):
            sp.dma_start(src_i[:], a["src"].rearrange("(c r e) -> r c e", c=CC, r=CR)).then_inc(loaded, 16)
            sp.dma_start(dst_i[:], a["dst"].rearrange("(c r e) -> r c e", c=CC, r=CR)).then_inc(loaded, 16)
            ends = a["dst"].rearrange("(t e) -> t e", e=TE)[:, TE - 1:TE]
            sp.wait_ge(pool_sem, 1)
            sp.dma_start(prev_i[1:CR, 0:1], ends[0:CR - 1], allow_slow_non_contiguous=True).then_inc(loaded, 16)
            for c in range(1, CC):
                sp.dma_start(prev_i[:, c:c + 1], ends[c * CR - 1:(c + 1) * CR - 1],
                             allow_slow_non_contiguous=True).then_inc(loaded, 16)
            sp.wait_ge(pool_sem, 2)
            for dst, src in (
                (m.x[:, 0:NT - 1, :], a["x"][0:MAIN].rearrange("(n p) d -> p n d", p=P)),
                (m.x[0:g.LAST, NT - 1, :], a["x"][MAIN:g.N]),
                (m.w0[:], a["W0"].rearrange("(c p) d -> p c d", p=P)),
                (m.w_lr[:, 0, :], a["W_l"]), (m.w_lr[:, 1, :], a["W_r"]), (m.w_e[:], a["W_e"]),
                (m.rows[0:1, 0, :], a["b0"].unsqueeze(0)), (m.rows[0:1, 1, :], a["b_l"].unsqueeze(0)),
                (m.rows[0:1, 2, :], a["b_r"].unsqueeze(0)),
                (m.rows[0:1, 3, :], a["att"].rearrange("h c -> (h c)").unsqueeze(0)),
                (m.rows[0:1, 4, :], a["bias"].unsqueeze(0)),
            ):
                sp.dma_start(dst, src).then_inc(weights_in, 16)
            sp.wait_ge(pool_sem, 3)
            w = g.K2 // NCLEAR
            for i in range(NCLEAR):
                sp.dma_start(m.sorted_rows[:, i * w:(i + 1) * w, :].rearrange("p k w -> p (k w)"),
                             zero).then_inc(cleared, 16)
            sp.wait_ge(cleared, 16 * NCLEAR)
            sp.wait_ge(weights_in, 16 * 11)

        @block.gpsimd
        def _(pool):
            pool.memset(prev_i[:], -1).then_inc(pool_sem, 1)
            pool.memset(m.x[:, NT - 1, :], 0.0).then_inc(pool_sem, 1)
            pool.memset(zero, 0.0).then_inc(pool_sem, 1)
            iota = dict(allow_small_or_imprecise_dtypes=True)
            pool.iota(m.column[:], [[1, P]], 0, 0, **iota).then_inc(pool_sem, 1)
            pool.iota(m.row_no[:], [[0, 1]], 0, 1, **iota).then_inc(pool_sem, 1)
            pool.iota(iota_k[:], [[1, K]], 0, 0, **iota).then_inc(pool_sem, 1)
            pool.iota(tile_no[:], [[CR, CC]], 0, 1, **iota).then_inc(pool_sem, 1)
            pool.iota(slot_k[:], [[1, K]], 0, 0, **iota).then_inc(pool_sem, 1)
            pool.iota(iota_k2[:], [[1, g.K2]], 0, 0, **iota).then_inc(pool_sem, 1)
            pool.iota(slot_rows[:], [[KR, KC]], 0, 1, **iota).then_inc(pool_sem, 1)
            pool.memset(ones[:], 1.0).then_inc(pool_sem, 1)
            pool.memset(ones_half[:], 1.0).then_inc(pool_sem, 1)
            pool.memset(one_row[:], 1.0).then_inc(pool_sem, 1)
            pool.memset(m.ones_row[:], 1.0).then_inc(pool_sem, 1)
            pool.memset(m.zeros[:], 0.0).then_inc(pool_sem, 1)

        PE_NODE, PE_TABLE, PE_ROWS, PE_COUNT, PE_TOTALS, PE_ENDC, PE_NK2, PE_ENDS, PE_PLACE = range(1, 10)
        step = Steps(dve_sem)
        at = {}

        @block.vector
        def _(dve):
            def link(ins):
                dve.wait_ge(dve_sem, step.inc(ins))

            dve.wait_ge(pool_sem, 15)
            dve.wait_ge(loaded, 16 * (2 + CC))
            step.inc(dve.tensor_scalar(before[:], m.column[0:CR, 0:CR], m.row_no[0:CR, 0:1], None, ALU.is_gt))
            step.inc(dve.tensor_scalar(uptoc[:], m.column[0:NT, 0:NT], m.row_no[0:NT, 0:1], None, ALU.is_ge))
            step.inc(dve.tensor_scalar(m.ident[:], m.column[:], m.row_no[:, 0:1], None, ALU.is_equal))
            step.inc(dve.tensor_copy(src_f[:], src_i[:]))
            step.inc(dve.tensor_copy(dst_f[:], dst_i[:]))
            step.inc(dve.tensor_copy(prev_f[:], prev_i[:]))
            step.inc(dve.tensor_scalar(tile_i[:, :, 0], dst_i[:, :, TE - 1], 7, None, ALU.arith_shift_right))
            link(dve.tensor_scalar(tile_i[:, :, 1], prev_i[:], 7, None, ALU.arith_shift_right))
            link(dve.tensor_copy(tile_f[:], tile_i[:]))
            step.inc(dve.tensor_tensor(tile_f[:, :, 0], tile_f[:, :, 0], tile_no[:], ALU.add))
            link(dve.scalar_tensor_tensor(tile_f[:, :, 1], tile_f[:, :, 1], -1.0, tile_no[:], ALU.add, ALU.add))
            link(dve.tensor_scalar(work2[0:CR, 0:CC], tile_no[:], float(T - 1), float(K), ALU.is_equal, ALU.mult))
            link(dve.tensor_tensor(tile_f[:, :, 0], tile_f[:, :, 0], work2[0:CR, 0:CC], ALU.max))
            for c in range(CC):
                step.inc(dve.tensor_scalar(upto[:, c, :], iota_k[:], tile_f[:, c, 0:1], None, ALU.is_le))
                step.inc(dve.tensor_scalar(pick[:, c, :], iota_k[:], tile_f[:, c, 1:2], None, ALU.is_gt))
            dve.wait_ge(dve_sem, step.n)
            link(dve.tensor_tensor(pick[:], pick[:], upto[:], ALU.mult))
            step.inc(dve.tensor_tensor(first_f[:, :, 1:TE], dst_f[:, :, 1:TE], dst_f[:, :, 0:TE - 1], ALU.not_equal))
            step.inc(dve.tensor_tensor(first_f[:, :, 0], dst_f[:, :, 0], prev_f[:], ALU.not_equal))
            step.inc(dve.tensor_copy(ends4[:, 0], repeat(dst_f[:, :, 0], 2, 4)))
            at["pick"] = step.inc(dve.tensor_copy(ends4[:, 1], repeat(dst_f[:, :, TE - 1], 2, 4)))
            dve.wait_ge(dve_sem, step.n)
            link(dve.tensor_scalar(bucket_i[:], src_i[:].rearrange("r c e -> r (c e)"), 7, None,
                                   ALU.arith_shift_right))
            link(dve.tensor_copy(bucket_f[:], bucket_i[:]))
            for b in range(NT):
                step.inc(dve.tensor_scalar(in_b[:, b, :], bucket_f[:], float(b), None, ALU.is_equal))
            dve.wait_ge(dve_sem, step.n)
            for b in range(NT):
                step.inc(dve.tensor_tensor_scan(run_b[:, b, :], repeat(ones[:, 0], 1, CC * TE), in_b[:, b, :], 0.0,
                                                ALU.mult, ALU.add))
            dve.wait_ge(dve_sem, step.n)
            at["count"] = step.inc(dve.tensor_copy(count_b[:], run_b[:, :, CC * TE - 1]))
            dve.wait_ge(pe_sem, PE_NODE)
            link(dve.scalar_tensor_tensor(node_of[:], slot_k[:], float(-T), ps[3][:, 0:K], ALU.add, ALU.add))
            step.inc(dve.tensor_scalar(m.node_i[:], node_of[0:1, :], float(NT - 1), None, ALU.min))
            link(dve.tensor_tensor(t_of[:], slot_k[0:1, :], node_of[0:1, :], ALU.subtract))
            blocks = numbers_f[:].rearrange("o (j u) -> o j u", u=U)
            link(dve.tensor_copy(numbers_f[:], m.node_i[:]))
            link(dve.tensor_copy(m.base_i[:], blocks[:, :, 0]))
            link(dve.tensor_tensor(m.window_i[:].rearrange("o (j u) -> o j u", u=U), blocks,
                                   repeat(blocks[:, :, 0], 2, U), ALU.subtract))
            link(dve.tensor_copy(m.tile_i[:], t_of[:]))
            dve.wait_ge(pe_sem, PE_COUNT)
            step.inc(dve.tensor_scalar(tiles_ri[:], ps[0][:, 0:NT], float(P - 1), float(P), ALU.add, ALU.max))
            link(dve.tensor_scalar(tiles_ci[:], ps[1][0:NT, 0:1], float(P - 1), float(P), ALU.add, ALU.max))
            step.inc(dve.tensor_scalar(tiles_ri[:], tiles_ri[:], 7, None, ALU.arith_shift_right))
            link(dve.tensor_scalar(tiles_ci[:], tiles_ci[:], 7, None, ALU.arith_shift_right))
            step.inc(dve.tensor_copy(tiles_r[:], tiles_ri[:]))
            at["tiles_c"] = step.inc(dve.tensor_copy(tiles_c[:], tiles_ci[:]))
            dve.wait_ge(dve_sem, step.n)
            link(dve.tensor_tensor_scan(tiles_end[:], one_row[:], tiles_r[:], 0.0, ALU.mult, ALU.add))
            link(dve.tensor_tensor(tiles_end[:], tiles_end[:], tiles_r[:], ALU.subtract))
            link(dve.tensor_scalar(start_b[:], tiles_end[0:CR, :], float(P), -1.0, ALU.mult, ALU.add))
            dve.wait_ge(pe_sem, PE_TOTALS)
            link(dve.tensor_tensor(start_b[:], start_b[:], ps[2][0:CR, 0:NT], ALU.add))
            dve.wait_ge(pe_sem, PE_ENDC)
            link(dve.tensor_copy(end_c[:], ps[1][0:NT, 1:2]))
            at["ended"] = step.inc(dve.tensor_scalar(ended[:], iota_k2[:], end_c[:, 0:1], None, ALU.is_ge))
            dve.wait_ge(pe_sem, PE_NK2)
            link(dve.tensor_scalar(m.node2_i[:], ps[0][0:1, 0:g.K2], float(NT - 1), None, ALU.min))
            at["done_banks"] = step.n
            at["cleared"] = step.inc(dve.memset(place, 0.0))
            dve.wait_ge(dve_sem, step.n)
            for b in range(NT):
                if b >= 4 and b % 2 == 1:
                    dve.wait_ge(part_added, b // 2 - 1)
                at["part", b] = step.inc(dve.scalar_tensor_tensor(
                    part[:, b % 4, :], run_b[:, b, :], start_b[:, b:b + 1], in_b[:, b, :], ALU.add, ALU.mult))
                if b % 2 == 0:
                    dve.wait_ge(dve_sem, step.n)
                    step.inc(dve.tensor_tensor(place[:, 0, :], place[:, 0, :], part[:, b % 4, :], ALU.add))
            dve.wait_ge(dve_sem, step.n)
            dve.wait_ge(part_added, NT // 2)
            at["place"] = step.inc(dve.tensor_tensor(place[:, 0, :], place[:, 0, :], place[:, 1, :], ALU.add))
            dve.wait_ge(pe_sem, PE_TABLE)
            link(dve.scalar_tensor_tensor(m.dst_lo[0:TE, :], node_of[0:TE, :], float(-P), ps[5][0:TE, 0:K],
                                          ALU.mult, ALU.add))
            link(dve.tensor_copy(m.src_idx[:], ps[4][0:TE, 0:K]))
            link(dve.tensor_scalar(work_i[0:TE, 0, :], m.src_idx[:], P - 1, None, ALU.bitwise_and))
            link(dve.tensor_copy(m.src_lo[:], work_i[0:TE, 0, :]))
            dve.wait_ge(pe_sem, PE_ROWS)
            link(dve.scalar_tensor_tensor(m.slot_node[:], ps[2][0:KR, 32:32 + KC], float(-T), slot_rows[:],
                                          ALU.add, ALU.add))
            link(dve.tensor_scalar(work[0:TE, :], m.dst_lo[0:TE, :], 0.0, float(P * g.K2), ALU.is_lt, ALU.mult))
            link(dve.tensor_scalar(work2[0:TE, :], m.dst_lo[0:TE, :], float(P), float(P * g.K2), ALU.is_ge, ALU.mult))
            link(dve.tensor_tensor(work[0:TE, :], work[0:TE, :], work2[0:TE, :], ALU.add))
            dve.wait_ge(pe_sem, PE_PLACE)
            link(dve.tensor_copy(work_i[0:TE, 0, :], ps[3][0:TE, 0:K]))
            link(dve.tensor_scalar(work_i[0:TE, 1, :], work_i[0:TE, 0, :], P - 1, None, ALU.bitwise_and))
            link(dve.tensor_scalar(work_i[0:TE, 0, :], work_i[0:TE, 0, :], 7, None, ALU.arith_shift_right))
            link(dve.tensor_copy(work2[0:TE, :], work_i[0:TE, 0, :]))
            link(dve.scalar_tensor_tensor(work2[0:TE, :], work_i[0:TE, 1, :], float(g.K2), work2[0:TE, :],
                                          ALU.mult, ALU.add))
            link(dve.tensor_tensor(work2[0:TE, :], work2[0:TE, :], work[0:TE, :], ALU.add))
            link(dve.tensor_copy(m.place_idx[:], work2[0:TE, :]))

        @block.scalar
        def _(act):
            act.wait_ge(pe_sem, PE_TABLE)
            act.copy(m.first[0:TE, :], ps[6][0:TE, 0:K]).then_inc(act_sem, 1)
            act.wait_ge(pe_sem, PE_ROWS)
            act.copy(m.slot_dst[:], ps[7][0:KR, 0:KC * TE].rearrange("k (c e) -> k c e", c=KC)).then_inc(act_sem, 1)
            act.wait_ge(pe_sem, PE_ENDS)
            act.copy(m.end_rows[:, 0, :], ps[0][0:4, 0:K]).then_inc(act_sem, 1)
            act.copy(m.end_rows[:, 1, :], ps[1][0:4, 0:K]).then_inc(act_sem, 1)

        @block.gpsimd
        def _(pool):
            pool.wait_ge(dve_sem, at["cleared"])
            for b in range(1, NT, 2):
                pool.wait_ge(dve_sem, at["part", b])
                if b > 1:
                    pool.wait_ge(part_added, b // 2)
                pool.tensor_tensor(place[:, 1, :], place[:, 1, :], part[:, b % 4, :], ALU.add).then_inc(part_added, 1)

        @block.tensor
        def _(pe):
            pe.wait_ge(dve_sem, at["pick"])
            for c in range(CC):
                mm = pe.matmul(ps[3][:, 0:K], ones_half[:], upto[:, c, :], start=(c == 0), stop=(c == CC - 1))
            mm.then_inc(pe_sem, 1)
            for bank, table in ((4, src_f), (5, dst_f), (6, first_f)):
                for c in range(CC):
                    mm = pe.matmul(ps[bank][0:TE, 0:K], table[:, c, :], pick[:, c, :],
                                   start=(c == 0), stop=(c == CC - 1))
            mm.then_inc(pe_sem, 1)
            for q in range(KC):
                for c in range(CC):
                    pe.matmul(ps[7][0:KR, q * TE:(q + 1) * TE], pick[:, c, q * KR:(q + 1) * KR], dst_f[:, c, :],
                              start=(c == 0), stop=(c == CC - 1))
                for c in range(CC):
                    mm = pe.matmul(ps[2][0:KR, 32 + q:33 + q], upto[:, c, q * KR:(q + 1) * KR], ones_half[:, 0:1],
                                   start=(c == 0), stop=(c == CC - 1))
            mm.then_inc(pe_sem, 1)
            pe.wait_ge(dve_sem, at["count"])
            pe.matmul(ps[0][:, 0:NT], ones[:], count_b[:], start=True, stop=True)
            pe.matmul(ps[1][0:NT, 0:1], count_b[:], ones[:, 0:1], start=True, stop=True).then_inc(pe_sem, 1)
            pe.matmul(ps[2][0:CR, 0:NT], before[:], count_b[:], start=True, stop=True).then_inc(pe_sem, 1)
            pe.wait_ge(dve_sem, at["tiles_c"])
            pe.matmul(ps[1][0:NT, 1:2], uptoc[:], tiles_c[:], start=True, stop=True).then_inc(pe_sem, 1)
            pe.wait_ge(dve_sem, at["ended"])
            pe.matmul(ps[0][0:1, 0:g.K2], ones[0:NT, 0:1], ended[:], start=True, stop=True).then_inc(pe_sem, 1)
            pe.wait_ge(dve_sem, at["done_banks"])
            for which in range(2):
                for c in range(CC):
                    mm = pe.matmul(ps[which][0:4, 0:K], ends4[:, which, c, :], pick[:, c, :],
                                   start=(c == 0), stop=(c == CC - 1))
            mm.then_inc(pe_sem, 1)
            pe.wait_ge(dve_sem, at["place"])
            for c in range(CC):
                mm = pe.matmul(ps[3][0:TE, 0:K], place[:, 0, c * TE:(c + 1) * TE], pick[:, c, :],
                               start=(c == 0), stop=(c == CC - 1))
            mm.then_inc(pe_sem, 1)


def slot_flags(dve, g, m, step, dst_tile):
    def link(ins):
        dve.wait_ge(step.sem, step.inc(ins))

    link(dve.tensor_copy(dst_tile[:], m.slot_dst[:]))
    link(dve.tensor_scalar(dst_tile[:], dst_tile[:], 7, None, ALU.arith_shift_right))
    for c in range(g.KC):
        link(dve.tensor_scalar(m.others[:, c, :], dst_tile[:, c, :], m.slot_node[:, c:c + 1], -BIG,
                               ALU.not_equal, ALU.mult))
        for h in range(g.H):
            step.inc(dve.memset(m.begins[:, c, h, 0:1], -BIG))
            step.inc(dve.memset(m.ends[:, c, h, g.TE - 1:g.TE], -BIG))
            step.inc(dve.tensor_tensor(m.begins[:, c, h, 1:g.TE], m.slot_dst[:, c, 1:g.TE],
                                       m.slot_dst[:, c, 0:g.TE - 1], ALU.not_equal))
            step.inc(dve.tensor_tensor(m.ends[:, c, h, 0:g.TE - 1], m.slot_dst[:, c, 1:g.TE],
                                       m.slot_dst[:, c, 0:g.TE - 1], ALU.not_equal))
        dve.wait_ge(step.sem, step.n)
        step.inc(dve.tensor_scalar(m.begins[:, c, :, 1:g.TE], m.begins[:, c, :, 1:g.TE], -BIG, None, ALU.mult))
        step.inc(dve.tensor_scalar(m.ends[:, c, :, 0:g.TE - 1], m.ends[:, c, :, 0:g.TE - 1], -BIG, None, ALU.mult))
        step.inc(dve.tensor_scalar(m.not_first[:, c, :], m.slot_dst[:, c, :], m.slot_dst[:, c, 0:1], -BIG,
                                   ALU.not_equal, ALU.mult))
        link(dve.tensor_scalar(m.not_last[:, c, :], m.slot_dst[:, c, :], m.slot_dst[:, c, g.TE - 1:g.TE], -BIG,
                               ALU.not_equal, ALU.mult))
    step.inc(dve.tensor_tensor(m.whole[:], m.end_rows[:, 0, :], m.end_rows[:, 1, :], ALU.not_equal))
    link(dve.tensor_tensor(m.joined[:, 1:g.K], m.end_rows[:, 0, 1:g.K], m.end_rows[:, 1, 0:g.K - 1], ALU.not_equal))
    step.inc(dve.tensor_scalar(m.whole[:], m.whole[:], -BIG, None, ALU.mult))
    link(dve.tensor_scalar(m.joined[:, 1:g.K], m.joined[:, 1:g.K], -BIG, None, ALU.mult))


def spread(nc, g, m, a):
    NB = g.K // U
    TE = g.TE
    with ExitStack() as ctx:
        def sb(name, shape, dt=F32):
            return ctx.enter_context(nc.sbuf_tensor(name, shape, dt))

        def sem(name):
            return ctx.enter_context(nc.semaphore(name))

        attr = [sb(f"attr{b}", [TE, U, P + 1]) for b in range(B)]
        onehot = [sb(f"onehot{b}", [TE, U, P]) for b in range(2)]
        onehot_t = [sb(f"onehot_t{b}", [P, U, TE]) for b in range(2)]
        row = [sb(f"row{b}", [TE, U, ROWW]) for b in range(B)]
        index = [sb(f"index{b}", [TE, B // 2 * U], I32) for b in range(2)]
        dst_tile = sb("dst_tile", [g.KR, g.KC, g.TE], I32)
        ps_t = [ctx.enter_context(nc.psum_tensor(f"ps_t{b}", [P, BANK], F32)) for b in range(2)]
        ps_x = [ctx.enter_context(nc.psum_tensor(f"ps_x{b}", [P, BANK], F32)) for b in range(2)]
        ps_a = [ctx.enter_context(nc.psum_tensor(f"ps_a{b}", [P, 2, BANK], F32)) for b in range(2)]
        attr_in = [sem(f"attr_in{b}") for b in range(B)]
        row_out = [sem(f"row_out{b}") for b in range(B)]
        block_summed, onehot_ready = sem("block_summed"), sem("onehot_ready")
        turned, turned_copied, spread_done, row_copied = (
            sem("turned"), sem("turned_copied"), sem("spread_done"), sem("row_copied"))
        meta_ready, sums_free, added = sem("meta_ready"), sem("sums_free"), sem("added")
        preset = sem("preset")
        step = Steps(sem("flag_steps"))
        index_ready, begun = sem("index_ready"), sem("begun")
        block = ctx.enter_context(nc.Block())

        @block.sync
        def _(sp):
            def one_pass(i):
                tiles = numbers(nc, sp, m.tile_i, i * (B * U), B * U, g.T - 1)
                for b in range(B):
                    wait_before(sp, block_summed, i * B + (b + 3 - B))
                    for u in range(U):
                        sp.dma_start(attr[b][:, u, 0:P], a["ea"][bass.ds(tiles[b * U + u] * TE, TE), :]).then_inc(
                            attr_in[b], 16)

            passes(sp, NB // B, one_pass)

        @block.gpsimd
        def _(pool):
            limit = pool.to_reg(P * g.K2 - 1)

            def one_pass(i):
                for b in range(B):
                    half, first = divmod(b, B // 2)
                    if first == 0:
                        for k in range(b, b + B // 2):
                            wait_before(pool, row_out[k], i * (16 * U))
                        pool.tensor_copy(index[half][:], m.place_idx[:, bass.ds(
                            i * (B * U) + b * U, B // 2 * U)]).then_inc(index_ready, 1)
                        pool.wait_ge(index_ready, i * 2 + half + 1)
                    pool.wait_ge(row_copied, i * B + b + 3)
                    pool.wait_ge(meta_ready, i * B + b + 2)
                    pool.sem_inc(begun, 1)
                    for u in range(U):
                        pool.indirect_dma_start(
                            out=m.sorted_rows.rearrange("p k w -> (p k) w"),
                            out_offset=bass.IndirectOffsetOnAxis(
                                ap=index[half][:, first * U + u:first * U + u + 1], axis=0),
                            in_=row[b][:, u, :], in_offset=None,
                            bounds_check=limit, oob_is_err=False).then_inc(row_out[b], 16)

            passes(pool, NB // B, one_pass)
            for b in range(B):
                pool.wait_ge(row_out[b], 16 * U * (NB // B))

        @block.scalar
        def _(act):
            act.sem_inc(row_copied, 2)

            def one_pass(i):
                for b in range(B):
                    act.wait_ge(turned, i * B + b + 1)
                    act.copy(onehot_t[b % 2][:], ps_t[b % 2][:, 0:U * TE].rearrange("p (u e) -> p u e", u=U)).then_inc(
                        turned_copied, 1)
                    act.wait_ge(spread_done, i * B + b + 1)
                    wait_before(act, row_out[b], i * (16 * U))
                    act.copy(row[b][:, :, 0:P], ps_x[b % 2][0:TE, :].rearrange("p (u d) -> p u d", u=U)).then_inc(
                        row_copied, 1)

            passes(act, NB // B, one_pass)

        @block.vector
        def _(dve):
            for b in range(B):
                dve.memset(attr[b][:, :, P:P + 1], 1.0).then_inc(preset, 1)
                dve.memset(row[b][:, :, P:ROWW], 1.0).then_inc(preset, 1)
            dve.memset(m.attr_sum[:], 0.0).then_inc(added, 1)
            dve.wait_ge(preset, 2 * B)
            dve.sem_inc(meta_ready, 1)
            dve.sem_inc(sums_free, 2)

            def add_sums(j, nodes, parity):
                dve.wait_ge(block_summed, j + 3)
                for u in range(U):
                    acc = m.attr_sum[:, bass.ds(nodes[u], 1), :]
                    dve.wait_ge(added, j * U + (u + 1))
                    c0 = u % 2 * (BANK // 2)
                    dve.tensor_tensor(acc, acc, ps_a[parity][:, u // 2, c0:c0 + P + 1].unsqueeze(1),
                                      ALU.add).then_inc(added, 1)
                dve.wait_ge(added, j * U + (U + 1))
                dve.sem_inc(sums_free, 1)

            def one_pass(i):
                nodes = block_numbers_before(nc, dve, m.node_i, i, g.NT - 1)
                for b in range(B):
                    k0 = i * (B * U) + b * U
                    dve.wait_ge(block_summed, i * B + b + 1)
                    dve.tensor_tensor(onehot[b % 2][:], repeat(m.column[0:TE, :], 1, U),
                                      repeat(m.dst_lo[0:TE, bass.ds(k0, U)], 2, P),
                                      ALU.is_equal).then_inc(onehot_ready, 1)
                    wait_before(dve, row_out[b], i * (16 * U))
                    dve.tensor_copy(row[b][:, :, P + 1], m.src_lo[:, bass.ds(k0, U)]).then_inc(meta_ready, 1)
                    if nodes[b] is not None:
                        add_sums(i * B + (b - 1), nodes[b], (b - 1) % 2)

            one_pass(0)
            with dve.Fori(1, NB // B // 2) as i:
                one_pass(i)
            slot_flags(dve, g, m, step, dst_tile)
            with dve.Fori(NB // B // 2, NB // B) as i:
                one_pass(i)
            add_sums(NB - 1, numbers(nc, dve, m.node_i, g.K - U, U, g.NT - 1), (NB - 1) % 2)

        @block.tensor
        def _(pe):
            pe.sem_inc(block_summed, 2)
            pe.wait_ge(preset, 2 * B)

            def one_pass(i):
                nodes = numbers(nc, pe, m.node_i, i * (B * U), B * U, g.NT - 1)
                for b in range(B):
                    k0 = i * (B * U) + b * U
                    pe.wait_ge(onehot_ready, i * B + b + 1)
                    for u in range(U):
                        mm = pe.transpose(ps_t[b % 2][:, u * TE:(u + 1) * TE], onehot[b % 2][:, u, :],
                                          m.ident[0:TE, 0:TE])
                    mm.then_inc(turned, 1)
                    pe.wait_ge(attr_in[b], (i + 1) * (16 * U))
                    pe.wait_ge(sums_free, i * B + b + 1)
                    for u in range(U):
                        c0 = u % 2 * (BANK // 2)
                        mm = pe.matmul(ps_a[b % 2][:, u // 2, c0:c0 + P + 1], onehot[b % 2][:, u, :],
                                       attr[b][:, u, :], start=True, stop=True)
                    mm.then_inc(block_summed, 1)
                    pe.wait_ge(turned_copied, i * B + b + 1)
                    pe.wait_ge(row_copied, i * B + b + 1)
                    for u in range(U):
                        mm = pe.matmul(ps_x[b % 2][0:TE, u * P:(u + 1) * P], onehot_t[b % 2][:, u, :],
                                       m.x[:, bass.ds(nodes[b * U + u], 1), :], start=True, stop=True)
                    mm.then_inc(spread_done, 1)

            passes(pe, NB // B, one_pass)


def clear_banks(pe, m, ps, banks):
    for bank in range(banks):
        mm = pe.matmul(ps[:, bank * BANK:(bank + 1) * BANK], m.zeros[:, 0:P], m.zeros[:, 0:BANK],
                       start=True, stop=False, skip_group_check=True)
    return mm


def gather_src(nc, g, m):
    NB = g.K2 // U
    NT = g.NT
    HALF = NT // 2
    with ExitStack() as ctx:
        def sb(name, shape, dt=F32):
            return ctx.enter_context(nc.sbuf_tensor(name, shape, dt))

        def sem(name):
            return ctx.enter_context(nc.semaphore(name))

        row = [sb(f"row_in{b}", [P, U, ROWW]) for b in range(B2)]
        onehot = [sb(f"onehot_s{b}", [P, U, P]) for b in range(B2)]
        onehot_half = [sb(f"onehot_half_s{b}", [P, U, P], BF16) for b in range(B2)]
        edge_half = [sb(f"edge_half_s{b}", [P, U, COUNT_W], BF16) for b in range(B2)]
        ps_sum = ctx.enter_context(nc.psum_tensor("ps_src_sum", [P, SUM_BANKS * BANK], F32))
        ps_degree = ctx.enter_context(nc.psum_tensor("ps_src_degree", [P, BANK], F32))
        row_in = [sem(f"row_in_sem{b}") for b in range(B2)]
        fill_ready = sem("fill_s_ready")
        onehot_ready, onehot_half_ready, block_summed, all_summed = (
            sem("onehot_ready_s"), sem("onehot_half_ready_s"), sem("block_summed_s"), sem("all_summed_s"))
        block = ctx.enter_context(nc.Block())

        @block.sync
        def _(sp):
            def one_pass(i):
                for b in range(B2):
                    wait_before(sp, block_summed, i * B2 + (b + 1 - B2))
                    sp.dma_start(row[b][:], m.sorted_rows[:, bass.ds(i * (B2 * U) + b * U, U), :]).then_inc(
                        row_in[b], 16)

            passes(sp, NB // B2, one_pass)

        @block.vector
        def _(dve):
            for b in range(B2):
                dve.memset(edge_half[b][:], 0.0).then_inc(fill_ready, 1)

            def one_pass(i):
                for b in range(B2):
                    dve.wait_ge(row_in[b], i * 16 + 16)
                    wait_before(dve, block_summed, i * B2 + (b + 1 - B2))
                    dve.tensor_tensor(onehot[b][:], repeat(m.column[:], 1, U), repeat(row[b][:, :, P + 1], 2, P),
                                      ALU.is_equal).then_inc(onehot_ready, 1)

            passes(dve, NB // B2, one_pass)
            dve.wait_ge(all_summed, 1)
            dve.tensor_copy(m.src_sum[:, 0:HALF, 0:P],
                            ps_sum[:, 0:HALF * P].rearrange("p (n d) -> p n d", n=HALF))
            dve.tensor_copy(m.src_sum[:, 0:NT, P], ps_degree[:, 0:NT])

        @block.scalar
        def _(act):
            act.wait_ge(fill_ready, B2)

            def one_pass(i):
                for b in range(B2):
                    wait_before(act, block_summed, i * B2 + (b + 1 - B2))
                    act.wait_ge(onehot_ready, i * B2 + b + 1)
                    act.copy(edge_half[b][:, :, 0:1], row[b][:, :, P:P + 1])
                    act.copy(onehot_half[b][:], onehot[b][:]).then_inc(onehot_half_ready, 1)

            passes(act, NB // B2, one_pass)
            act.wait_ge(all_summed, 1)
            act.copy(m.src_sum[:, HALF:NT, 0:P],
                     ps_sum[:, HALF * P:NT * P].rearrange("p (n d) -> p n d", n=NT - HALF))

        @block.tensor
        def _(pe):
            clear_banks(pe, m, ps_sum, SUM_BANKS)
            clear_banks(pe, m, ps_degree, 1)

            def one_pass(i):
                nodes = numbers(nc, pe, m.node2_i, i * (B2 * U), B2 * U, NT - 1)
                for b in range(B2):
                    pe.wait_ge(onehot_ready, i * B2 + b + 1)
                    pe.wait_ge(onehot_half_ready, i * B2 + b + 1)
                    for u in range(U):
                        node = nodes[b * U + u]
                        pe.matmul(ps_sum[:, bass.ds(node * P, P)], onehot[b][:, u, :], row[b][:, u, 0:P],
                                  start=False, stop=False, skip_group_check=True)
                        mm = pe.matmul(ps_degree[:, bass.ds(node, COUNT_W)], onehot_half[b][:, u, :],
                                       edge_half[b][:, u, :], start=False, stop=False, skip_group_check=True)
                    mm.then_inc(block_summed, 1)

            passes(pe, NB // B2, one_pass)
            pe.matmul(ps_degree[:, 0:P], m.zeros[:, 0:P], m.zeros[:, 0:P], start=False, stop=True,
                      skip_group_check=True).then_inc(all_summed, 1)


def center(vec, done, y, stats):
    D = y.shape[2]
    mean = stats[:, 0, :]
    vec.wait_ge(done.sem, done.inc(vec.tensor_reduce(mean, y, AX.X, ALU.add)))
    vec.wait_ge(done.sem, done.inc(vec.tensor_scalar(mean, mean, 1.0 / D, None, ALU.mult)))
    vec.wait_ge(done.sem, done.inc(vec.tensor_tensor(y, y, repeat(mean, 2, D), ALU.subtract)))
    return done.n


def find_variance(vec, done, square, stats):
    var = stats[:, 1, :]
    vec.wait_ge(done.sem, done.inc(vec.tensor_reduce(var, square, AX.X, ALU.add)))
    vec.wait_ge(done.sem, done.inc(vec.tensor_scalar(var, var, 1.0 / square.shape[2], LN_EPS, ALU.mult, ALU.add)))
    return done.n


def normalize(vec, done, y, stats):
    D = y.shape[2]
    rstd = stats[:, 2, :]
    vec.wait_ge(done.sem, done.inc(vec.reciprocal(rstd, rstd)))
    vec.wait_ge(done.sem, done.inc(vec.tensor_tensor(y, y, repeat(rstd, 2, D), ALU.mult)))
    return done.n


def nodes(nc, g, m):
    NT, D = g.NT, P
    CH, LAG = 5, 2
    NCH = NT // CH
    PLACES = 2 * NT
    SQUARE_AT, ROOT_AT = CH + 3, 2 * CH + 3
    assert NCH * CH == NT
    with ExitStack() as ctx:
        def sb(name, shape, dt=F32):
            return ctx.enter_context(nc.sbuf_tensor(name, shape, dt))

        def sem(name):
            return ctx.enter_context(nc.semaphore(name))

        pair_t = [sb(f"pair_t{b}", [P, 2, P]) for b in range(4)]
        square = sb("square", [P, NT, D])
        stats = sb("stats", [P, 3, NT])
        degree = sb("degree", [P, 2, NT])
        ps_t = [ctx.enter_context(nc.psum_tensor(f"ps_node_t{b}", [P, BANK], F32)) for b in range(3)]
        ps = [ctx.enter_context(nc.psum_tensor(f"ps_node{b}", [P, BANK], F32)) for b in range(3)]
        ps_att = ctx.enter_context(nc.psum_tensor("ps_att", [P, BANK], F32))
        steps_sem, squared, sqrt_done = sem("node_steps"), sem("squared_n"), sem("sqrt_done")
        turned, copied, product, added, stored = (
            sem("node_turned"), sem("node_copied"), sem("node_product"), sem("node_added"), sem("node_stored"))
        table_out, att_ready = sem("table_out"), sem("att_ready")
        block = ctx.enter_context(nc.Block())
        step = Steps(steps_sem)
        src_mean, attr_mean, centered, variance, x1_ready = {}, {}, {}, {}, {}

        def chunk(c):
            return slice(c * CH, (c + 1) * CH)

        @block.vector
        def _(dve):
            def link(ins):
                dve.wait_ge(steps_sem, step.inc(ins))

            link(dve.tensor_scalar(degree[:, 0, :], m.src_sum[:, 0:NT, D], DEG_EPS, None, ALU.add))
            link(dve.tensor_scalar(degree[:, 1, :], m.attr_sum[:, :, D], 1.0, None, ALU.max))
            link(dve.reciprocal(degree[:], degree[:]))
            for which, sums, mean in ((0, m.src_sum, src_mean), (1, m.attr_sum, attr_mean)):
                for c in range(NCH):
                    mean[c] = step.inc(dve.tensor_tensor(
                        sums[:, chunk(c), 0:D], sums[:, chunk(c), 0:D], repeat(degree[:, which, chunk(c)], 2, D),
                        ALU.mult))
            dve.wait_ge(att_ready, 1)
            step.inc(dve.tensor_copy(m.att[:], ps_att[:, 0:D]))
            step.inc(dve.tensor_copy(m.bias[:], ps_att[:, D:2 * D]))

            for c in range(NCH + 2):
                for n in range(c * CH, min(c + 1, NCH) * CH):
                    dve.wait_ge(product, n + 1)
                    dve.scalar_tensor_tensor(m.x1[:, n, :], ps[n % 3][:, 0:D], 0.0, m.x[:, n, :],
                                             ALU.max, ALU.add).then_inc(added, 1)
                if c < NCH:
                    dve.wait_ge(added, (c + 1) * CH)
                    centered[c] = center(dve, step, m.x1[:, chunk(c), :], stats[:, :, chunk(c)])
                if 1 <= c <= NCH:
                    k = c - 1
                    dve.wait_ge(squared, k + 1)
                    variance[k] = find_variance(dve, step, square[:, chunk(k), :], stats[:, :, chunk(k)])
                if c >= 2:
                    k = c - 2
                    dve.wait_ge(sqrt_done, k + 1)
                    x1_ready[k] = normalize(dve, step, m.x1[:, chunk(k), :], stats[:, :, chunk(k)])
            for c in range(NCH):
                s = square[:, chunk(c), :]
                dve.wait_ge(stored, (c + 1) * CH)
                link(dve.tensor_tensor(s, s, m.x[:, chunk(c), :], ALU.add))
                link(dve.tensor_tensor(s, s, m.src_sum[:, chunk(c), 0:D], ALU.add))
                link(dve.scalar_tensor_tensor(s, s, SLOPE, s, ALU.mult, ALU.max))
                link(dve.tensor_tensor(s, s, repeat(m.att[:], 1, CH), ALU.mult))
                step.inc(dve.tensor_reduce(m.loop_score[:, chunk(c), :], s.rearrange("p n (h c) -> p n h c", h=g.H),
                                           AX.X, ALU.add))

        @block.scalar
        def _(act):
            def keep(n):
                part = ps[(NT + n) % 3]
                act.wait_ge(product, NT + n + 1)
                act.copy(m.x[:, n, :], part[:, 0:D])
                act.copy(m.src_sum[:, n, 0:D], part[:, D:2 * D])
                act.copy(square[:, n, :], part[:, 2 * D:3 * D]).then_inc(stored, 1)

            for k in range(PLACES):
                act.wait_ge(turned, k + 1)
                if k >= 4:
                    act.wait_ge(product, k - 3)
                act.copy(pair_t[k % 4][:], ps_t[k % 3][:, 0:2 * P].rearrange("p (c n) -> p c n", c=2)).then_inc(
                    copied, 1)
                c = (k - SQUARE_AT) // CH
                if (k - SQUARE_AT) % CH == 0 and 0 <= c < NCH:
                    act.wait_ge(steps_sem, centered[c])
                    act.activation(square[:, chunk(c), :], m.x1[:, chunk(c), :], ACT.Square).then_inc(squared, 1)
                c = (k - ROOT_AT) // CH
                if (k - ROOT_AT) % CH == 0 and 0 <= c < NCH:
                    act.wait_ge(steps_sem, variance[c])
                    act.activation(stats[:, 2, chunk(c)], stats[:, 1, chunk(c)], ACT.Sqrt).then_inc(sqrt_done, 1)
                if k >= NT + LAG + 1:
                    keep(k - NT - LAG - 1)
            for n in range(NT - LAG - 1, NT):
                keep(n)

        @block.sync
        def _(sp):
            table = m.xl_rows.rearrange("(n p) d -> p n d", p=P)
            for c in range(NCH):
                sp.wait_ge(stored, (c + 1) * CH)
                sp.dma_start(table[:, chunk(c), :], m.x[:, chunk(c), :]).then_inc(table_out, 16)
            sp.wait_ge(table_out, 16 * NCH)

        @block.tensor
        def _(pe):
            pe.matmul(ps_att[:, 0:2 * D], m.ones_row[:], m.rows[0:1, 3:5, :].rearrange("p c d -> p (c d)"),
                      start=True, stop=True).then_inc(att_ready, 1)

            def turn(k):
                which, n = divmod(k, NT)
                pe.wait_ge(steps_sem, (src_mean, x1_ready)[which][n // CH])
                if k >= 3:
                    pe.wait_ge(copied, k - 2)
                first, second = ((m.x, m.src_sum), (m.x1, m.attr_sum))[which]
                pe.transpose(ps_t[k % 3][:, 0:P], first[:, n, :], m.ident[:])
                pe.transpose(ps_t[k % 3][:, P:2 * P], second[:, n, 0:D], m.ident[:]).then_inc(turned, 1)

            def multiply(k):
                pe.wait_ge(copied, k + 1)
                if k >= 3:
                    if k - 3 < NT:
                        pe.wait_ge(added, k - 2)
                    else:
                        pe.wait_ge(stored, k - 2 - NT)
                out, ones, left = ps[k % 3], m.ones_row[:], pair_t[k % 4]
                if k < NT:
                    pe.matmul(out[:, 0:D], left[:, 0, :], m.w0[:, 0, :], start=True, stop=False)
                    pe.matmul(out[:, 0:D], left[:, 1, :], m.w0[:, 1, :], start=False, stop=False)
                    pe.matmul(out[:, 0:D], ones, m.rows[0:1, 0, :], start=False, stop=True).then_inc(product, 1)
                else:
                    pe.matmul(out[:, 0:2 * D], left[:, 0, :], m.w_lr[:].rearrange("p c d -> p (c d)"),
                              start=True, stop=False)
                    pe.matmul(out[:, 0:2 * D], ones, m.rows[0:1, 1:3, :].rearrange("p c d -> p (c d)"),
                              start=False, stop=True)
                    pe.matmul(out[:, 2 * D:3 * D], left[:, 1, :], m.w_e[:], start=True, stop=True).then_inc(product, 1)

            for k in range(PLACES + LAG):
                if k < PLACES:
                    turn(k)
                if k >= LAG:
                    multiply(k - LAG)


def scores(nc, g, m, a):
    NB = g.K // U
    TE = g.TE
    with ExitStack() as ctx:
        def sb(name, shape, dt=F32):
            return ctx.enter_context(nc.sbuf_tensor(name, shape, dt))

        def sem(name):
            return ctx.enter_context(nc.semaphore(name))

        attr = [sb(f"attr_c{b}", [TE, U, P]) for b in range(B)]
        xl = [sb(f"xl{b}", [TE, U, P]) for b in range(B)]
        index = [sb(f"index_c{b}", [TE, B // 2 * U], I32) for b in range(2)]
        onehot = [sb(f"onehot_c{b}", [TE, U, P]) for b in range(2)]
        onehot_t = [sb(f"onehot_ct{b}", [P, U, TE]) for b in range(2)]
        attr_t = [sb(f"attr_t{b}", [P, U, TE]) for b in range(2)]
        work = [sb(f"work_c{b}", [TE, U, P]) for b in range(2)]
        ps_t = [ctx.enter_context(nc.psum_tensor(f"ps_ct{b}", [P, BANK], F32)) for b in range(2)]
        ps_e = [ctx.enter_context(nc.psum_tensor(f"ps_ce{b}", [P, BANK], F32)) for b in range(2)]
        ps_s = [ctx.enter_context(nc.psum_tensor(f"ps_cs{b}", [P, BANK], F32)) for b in range(2)]
        attr_in = [sem(f"attr_c_in{b}") for b in range(B)]
        xl_in = [sem(f"xl_in{b}") for b in range(B)]
        xl_out = [sem(f"xl_out{b}") for b in range(B)]
        index_ready, begun, onehot_ready, turned, turned_copied = (
            sem("index_c_ready"), sem("begun_c"), sem("onehot_c_ready"), sem("turned_c"), sem("turned_c_copied"))
        attr_turned, attr_copied, summed, score_steps, xl_used = (
            sem("attr_turned"), sem("attr_copied"), sem("summed_c"), sem("score_steps"), sem("xl_used"))
        block = ctx.enter_context(nc.Block())

        @block.sync
        def _(sp):
            def keep_xl(i, b):
                sp.wait_ge(xl_in[b], i * (16 * U) + 16 * U)
                sp.dma_start(m.xl_edges[:, bass.ds(i * (B * U) + b * U, U), :], xl[b][:]).then_inc(xl_out[b], 16)

            def one_pass(i):
                tiles = numbers(nc, sp, m.tile_i, i * (B * U), B * U, g.T - 1)
                for b in range(B):
                    sp.wait_ge(attr_turned, i * B + b + 1)
                    for u in range(U):
                        sp.dma_start(attr[b][:, u, :], a["ea"][bass.ds(tiles[b * U + u] * TE, TE), :]).then_inc(
                            attr_in[b], 16)
                    if b >= 2:
                        keep_xl(i, b - 2)
                    elif not isinstance(i, int):
                        keep_xl(i - 1, b + B - 2)

            passes(sp, NB // B, one_pass)
            for b in (B - 2, B - 1):
                keep_xl(NB // B - 1, b)
            for b in range(B):
                sp.wait_ge(xl_out[b], 16 * (NB // B))

        @block.gpsimd
        def _(pool):
            def one_pass(i):
                for b in range(B):
                    half, first = divmod(b, B // 2)
                    if first == 0:
                        for k in range(b, b + B // 2):
                            wait_before(pool, xl_in[k], i * (16 * U))
                        pool.tensor_copy(index[half][:], m.src_idx[:, bass.ds(
                            i * (B * U) + b * U, B // 2 * U)]).then_inc(index_ready, 1)
                        pool.wait_ge(index_ready, i * 2 + half + 1)
                    wait_before(pool, xl_out[b], i * 16)
                    pool.wait_ge(xl_used, i * B + b + 1)
                    pool.sem_inc(begun, 1)
                    for u in range(U):
                        pool.indirect_dma_start(
                            out=xl[b][:, u, :], out_offset=None, in_=m.xl_rows,
                            in_offset=bass.IndirectOffsetOnAxis(
                                ap=index[half][:, first * U + u:first * U + u + 1], axis=0)).then_inc(xl_in[b], 16)

            passes(pool, NB // B, one_pass)

        @block.scalar
        def _(act):
            def one_pass(i):
                for b in range(B):
                    act.wait_ge(attr_turned, i * B + b + 1 + B)
                    wait_before(act, summed, i * B + (b + 1))
                    act.copy(attr_t[b % 2][:], ps_e[b % 2][:, 0:U * TE].rearrange("p (u e) -> p u e", u=U)).then_inc(
                        attr_copied, 1)
                    act.wait_ge(turned, i * B + b + 1)
                    act.copy(onehot_t[b % 2][:], ps_t[b % 2][:, 0:U * TE].rearrange("p (u e) -> p u e", u=U)).then_inc(
                        turned_copied, 1)

            passes(act, NB // B, one_pass)

        @block.vector
        def _(dve):
            dve.sem_inc(xl_used, B)
            dve.sem_inc(score_steps, 1)

            def score_block(i, b):
                k0 = i * (B * U) + b * U
                s = work[b % 2]
                base = i * (4 * B) + 4 * b
                dve.wait_ge(xl_in[b], i * (16 * U) + 16 * U)
                dve.wait_ge(summed, i * B + b + 3)
                dve.wait_ge(score_steps, base + 1)
                dve.tensor_tensor(s[:], ps_s[b % 2][0:TE, :].rearrange("p (u d) -> p u d", u=U), xl[b][:],
                                  ALU.add).then_inc(score_steps, 1)
                dve.wait_ge(score_steps, base + 2)
                dve.sem_inc(xl_used, 1)
                dve.scalar_tensor_tensor(s[:], s[:], SLOPE, s[:], ALU.mult, ALU.max).then_inc(score_steps, 1)
                dve.wait_ge(score_steps, base + 3)
                dve.tensor_tensor(s[:], s[:], repeat(m.att[0:TE, :], 1, U), ALU.mult).then_inc(score_steps, 1)
                dve.wait_ge(score_steps, base + 4)
                dve.tensor_reduce(m.score[:, :, bass.ds(k0, U)].rearrange("p h u -> p u h"),
                                  s[:].rearrange("p u (h c) -> p u h c", h=g.H), AX.X, ALU.add).then_inc(score_steps, 1)

            def one_pass(i):
                for b in range(B):
                    wait_before(dve, turned, i * B + (b - 1))
                    dve.tensor_tensor(onehot[b % 2][:], repeat(m.column[0:TE, :], 1, U),
                                      repeat(m.dst_lo[0:TE, bass.ds(i * (B * U) + b * U, U)], 2, P),
                                      ALU.is_equal).then_inc(onehot_ready, 1)
                    if b >= 2:
                        score_block(i, b - 2)
                    elif not isinstance(i, int):
                        score_block(i - 1, b + B - 2)

            passes(dve, NB // B, one_pass)
            for b in (B - 2, B - 1):
                score_block(NB // B - 1, b)

        @block.tensor
        def _(pe):
            pe.sem_inc(attr_turned, B)
            pe.sem_inc(summed, 2)

            def sum_block(j, nodes, parity):
                pe.wait_ge(attr_copied, j + 1)
                wait_before(pe, xl_used, j + (B - 1))
                pe.wait_ge(turned_copied, j + 1)
                for u in range(U):
                    out = ps_s[parity][0:TE, u * P:(u + 1) * P]
                    pe.matmul(out, attr_t[parity][:, u, :], m.w_e[:], start=True, stop=False)
                    mm = pe.matmul(out, onehot_t[parity][:, u, :], m.src_sum[:, bass.ds(nodes[u], 1), 0:P],
                                   start=False, stop=True)
                mm.then_inc(summed, 1)

            def one_pass(i):
                nodes = block_numbers_before(nc, pe, m.node_i, i, g.NT - 1)
                for b in range(B):
                    pe.wait_ge(attr_in[b], i * (16 * U) + 16 * U)
                    for u in range(U):
                        mm = pe.transpose(ps_e[b % 2][:, u * TE:(u + 1) * TE], attr[b][:, u, :], m.ident[0:TE, 0:TE])
                    mm.then_inc(attr_turned, 1)
                    pe.wait_ge(onehot_ready, i * B + b + 1)
                    for u in range(U):
                        mm = pe.transpose(ps_t[b % 2][:, u * TE:(u + 1) * TE], onehot[b % 2][:, u, :],
                                          m.ident[0:TE, 0:TE])
                    mm.then_inc(turned, 1)
                    if nodes[b] is not None:
                        sum_block(i * B + (b - 1), nodes[b], (b - 1) % 2)

            passes(pe, NB // B, one_pass)
            sum_block(NB - 1, numbers(nc, pe, m.node_i, g.K - U, U, g.NT - 1), (NB - 1) % 2)


def maxima(nc, g, m):
    TE, KR, KC, H, K = g.TE, g.KR, g.KC, g.H, g.K
    with ExitStack() as ctx:
        def sb(name, shape, dt=F32):
            return ctx.enter_context(nc.sbuf_tensor(name, shape, dt))

        def sem(name):
            return ctx.enter_context(nc.semaphore(name))

        score = sb("score_rows", [KR, KC, H, TE])
        masked = sb("masked_rows", [KR, KC, H, TE])
        run = sb("run_rows", [KR, 2, KC * H * TE])
        ends = sb("max_ends", [KR, 2, KC, H])
        rows = sb("max_rows", [H, 2, K])
        way = sb("way", [H, 2, 2, K])
        carry = sb("carry", [H, 2, K])
        carry_k = sb("carry_k", [KR, 2, KC, H])
        extra = sb("extra", [KR, KC, H, TE])
        ps = [ctx.enter_context(nc.psum_tensor(f"ps_max{q}", [P, BANK], F32)) for q in range(8)]
        rows_ready, steps_sem, ends_turned, carry_turned, exp_done, back = (
            sem("rows_ready"), sem("max_steps"), sem("ends_turned"), sem("carry_turned"), sem("exp_done"), sem("back"))
        rows_copied = sem("rows_copied")
        block = ctx.enter_context(nc.Block())
        step = Steps(steps_sem)
        at = {}
        flat = "k c h e -> k (c h e)"
        R = H * TE

        @block.vector
        def _(dve):
            def link(ins):
                dve.wait_ge(steps_sem, step.inc(ins))

            for q in range(KC):
                dve.wait_ge(rows_ready, q + 1)
                at["masked", q] = step.inc(dve.tensor_tensor(
                                           masked[:, q], ps[q][0:KR, 0:R].rearrange("k (h e) -> k h e", h=H),
                                           repeat(m.others[:, q], 1, H), ALU.add))
            dve.wait_ge(steps_sem, step.n)
            link(dve.tensor_tensor_scan(run[:, 0, :], m.begins[:].rearrange(flat), masked[:].rearrange(flat),
                                        -BIG, ALU.add, ALU.max))
            link(dve.tensor_tensor_scan(run[:, 1, ::-1], m.ends[:].rearrange(flat)[:, ::-1],
                                        masked[:].rearrange(flat)[:, ::-1], -BIG, ALU.add, ALU.max))
            link(dve.tensor_tensor(run[:, 0, :], run[:, 0, :], run[:, 1, :], ALU.max))
            by_slot = run[:, 0, :].rearrange("k (c h e) -> k c h e", c=KC, h=H)
            step.inc(dve.tensor_copy(ends[:, 0], by_slot[:, :, :, 0]))
            at["ends"] = step.inc(dve.tensor_copy(ends[:, 1], by_slot[:, :, :, TE - 1]))
            dve.wait_ge(ends_turned, 1)
            step.inc(dve.tensor_copy(rows[:, 0, :], ps[4][0:H, 0:K]))
            link(dve.tensor_copy(rows[:, 1, :], ps[5][0:H, 0:K]))
            step.inc(dve.tensor_tensor(way[:, 0, 0, 1:K], m.joined[0:H, 1:K], m.whole[0:H, 0:K - 1], ALU.add))
            step.inc(dve.tensor_tensor(way[:, 0, 1, 1:K], m.joined[0:H, 1:K], rows[:, 1, 0:K - 1], ALU.add))
            step.inc(dve.tensor_tensor(way[:, 1, 0, 0:K - 1], m.joined[0:H, 1:K], m.whole[0:H, 1:K], ALU.add))
            step.inc(dve.tensor_tensor(way[:, 1, 1, 0:K - 1], m.joined[0:H, 1:K], rows[:, 0, 1:K], ALU.add))
            link(dve.memset(carry[:], -BIG))
            link(dve.tensor_tensor_scan(carry[:, 0, 1:K], way[:, 0, 0, 1:K], way[:, 0, 1, 1:K], -BIG, ALU.add, ALU.max))
            link(dve.tensor_tensor_scan(carry[:, 1, 0:K - 1][:, ::-1], way[:, 1, 0, 0:K - 1][:, ::-1],
                                        way[:, 1, 1, 0:K - 1][:, ::-1], -BIG, ALU.add, ALU.max))
            at["carry"] = step.n
            dve.wait_ge(carry_turned, 1)
            link(dve.tensor_copy(carry_k[:].rearrange("k f c h -> k (f c h)"), ps[6][0:KR, 0:2 * KC * H]))
            for f, away in ((0, m.not_first), (1, m.not_last)):
                for q in range(KC):
                    step.inc(dve.tensor_tensor(extra[:, q], repeat(carry_k[:, f, q, :], 2, TE),
                                               repeat(away[:, q], 1, H), ALU.add))
                dve.wait_ge(steps_sem, step.n)
                link(dve.tensor_tensor(run[:, 0, :], run[:, 0, :], extra[:].rearrange(flat), ALU.max))
            dve.wait_ge(rows_copied, 1)
            link(dve.tensor_tensor(run[:, 0, :], run[:, 0, :], score[:].rearrange(flat), ALU.max))
            link(dve.tensor_tensor(score[:].rearrange(flat), score[:].rearrange(flat), run[:, 0, :], ALU.subtract))
            at["shifted"] = step.n
            for h in range(H):
                dve.wait_ge(back, h + 1)
                step.inc(dve.tensor_tensor(m.exp_max[:, :, H + h], ps[H + h][0:TE, 0:K], m.first[0:TE, :], ALU.mult))

        @block.scalar
        def _(act):
            for q in range(KC):
                act.wait_ge(steps_sem, at["masked", q])
                mm = act.copy(score[:, q], ps[q][0:KR, 0:R].rearrange("k (h e) -> k h e", h=H))
            mm.then_inc(rows_copied, 1)
            act.wait_ge(steps_sem, at["shifted"])
            act.activation(score[:], score[:], ACT.Exp).then_inc(exp_done, 1)
            for h in range(H):
                act.wait_ge(back, H + h + 1)
                act.copy(m.exp_max[:, :, h], ps[h][0:TE, 0:K])

        @block.gpsimd
        def _(pool):
            pool.tensor_tensor(m.x1[:], m.x1[:], repeat(m.bias[:], 1, g.NT), ALU.add)

        @block.tensor
        def _(pe):
            for q in range(KC):
                for h in range(H):
                    mm = pe.transpose(ps[q][0:KR, h * TE:(h + 1) * TE], m.score[:, h, q * KR:(q + 1) * KR],
                                      m.ident[0:TE, 0:TE])
                mm.then_inc(rows_ready, 1)
            pe.wait_ge(steps_sem, at["ends"])
            for f in range(2):
                for q in range(KC):
                    mm = pe.transpose(ps[4 + f][0:H, q * KR:(q + 1) * KR], ends[:, f, q, :], m.ident[0:KR, 0:KR])
            mm.then_inc(ends_turned, 1)
            pe.wait_ge(steps_sem, at["carry"])
            for f in range(2):
                for q in range(KC):
                    c0 = (f * KC + q) * H
                    mm = pe.transpose(ps[6][0:KR, c0:c0 + H], carry[:, f, q * KR:(q + 1) * KR], m.ident[0:H, 0:H])
            mm.then_inc(carry_turned, 1)
            by_slot = run[:, 0, :].rearrange("k (c h e) -> k c h e", c=KC, h=H)
            pe.wait_ge(steps_sem, at["shifted"])
            for which, table in ((1, by_slot), (0, score[:])):
                if which == 0:
                    pe.wait_ge(exp_done, 1)
                for h in range(H):
                    for q in range(KC):
                        mm = pe.transpose(ps[which * H + h][0:TE, q * KR:(q + 1) * KR], table[:, q, h, :],
                                          m.ident[0:KR, 0:KR])
                    mm.then_inc(back, 1)


def messages(nc, g, m):
    NB = g.K // U
    TE, H = g.TE, g.H
    W = P + 2 * H
    WINDOWS, LAG = 3, 2
    assert B % WINDOWS == 0
    with ExitStack() as ctx:
        def sb(name, shape, dt=F32):
            return ctx.enter_context(nc.sbuf_tensor(name, shape, dt))

        def sem(name):
            return ctx.enter_context(nc.semaphore(name))

        xl = [sb(f"xl_m{b}", [TE, U, P]) for b in range(B)]
        message = [sb(f"message{b}", [TE, U, W]) for b in range(B)]
        onehot = [sb(f"onehot_m{b}", [TE, U, P]) for b in range(B)]
        ps = [ctx.enter_context(nc.psum_tensor(f"ps_m{b}", [P, U, BANK // 2], F32)) for b in range(WINDOWS)]
        xl_in = [sem(f"xl_m_in{b}") for b in range(B)]
        onehot_ready, message_ready, column_ready, summed, added = (
            sem("onehot_m_ready"), sem("message_ready"), sem("column_ready"), sem("summed_m"), sem("added_m"))
        block = ctx.enter_context(nc.Block())

        @block.sync
        def _(sp):
            def one_pass(i):
                for b in range(B):
                    wait_before(sp, message_ready, i * B + (b + 1 - B))
                    sp.dma_start(xl[b][:], m.xl_edges[:, bass.ds(i * (B * U) + b * U, U), :]).then_inc(xl_in[b], 16)

            passes(sp, NB // B, one_pass)

        @block.gpsimd
        def _(pool):
            def one_pass(i):
                for b in range(B):
                    pool.wait_ge(xl_in[b], i * 16 + 16)
                    wait_before(pool, summed, i * B + (b + 1 - B))
                    pool.tensor_tensor(message[b][:, :, 0:P].rearrange("p u (h c) -> p u h c", h=H),
                                       xl[b][:].rearrange("p u (h c) -> p u h c", h=H),
                                       repeat(m.exp_max[:, bass.ds(i * (B * U) + b * U, U), 0:H], 3, P // H),
                                       ALU.mult).then_inc(message_ready, 1)

            passes(pool, NB // B, one_pass)

        @block.scalar
        def _(act):
            def one_pass(i):
                for b in range(B):
                    wait_before(act, summed, i * B + (b + 1 - B))
                    act.copy(message[b][:, :, P:W], m.exp_max[:, bass.ds(i * (B * U) + b * U, U), :]).then_inc(
                        column_ready, 1)

            passes(act, NB // B, one_pass)

        @block.vector
        def _(dve):
            dve.memset(m.message_sum[:], 0.0).then_inc(added, 1)

            def add_sums(j, base, window):
                acc = m.message_sum[:, bass.ds(base, U), :]
                dve.wait_ge(summed, j + 1)
                dve.wait_ge(added, j + 1)
                dve.tensor_tensor(acc, acc, ps[window][:, :, 0:W], ALU.add).then_inc(added, 1)

            def one_pass(i):
                bases = numbers_before(nc, dve, m.base_i, i, B, g.NT - 1, LAG)
                for b in range(B):
                    wait_before(dve, summed, i * B + (b + 1 - B))
                    dve.tensor_tensor(onehot[b][:], repeat(m.column[0:TE, :], 1, U),
                                      repeat(m.dst_lo[0:TE, bass.ds(i * (B * U) + b * U, U)], 2, P),
                                      ALU.is_equal).then_inc(onehot_ready, 1)
                    if bases[b] is not None:
                        add_sums(i * B + (b - LAG), bases[b], (b - LAG) % WINDOWS)

            passes(dve, NB // B, one_pass)
            last = numbers(nc, dve, m.base_i, NB - LAG, LAG, g.NT - 1)
            for k in range(LAG):
                add_sums(NB - LAG + k, last[k], (NB - LAG + k) % WINDOWS)

        @block.tensor
        def _(pe):
            def one_pass(i):
                window = numbers(nc, pe, m.window_i, i * (B * U), B * U, U - 1)
                for b in range(B):
                    wait_before(pe, added, i * B + (b + 2 - WINDOWS))
                    clear_window(pe, m, ps[b % WINDOWS], W)
                    pe.wait_ge(onehot_ready, i * B + b + 1)
                    pe.wait_ge(column_ready, i * B + b + 1)
                    pe.wait_ge(message_ready, i * B + b + 1)
                    for u in range(U):
                        mm = pe.matmul(ps[b % WINDOWS][:, bass.ds(window[b * U + u], 1), 0:W], onehot[b][:, u, :],
                                       message[b][:, u, :], start=False, stop=(u == U - 1),
                                       skip_group_check=True)
                    mm.then_inc(summed, 1)

            passes(pe, NB // B, one_pass)


def finish(nc, g, m, out):
    NT, H, D = g.NT, g.H, P
    CH = 5
    NCH = NT // CH
    with ExitStack() as ctx:
        def sb(name, shape, dt=F32):
            return ctx.enter_context(nc.sbuf_tensor(name, shape, dt))

        def sem(name):
            return ctx.enter_context(nc.semaphore(name))

        top = sb("top", [P, NT, H])
        part = sb("part", [P, 2, NT, H])
        total = sb("total", [P, NT, H])
        square = sb("square_f", [P, NT, D])
        stats = sb("stats_f", [P, 3, NT])
        steps_sem, exp_done, loop_ready, squared, sqrt_done, stored = (
            sem("finish_steps"), sem("part_exp"), sem("loop_ready"), sem("squared"), sem("sqrt_f_done"),
            sem("out_stored"))
        block = ctx.enter_context(nc.Block())
        step = Steps(steps_sem)
        at = {}
        sums = m.message_sum[:, 0:NT]

        def chunk(c):
            return slice(c * CH, (c + 1) * CH)

        def weigh(engine, rows, which, c):
            by_head = rows.rearrange("p n (h c) -> p n h c", h=H)
            return engine.tensor_tensor(by_head, by_head, repeat(part[:, which, chunk(c), :], 3, D // H), ALU.mult)

        @block.vector
        def _(dve):
            def link(ins):
                dve.wait_ge(steps_sem, step.inc(ins))

            link(dve.tensor_scalar(total[:, :, 0], m.attr_sum[:, :, D], 0.0, -BIG, ALU.is_equal, ALU.mult))
            link(dve.tensor_tensor(part[:, 0], sums[:, :, D + H:D + 2 * H], repeat(total[:, :, 0], 2, H), ALU.add))
            link(dve.tensor_tensor(top[:], part[:, 0], m.loop_score[:], ALU.max))
            link(dve.tensor_tensor(part[:, 0], part[:, 0], top[:], ALU.subtract))
            link(dve.tensor_tensor(part[:, 1], m.loop_score[:], top[:], ALU.subtract))
            at["part"] = step.n
            dve.wait_ge(exp_done, 1)
            link(dve.tensor_tensor(total[:], sums[:, :, D:D + H], part[:, 0], ALU.mult))
            link(dve.tensor_tensor(total[:], total[:], part[:, 1], ALU.add))
            link(dve.reciprocal(total[:], total[:]))
            for w in (1, 0):
                link(dve.tensor_tensor(part[:, w], part[:, w], total[:], ALU.mult))
                at["weights", w] = step.n

            def add_up(c):
                y = m.x1[:, chunk(c), :]
                link(weigh(dve, sums[:, chunk(c), 0:D], 0, c))
                link(dve.tensor_tensor(y, y, sums[:, chunk(c), 0:D], ALU.add))
                dve.wait_ge(loop_ready, c + 1)
                link(dve.tensor_tensor(y, y, m.x[:, chunk(c), :], ALU.add))
                at["centered", c] = center(dve, step, y, stats[:, :, chunk(c)])

            for k in range(NCH + 2):
                if k < NCH:
                    add_up(k)
                if 1 <= k <= NCH:
                    dve.wait_ge(squared, k)
                    at["variance", k - 1] = find_variance(dve, step, square[:, chunk(k - 1), :],
                                                          stats[:, :, chunk(k - 1)])
                if k >= 2:
                    dve.wait_ge(sqrt_done, k - 1)
                    at["out", k - 2] = normalize(dve, step, m.x1[:, chunk(k - 2), :], stats[:, :, chunk(k - 2)])

        @block.gpsimd
        def _(pool):
            pool.wait_ge(steps_sem, at["weights", 1])
            for c in range(NCH):
                weigh(pool, m.x[:, chunk(c), :], 1, c).then_inc(loop_ready, 1)

        @block.scalar
        def _(act):
            act.wait_ge(steps_sem, at["part"])
            act.activation(part[:], part[:], ACT.Exp).then_inc(exp_done, 1)
            for k in range(NCH + 1):
                if k < NCH:
                    act.wait_ge(steps_sem, at["centered", k])
                    act.activation(square[:, chunk(k), :], m.x1[:, chunk(k), :], ACT.Square).then_inc(squared, 1)
                if k >= 1:
                    act.wait_ge(steps_sem, at["variance", k - 1])
                    act.activation(stats[:, 2, chunk(k - 1)], stats[:, 1, chunk(k - 1)], ACT.Sqrt).then_inc(
                        sqrt_done, 1)

        @block.sync
        def _(sp):
            main = out[0:(NT - 1) * P].rearrange("(n p) d -> p n d", p=P)
            for c in range(NCH):
                sp.wait_ge(steps_sem, at["out", c])
                last = min((c + 1) * CH, NT - 1)
                sp.dma_start(main[:, c * CH:last, :], m.x1[:, c * CH:last, :]).then_inc(stored, 16)
            sp.dma_start(out[(NT - 1) * P:g.N], m.x1[0:g.LAST, NT - 1, :]).then_inc(stored, 16)
            sp.wait_ge(stored, 16 * (NCH + 1))


def program(nc, a, out):
    g = Shapes(a["x"].shape[0], a["src"].shape[0], a["att"].shape[0])
    m = Tables()
    with ExitStack() as ctx:
        def sb(name, shape, dt=F32):
            return ctx.enter_context(nc.sbuf_tensor(name, shape, dt))

        D = a["x"].shape[1]
        m.x = sb("x_nodes", [P, g.NT, D])
        m.w0 = sb("w0", [P, 2, D])
        m.w_lr = sb("w_lr", [P, 2, D])
        m.w_e = sb("w_e", [P, D])
        m.rows = sb("rows", [1, 5, D])
        m.ones_row = sb("ones_row", [1, P])
        m.column = sb("column", [P, P])
        m.row_no = sb("row_no", [P, 1])
        m.ident = sb("ident", [P, P])
        m.node_i = sb("slot_node", [1, g.K], I32)
        m.tile_i = sb("slot_tile", [1, g.K], I32)
        m.base_i = sb("base_i", [1, g.K // U], I32)
        m.window_i = sb("window_i", [1, g.K], I32)
        m.zeros = sb("zeros", [1, 512], BF16)
        m.node2_i = sb("node2_i", [1, g.K2], I32)
        m.dst_lo = sb("dst_lo", [P, g.K])
        m.first = sb("first", [P, g.K])
        m.src_idx = sb("src_idx", [g.TE, g.K], I32)
        m.src_lo = sb("src_lo", [g.TE, g.K])
        m.place_idx = sb("place_idx", [g.TE, g.K], I32)
        m.slot_dst = sb("slot_dst", [g.KR, g.KC, g.TE])
        m.slot_node = sb("slot_node_rows", [g.KR, g.KC])
        m.others = sb("others", [g.KR, g.KC, g.TE])
        m.not_first = sb("not_first", [g.KR, g.KC, g.TE])
        m.not_last = sb("not_last", [g.KR, g.KC, g.TE])
        m.begins = sb("begins", [g.KR, g.KC, g.H, g.TE])
        m.ends = sb("ends", [g.KR, g.KC, g.H, g.TE])
        m.end_rows = sb("end_rows", [4, 2, g.K])
        m.whole = sb("whole", [4, g.K])
        m.joined = sb("joined", [4, g.K])
        m.sorted_rows = nc.dram_tensor("sorted_rows", (P, g.K2, ROWW), F32, kind="Internal").ap()
        m.att = sb("att_all", [P, D])
        m.bias = sb("bias_all", [P, D])
        m.x1 = sb("x1", [P, g.NT, D])
        m.loop_score = sb("loop_score", [P, g.NT, g.H])
        m.src_sum = sb("src_sum", [P, g.NT + U - 1, D + 1])
        m.xl_rows = nc.dram_tensor("xl_rows", (P * g.NT, D), F32, kind="Internal").ap()
        m.xl_edges = nc.dram_tensor("xl_edges", (g.TE, g.K, D), F32, kind="Internal").ap()
        m.attr_sum = sb("attr_sum", [P, g.NT, D + 1])
        prepare(nc, g, m, a)
        spread(nc, g, m, a)
        gather_src(nc, g, m)
        nodes(nc, g, m)
        m.score = sb("score", [g.TE, g.H, g.K])
        scores(nc, g, m, a)
        m.exp_max = sb("exp_max", [g.TE, g.K, 2 * g.H])
        maxima(nc, g, m)
        m.message_sum = sb("message_sum", [P, g.NT + U - 1, D + 2 * g.H])
        messages(nc, g, m)
        finish(nc, g, m, out)


_NAMES = {
    "x": "x", "src": "src", "dst": "dst", "edge_attr_128": "ea", "L0_gnn_W": "W0", "L0_gnn_b": "b0",
    "L1_gnn_W_l": "W_l", "L1_gnn_b_l": "b_l", "L1_gnn_W_r": "W_r", "L1_gnn_b_r": "b_r", "L1_gnn_W_e": "W_e",
    "L1_gnn_att": "att", "L1_gnn_bias": "bias",
}


def kernel(**inputs):
    import numpy as _np
    import concourse.bacc as _bacc
    from concourse import mybir as _mybir
    from concourse.bass_utils import run_bass_kernel_spmd as _run

    nc = _bacc.Bacc("TRN2", target_bir_lowering=False, num_devices=1)
    arrays, aps = {}, {}
    for name, short in _NAMES.items():
        array = _np.ascontiguousarray(inputs[name])
        arrays[f"in_{short}"] = array
        aps[short] = nc.dram_tensor(f"in_{short}", array.shape, _mybir.dt.from_np(array.dtype),
                                    kind="ExternalInput").ap()
    out = nc.dram_tensor("out_0", inputs["x"].shape, _mybir.dt.float32, kind="ExternalOutput").ap()
    program(nc, aps, out)
    result = _run(nc, [arrays], core_ids=[0])
    return result.results[0]["out_0"]
```
